# Optimizing a Trainium2 kernel written in Bass

```python
import numpy as np
import jax
import jax.numpy as jnp

def _softmax(x, axis=-1):
    return jax.nn.softmax(x, axis=axis)

def _gelu(x):
    return jax.nn.gelu(x, approximate=True)

def _silu(x):
    return jax.nn.silu(x)

def _sigmoid(x):
    return jax.nn.sigmoid(x)

def _layernorm(x, axis=-1, eps=1e-05):
    m = jnp.mean(x, axis=axis, keepdims=True)
    v = jnp.var(x, axis=axis, keepdims=True)
    return (x - m) / jnp.sqrt(v + eps)

def _scatter_add(tgt, idx, src, axis=0):
    return tgt.at[idx].add(src)

def _segment_sum(src, seg, n):
    return jax.ops.segment_sum(src, seg, n)
kernel_name = 'mk_decoder_postln_d2_seqx_r4_793a3d'

def setup_inputs(seed: int=0):
    np.random.seed(seed)
    _w = jnp.asarray

    def _rec_inputs():
        import jax
        import jax.numpy as jnp
        _rk = jax.random.key(seed)
        x = 7.22e-05 + 1 * jax.random.normal(jax.random.fold_in(_rk, 1), (16, 100, 256), jnp.float32)
        _lenS = 100 - jax.random.randint(jax.random.fold_in(_rk, 7), (16,), 0, max(1, 100 // 4) + 1, jnp.int32)
        _lenS2 = 361 - jax.random.randint(jax.random.fold_in(_rk, 8), (16,), 0, max(1, 361 // 4) + 1, jnp.int32)
        _ctx_1024P = jax.random.normal(jax.random.fold_in(_rk, 11), (16, 16, 256), jnp.float32)
        _ctx_1024c = jax.random.dirichlet(jax.random.fold_in(_rk, 511), 0.3 * jnp.ones((16,), jnp.float32), (16, 361))
        _ctx_1024t = jnp.einsum('bsk,bkd->bsd', _ctx_1024c, _ctx_1024P)
        _ctx_1024t = _ctx_1024t * jax.lax.rsqrt(jnp.mean(jnp.square(_ctx_1024t)) + 1e-12) * 0.953939
        ctx_1024 = 4.13588e-05 + 0.999923 * (_ctx_1024t + 0.3 * jax.random.normal(jax.random.fold_in(_rk, 611), (16, 361, 256), jnp.float32))
        _validS = jnp.arange(100)[None, :] < _lenS[:, None]
        _validS2 = jnp.arange(361)[None, :] < _lenS2[:, None]
        _causal = jnp.tril(jnp.ones((100, 100), dtype=bool))
        mask_BxS2_bf1 = jnp.ones((16, 361), dtype=bool)
        return (x, ctx_1024, mask_BxS2_bf1)
    x, ctx_1024, mask_BxS2_bf1 = _rec_inputs()

    def _L0_attn_setup():
        import jax, jax.numpy as jnp
        import numpy as np
        D_MODEL = 256
        N_HEAD = 16
        N_BR = 4
        DH = D_MODEL // N_HEAD
        H_TOT = N_BR * N_HEAD
        SCALE = float(np.pi / np.sqrt(3.0))
        ATTN_SCALE = DH ** (-0.5)

        def _rope(x):
            B, H, T, Dh = x.shape
            inv_freq = 1.0 / 10000.0 ** (jnp.arange(0, Dh, 2, dtype=jnp.float32) / Dh)
            t = jnp.arange(T, dtype=jnp.float32)
            freqs = t[:, None] * inv_freq[None, :]
            cos = jnp.cos(freqs)[None, None]
            sin = jnp.sin(freqs)[None, None]
            x1 = x[..., 0::2]
            x2 = x[..., 1::2]
            return jnp.concatenate([-x2 * sin + x1 * cos, x1 * sin + x2 * cos], axis=-1)
        if __name__ == '__main__':
            out = reference(**setup_inputs())
            print(out.shape)
        key = jax.random.key(seed)
        ks = jax.random.split(key, 8)
        s = 0.02
        B, T = (1, 256)
        return {'X': jax.random.normal(ks[0], (B, T, D_MODEL), jnp.float32), 'Wq': jax.random.normal(ks[1], (D_MODEL, H_TOT * DH), jnp.float32) * s, 'bq': jnp.zeros((H_TOT * DH,), jnp.float32), 'Wk': jax.random.normal(ks[2], (D_MODEL, D_MODEL), jnp.float32) * s, 'bk': jnp.zeros((D_MODEL,), jnp.float32), 'Wv': jax.random.normal(ks[3], (D_MODEL, H_TOT * DH), jnp.float32) * s, 'bv': jnp.zeros((H_TOT * DH,), jnp.float32), 'sink_scalars': jax.random.normal(ks[4], (H_TOT, 1, 1), jnp.float32) * s, 'v_nulls': jax.random.normal(ks[5], (H_TOT, DH), jnp.float32) * s, 'Wo': jax.random.normal(ks[6], (D_MODEL, D_MODEL), jnp.float32) * s, 'bo': jnp.zeros((D_MODEL,), jnp.float32)}
    _L0_attn_all = _L0_attn_setup()
    _L0_attn_in = {k: v for k, v in _L0_attn_all.items() if k in ('Wq', 'bq', 'Wk', 'bk', 'Wv', 'bv', 'sink_scalars', 'v_nulls', 'Wo', 'bo')}
    del _L0_attn_all

    def _L0_xattn_setup():
        import jax, jax.numpy as jnp
        import numpy as np
        H = 16
        key = jax.random.key(seed)
        ks = jax.random.split(key, 11)
        B, S, D = (4, 512, 256)
        s = 1.0 / np.sqrt(D)
        return {'query': jax.random.normal(ks[0], (B, S, D), jnp.float32), 'key': jax.random.normal(ks[1], (B, S, D), jnp.float32), 'value': jax.random.normal(ks[2], (B, S, D), jnp.float32), 'Wq': jax.random.normal(ks[3], (D, D), jnp.float32) * s, 'bq': jax.random.normal(ks[4], (D,), jnp.float32) * 0.01, 'Wk': jax.random.normal(ks[5], (D, D), jnp.float32) * s, 'bk': jax.random.normal(ks[6], (D,), jnp.float32) * 0.01, 'Wv': jax.random.normal(ks[7], (D, D), jnp.float32) * s, 'bv': jax.random.normal(ks[8], (D,), jnp.float32) * 0.01, 'Wo': jax.random.normal(ks[9], (D, D), jnp.float32) * s, 'bo': jax.random.normal(ks[10], (D,), jnp.float32) * 0.01}
    _L0_xattn_all = _L0_xattn_setup()
    _L0_xattn_in = {k: v for k, v in _L0_xattn_all.items() if k in ('Wq', 'bq', 'Wk', 'bk', 'Wv', 'bv', 'Wo', 'bo')}
    del _L0_xattn_all

    def _L0_ffn_setup():
        import jax, jax.numpy as jnp
        import numpy as np
        B, T, D, R, E = (32, 256, 256, 64, 8)
        key = jax.random.key(seed)
        ks = jax.random.split(key, 12)
        inp = {}
        inp['x'] = jax.random.normal(ks[0], (B, T, D), dtype=jnp.float32)
        inp['base_W'] = jax.random.normal(ks[1], (D, D), dtype=jnp.float32) * (1.0 / np.sqrt(D))
        inp['base_b'] = jax.random.normal(ks[2], (D,), dtype=jnp.float32) * 0.01
        inp['disc_mu'] = jax.random.normal(ks[3], (E, D), dtype=jnp.float32) * 0.5
        inp['disc_sigma'] = jax.random.uniform(ks[4], (E, D), dtype=jnp.float32, minval=0.5, maxval=1.5)
        inp['down_W'] = jax.random.normal(ks[5], (E, D, R), dtype=jnp.float32) * (1.0 / np.sqrt(D))
        inp['down_b'] = jax.random.normal(ks[6], (E, R), dtype=jnp.float32) * 0.01
        inp['up_W'] = jax.random.normal(ks[7], (E, R, D), dtype=jnp.float32) * (1.0 / np.sqrt(R))
        inp['up_b'] = jax.random.normal(ks[8], (E, D), dtype=jnp.float32) * 0.01
        inp['conv_W'] = jax.random.normal(ks[9], (E, D, D), dtype=jnp.float32) * 0.02
        inp['conv_b'] = jax.random.normal(ks[10], (E, D), dtype=jnp.float32) * 0.01
        return inp
    _L0_ffn_all = _L0_ffn_setup()
    _L0_ffn_in = {k: v for k, v in _L0_ffn_all.items() if k in ('base_W', 'base_b', 'disc_mu', 'disc_sigma', 'down_W', 'down_b', 'up_W', 'up_b', 'conv_W', 'conv_b')}
    del _L0_ffn_all

    def _L1_attn_setup():
        import jax, jax.numpy as jnp
        import numpy as np
        H = 16
        NB = 64
        NH = 6
        key = jax.random.key(seed)
        k = jax.random.split(key, 6)
        E = 256
        B, S = (2, 512)
        return {'x': jax.random.normal(k[0], (B, S, E), jnp.float32), 'Wq': jax.random.normal(k[1], (E, E), jnp.float32) * E ** (-0.5), 'bq': jax.random.normal(k[2], (E,), jnp.float32) * 0.02, 'Wv': jax.random.normal(k[3], (E, E), jnp.float32) * E ** (-0.5), 'bv': jax.random.normal(k[4], (E,), jnp.float32) * 0.02, 'hyperplanes': jax.random.normal(k[5], (E // H + 1, NH), jnp.float32)}
    _L1_attn_all = _L1_attn_setup()
    _L1_attn_in = {k: v for k, v in _L1_attn_all.items() if k in ('Wq', 'bq', 'Wv', 'bv', 'hyperplanes')}
    del _L1_attn_all

    def _L1_xattn_setup():
        import jax, jax.numpy as jnp
        import numpy as np
        DIM = 256
        HEADS = 16
        DIM_HEAD = 64
        INNER = HEADS * DIM_HEAD
        EPS = 1e-05

        def layer_norm(x, gamma, beta):
            mu = jnp.mean(x, axis=-1, keepdims=True)
            var = jnp.var(x, axis=-1, keepdims=True)
            return (x - mu) * jax.lax.rsqrt(var + EPS) * gamma + beta
        key = jax.random.key(seed)
        ks = jax.random.split(key, 8)
        b, n, m = (8, 1024, 64)
        x = jax.random.normal(ks[0], (b, n, DIM), dtype=jnp.float32)
        latents = jax.random.normal(ks[1], (b, m, DIM), dtype=jnp.float32)
        mask = jnp.ones((b, n), dtype=bool)
        s = 0.02
        Wq = jax.random.normal(ks[2], (DIM, INNER), dtype=jnp.float32) * s
        Wkv = jax.random.normal(ks[3], (DIM, 2 * INNER), dtype=jnp.float32) * s
        Wout = jax.random.normal(ks[4], (INNER, DIM), dtype=jnp.float32) * s
        g_x = jnp.ones((DIM,), jnp.float32)
        b_x = jnp.zeros((DIM,), jnp.float32)
        g_l = jnp.ones((DIM,), jnp.float32)
        b_l = jnp.zeros((DIM,), jnp.float32)
        g_o = jnp.ones((DIM,), jnp.float32)
        b_o = jnp.zeros((DIM,), jnp.float32)
        return {'x': x, 'latents': latents, 'mask': mask, 'g_x': g_x, 'b_x': b_x, 'g_l': g_l, 'b_l': b_l, 'Wq': Wq, 'Wkv': Wkv, 'Wout': Wout, 'g_o': g_o, 'b_o': b_o}
    _L1_xattn_all = _L1_xattn_setup()
    _L1_xattn_in = {k: v for k, v in _L1_xattn_all.items() if k in ('g_x', 'b_x', 'g_l', 'b_l', 'Wq', 'Wkv', 'Wout', 'g_o', 'b_o')}
    del _L1_xattn_all

    def _L1_ffn_setup():
        import jax, jax.numpy as jnp
        import numpy as np
        B, S, H, FFN, E = (2, 512, 256, 1024, 8)
        key = jax.random.key(seed)
        k0, k1, k2, k3 = jax.random.split(key, 4)
        return {'hidden_states': jax.random.normal(k0, (B, S, H), dtype=jnp.float32), 'Wr': jax.random.normal(k1, (H, E), dtype=jnp.float32) * 0.02, 'br': jnp.zeros((E,), dtype=jnp.float32), 'W1': jax.random.normal(k2, (E, H, FFN), dtype=jnp.float32) * 0.02, 'W2': jax.random.normal(k3, (E, FFN, H), dtype=jnp.float32) * 0.02}
    _L1_ffn_all = _L1_ffn_setup()
    _L1_ffn_in = {k: v for k, v in _L1_ffn_all.items() if k in ('Wr', 'br', 'W1', 'W2')}
    del _L1_ffn_all
    return {'x': x, 'ctx_1024': ctx_1024, 'mask_BxS2_bf1': mask_BxS2_bf1, 'L0_attn_Wq': _L0_attn_in['Wq'], 'L0_attn_bq': _L0_attn_in['bq'], 'L0_attn_Wk': _L0_attn_in['Wk'], 'L0_attn_bk': _L0_attn_in['bk'], 'L0_attn_Wv': _L0_attn_in['Wv'], 'L0_attn_bv': _L0_attn_in['bv'], 'L0_attn_sink_scalars': _L0_attn_in['sink_scalars'], 'L0_attn_v_nulls': _L0_attn_in['v_nulls'], 'L0_attn_Wo': _L0_attn_in['Wo'], 'L0_attn_bo': _L0_attn_in['bo'], 'L0_xattn_Wq': _L0_xattn_in['Wq'], 'L0_xattn_bq': _L0_xattn_in['bq'], 'L0_xattn_Wk': _L0_xattn_in['Wk'], 'L0_xattn_bk': _L0_xattn_in['bk'], 'L0_xattn_Wv': _L0_xattn_in['Wv'], 'L0_xattn_bv': _L0_xattn_in['bv'], 'L0_xattn_Wo': _L0_xattn_in['Wo'], 'L0_xattn_bo': _L0_xattn_in['bo'], 'L0_ffn_base_W': _L0_ffn_in['base_W'], 'L0_ffn_base_b': _L0_ffn_in['base_b'], 'L0_ffn_disc_mu': _L0_ffn_in['disc_mu'], 'L0_ffn_disc_sigma': _L0_ffn_in['disc_sigma'], 'L0_ffn_down_W': _L0_ffn_in['down_W'], 'L0_ffn_down_b': _L0_ffn_in['down_b'], 'L0_ffn_up_W': _L0_ffn_in['up_W'], 'L0_ffn_up_b': _L0_ffn_in['up_b'], 'L0_ffn_conv_W': _L0_ffn_in['conv_W'], 'L0_ffn_conv_b': _L0_ffn_in['conv_b'], 'L1_attn_Wq': _L1_attn_in['Wq'], 'L1_attn_bq': _L1_attn_in['bq'], 'L1_attn_Wv': _L1_attn_in['Wv'], 'L1_attn_bv': _L1_attn_in['bv'], 'L1_attn_hyperplanes': _L1_attn_in['hyperplanes'], 'L1_xattn_g_x': _L1_xattn_in['g_x'], 'L1_xattn_b_x': _L1_xattn_in['b_x'], 'L1_xattn_g_l': _L1_xattn_in['g_l'], 'L1_xattn_b_l': _L1_xattn_in['b_l'], 'L1_xattn_Wq': _L1_xattn_in['Wq'], 'L1_xattn_Wkv': _L1_xattn_in['Wkv'], 'L1_xattn_Wout': _L1_xattn_in['Wout'], 'L1_xattn_g_o': _L1_xattn_in['g_o'], 'L1_xattn_b_o': _L1_xattn_in['b_o'], 'L1_ffn_Wr': _L1_ffn_in['Wr'], 'L1_ffn_br': _L1_ffn_in['br'], 'L1_ffn_W1': _L1_ffn_in['W1'], 'L1_ffn_W2': _L1_ffn_in['W2']}

def reference(x, ctx_1024, mask_BxS2_bf1, L0_attn_Wq, L0_attn_bq, L0_attn_Wk, L0_attn_bk, L0_attn_Wv, L0_attn_bv, L0_attn_sink_scalars, L0_attn_v_nulls, L0_attn_Wo, L0_attn_bo, L0_xattn_Wq, L0_xattn_bq, L0_xattn_Wk, L0_xattn_bk, L0_xattn_Wv, L0_xattn_bv, L0_xattn_Wo, L0_xattn_bo, L0_ffn_base_W, L0_ffn_base_b, L0_ffn_disc_mu, L0_ffn_disc_sigma, L0_ffn_down_W, L0_ffn_down_b, L0_ffn_up_W, L0_ffn_up_b, L0_ffn_conv_W, L0_ffn_conv_b, L1_attn_Wq, L1_attn_bq, L1_attn_Wv, L1_attn_bv, L1_attn_hyperplanes, L1_xattn_g_x, L1_xattn_b_x, L1_xattn_g_l, L1_xattn_b_l, L1_xattn_Wq, L1_xattn_Wkv, L1_xattn_Wout, L1_xattn_g_o, L1_xattn_b_o, L1_ffn_Wr, L1_ffn_br, L1_ffn_W1, L1_ffn_W2):
    import jax
    import jax.numpy as jnp

    def _L0_attn_ref(X, Wq, bq, Wk, bk, Wv, bv, sink_scalars, v_nulls, Wo, bo):
        import jax, jax.numpy as jnp
        import numpy as np
        D_MODEL = 256
        N_HEAD = 16
        N_BR = 4
        DH = D_MODEL // N_HEAD
        H_TOT = N_BR * N_HEAD
        SCALE = float(np.pi / np.sqrt(3.0))
        ATTN_SCALE = DH ** (-0.5)

        def _rope(x):
            B, H, T, Dh = x.shape
            inv_freq = 1.0 / 10000.0 ** (jnp.arange(0, Dh, 2, dtype=jnp.float32) / Dh)
            t = jnp.arange(T, dtype=jnp.float32)
            freqs = t[:, None] * inv_freq[None, :]
            cos = jnp.cos(freqs)[None, None]
            sin = jnp.sin(freqs)[None, None]
            x1 = x[..., 0::2]
            x2 = x[..., 1::2]
            return jnp.concatenate([-x2 * sin + x1 * cos, x1 * sin + x2 * cos], axis=-1)
        if __name__ == '__main__':
            out = reference(**setup_inputs())
            print(out.shape)
        B, T, C = X.shape
        q = (X @ Wq + bq).reshape(B, T, H_TOT, DH).transpose(0, 2, 1, 3)
        v = (X @ Wv + bv).reshape(B, T, H_TOT, DH).transpose(0, 2, 1, 3)
        k_base = (X @ Wk + bk).reshape(B, T, N_HEAD, DH).transpose(0, 2, 1, 3)
        k = jnp.tile(k_base, (1, N_BR, 1, 1))
        q = _rope(q)
        k = _rope(k)
        scores = jnp.einsum('bhtd,bhsd->bhts', q, k) * ATTN_SCALE
        key_self = jnp.clip(jnp.sum(k * k, axis=-1), 1e-06, None)
        denom = jnp.sqrt(key_self)[:, :, None, :]
        w = jax.nn.softplus(scores / denom)
        causal = jnp.tril(jnp.ones((T, T), dtype=bool))
        w = jnp.where(causal[None, None], w, 0.0)
        w = w * jax.nn.sigmoid(SCALE * w)
        sinks = jnp.tanh(sink_scalars).reshape(1, H_TOT, 1, 1) + 1e-06
        alpha = 1.0 / (jnp.sum(w, axis=-1, keepdims=True) + sinks + 1e-06)
        probs_tokens = w * alpha
        probs_sink = sinks * alpha
        out_tokens = jnp.einsum('bhts,bhsd->bhtd', probs_tokens, v)
        out_sinks = probs_sink * v_nulls[None, :, None, :]
        context = out_tokens + out_sinks
        context = context.reshape(B, N_BR, N_HEAD, T, DH)
        context = context.transpose(0, 1, 3, 2, 4).reshape(B, N_BR, T, C)
        y = context @ Wo + bo
        return jnp.mean(y, axis=1)

    def _L0_xattn_ref(query, key, value, Wq, bq, Wk, bk, Wv, bv, Wo, bo):
        import jax, jax.numpy as jnp
        import numpy as np
        H = 16
        B, S, D = query.shape
        d_k = D // H

        def proj(x, W, b):
            y = jnp.einsum('bsd,ed->bse', x, W) + b
            return y.reshape(B, -1, H, d_k).transpose(0, 2, 1, 3)
        q = proj(query, Wq, bq)
        k = proj(key, Wk, bk)
        v = proj(value, Wv, bv)
        scores = jnp.einsum('bhqd,bhkd->bhqk', q, k) / jnp.sqrt(jnp.float32(d_k))
        p = jax.nn.softmax(scores, axis=-1)
        x = jnp.einsum('bhqk,bhkd->bhqd', p, v)
        x = x.transpose(0, 2, 1, 3).reshape(B, S, D)
        return jnp.einsum('bsd,ed->bse', x, Wo) + bo

    def _L0_ffn_ref(x, base_W, base_b, disc_mu, disc_sigma, down_W, down_b, up_W, up_b, conv_W, conv_b):
        import jax, jax.numpy as jnp
        import numpy as np
        B, T, D, R, E = (32, 256, 256, 64, 8)
        base = jnp.einsum('btd,od->bto', x, base_W) + base_b
        m1 = x.mean(axis=1)
        m2 = (x * x).mean(axis=1)
        inv_var = 1.0 / (disc_sigma * disc_sigma)
        losses = (jnp.einsum('bd,ed->eb', m2, inv_var) - 2.0 * jnp.einsum('bd,ed->eb', m1, disc_mu * inv_var) + jnp.sum(disc_mu * disc_mu * inv_var, axis=1)[:, None]) / D
        idx = jnp.argmin(losses, axis=0)
        Wd, bd = (down_W[idx], down_b[idx])
        Wu, bu = (up_W[idx], up_b[idx])
        Wc, bc = (conv_W[idx], conv_b[idx])
        h = jax.nn.relu(jnp.einsum('btd,bdr->btr', x, Wd) + bd[:, None, :])
        a = jnp.einsum('btr,brd->btd', h, Wu) + bu[:, None, :]
        y = jnp.einsum('btd,bod->bto', a, Wc) + bc[:, None, :]
        return base + y

    def _L1_attn_ref(x, Wq, bq, Wv, bv, hyperplanes):
        import jax, jax.numpy as jnp
        import numpy as np
        H = 16
        NB = 64
        NH = 6
        B, S, E = x.shape
        Dh = E // H
        q = (x @ Wq.T + bq).reshape(B, S, H, Dh)
        v = (x @ Wv.T + bv).reshape(B, S, H, Dh)
        qa = jnp.concatenate([q, jnp.ones((B, S, H, 1), q.dtype)], axis=-1)
        proj = jnp.einsum('bshe,en->bshn', qa, hyperplanes)
        bits = (proj >= 0).astype(jnp.int32)
        buckets = jnp.einsum('bshn,n->bsh', bits, 2 ** jnp.arange(NH, dtype=jnp.int32))
        b_hs = buckets.transpose(0, 2, 1)
        q = q.transpose(0, 2, 1, 3)
        v = v.transpose(0, 2, 1, 3)
        scores = jnp.einsum('bhsd,bhtd->bhst', q, q) / jnp.sqrt(jnp.float32(E))
        same = (b_hs[:, :, :, None] == b_hs[:, :, None, :]).astype(scores.dtype)
        coeff = NB - 2 + same
        attn = jax.nn.softmax(scores * coeff, axis=-1)
        out = jnp.einsum('bhst,bhtd->bhsd', attn, v)
        return out.transpose(0, 2, 1, 3).reshape(B, S, E)

    def _L1_xattn_ref(x, latents, mask, g_x, b_x, g_l, b_l, Wq, Wkv, Wout, g_o, b_o):
        import jax, jax.numpy as jnp
        import numpy as np
        DIM = 256
        HEADS = 16
        DIM_HEAD = 64
        INNER = HEADS * DIM_HEAD
        EPS = 1e-05

        def layer_norm(x, gamma, beta):
            mu = jnp.mean(x, axis=-1, keepdims=True)
            var = jnp.var(x, axis=-1, keepdims=True)
            return (x - mu) * jax.lax.rsqrt(var + EPS) * gamma + beta
        scale = DIM_HEAD ** (-0.5)
        xn = layer_norm(x, g_x, b_x)
        ln = layer_norm(latents, g_l, b_l)
        b, m = (ln.shape[0], ln.shape[1])
        q = jnp.einsum('bnd,de->bne', ln, Wq)
        kv_in = jnp.concatenate([xn, ln], axis=1)
        kv = jnp.einsum('bnd,de->bne', kv_in, Wkv)
        k, v = jnp.split(kv, 2, axis=-1)

        def split_heads(t):
            return t.reshape(t.shape[0], t.shape[1], HEADS, DIM_HEAD).transpose(0, 2, 1, 3)
        q, k, v = (split_heads(q), split_heads(k), split_heads(v))
        q = q * scale
        sim = jnp.einsum('bhid,bhjd->bhij', q, k)
        full_mask = jnp.concatenate([mask, jnp.ones((b, m), dtype=bool)], axis=1)
        max_neg = -jnp.finfo(sim.dtype).max
        sim = jnp.where(full_mask[:, None, None, :], sim, max_neg)
        attn = jax.nn.softmax(sim, axis=-1)
        out = jnp.einsum('bhij,bhjd->bhid', attn, v)
        out = out.transpose(0, 2, 1, 3).reshape(b, m, INNER)
        out = jnp.einsum('bne,ed->bnd', out, Wout)
        return layer_norm(out, g_o, b_o)

    def _L1_ffn_ref(hidden_states, Wr, br, W1, W2):
        import jax, jax.numpy as jnp
        import numpy as np
        B, S, H, FFN, E = (2, 512, 256, 1024, 8)
        b, s, h = hidden_states.shape
        x = hidden_states.reshape(-1, h)
        route = jax.nn.sigmoid(x @ Wr + br)
        max_prob = jnp.max(route, axis=1, keepdims=True)
        max_ind = jnp.argmax(route, axis=1)
        out = jnp.zeros_like(x)
        n_experts = Wr.shape[1]
        for e in range(n_experts):
            mask = (max_ind == e)[:, None].astype(x.dtype)
            y = jax.nn.gelu(x @ W1[e], approximate=False) @ W2[e]
            out = out + mask * y
        out = out * max_prob
        return out.reshape(b, s, h)
    x = _layernorm(x + _L0_attn_ref(x, L0_attn_Wq, L0_attn_bq, L0_attn_Wk, L0_attn_bk, L0_attn_Wv, L0_attn_bv, L0_attn_sink_scalars, L0_attn_v_nulls, L0_attn_Wo, L0_attn_bo), axis=-1)
    x = _layernorm(x + _L0_xattn_ref(x, ctx_1024, ctx_1024, L0_xattn_Wq, L0_xattn_bq, L0_xattn_Wk, L0_xattn_bk, L0_xattn_Wv, L0_xattn_bv, L0_xattn_Wo, L0_xattn_bo), axis=-1)
    x = _layernorm(x + _L0_ffn_ref(x, L0_ffn_base_W, L0_ffn_base_b, L0_ffn_disc_mu, L0_ffn_disc_sigma, L0_ffn_down_W, L0_ffn_down_b, L0_ffn_up_W, L0_ffn_up_b, L0_ffn_conv_W, L0_ffn_conv_b), axis=-1)
    x = _layernorm(x + _L1_attn_ref(x, L1_attn_Wq, L1_attn_bq, L1_attn_Wv, L1_attn_bv, L1_attn_hyperplanes), axis=-1)
    x = _layernorm(x + _L1_xattn_ref(ctx_1024, x, mask_BxS2_bf1, L1_xattn_g_x, L1_xattn_b_x, L1_xattn_g_l, L1_xattn_b_l, L1_xattn_Wq, L1_xattn_Wkv, L1_xattn_Wout, L1_xattn_g_o, L1_xattn_b_o), axis=-1)
    x = _layernorm(x + _L1_ffn_ref(x, L1_ffn_Wr, L1_ffn_br, L1_ffn_W1, L1_ffn_W2), axis=-1)
    return x

_drawn_inputs = setup_inputs


def setup_inputs(seed=0):
    import zlib

    import numpy as np

    out = dict(_drawn_inputs(seed))
    spreads = {'L0_attn_bq': (0.0, 0.8),
     'L0_attn_bk': (0.0, 0.8),
     'L0_attn_bv': (0.0, 0.455),
     'L0_attn_bo': (0.0, 0.1),
     'L1_xattn_g_x': (1.0, 0.2),
     'L1_xattn_b_x': (0.0, 0.1),
     'L1_xattn_g_l': (1.0, 0.2),
     'L1_xattn_b_l': (0.0, 0.1),
     'L1_xattn_g_o': (1.0, 0.2),
     'L1_xattn_b_o': (0.0, 0.1),
     'L1_ffn_br': (0.0, 0.1)}
    factors = {'L0_attn_Wq': 8.0,
     'L0_attn_Wk': 8.0,
     'L0_attn_Wv': 4.104,
     'L0_attn_sink_scalars': 8.0,
     'L0_attn_v_nulls': 64.0,
     'L0_xattn_bq': 22.817,
     'L0_xattn_bk': 64.0,
     'L0_xattn_bv': 5.444,
     'L0_xattn_bo': 4.448,
     'L0_ffn_base_b': 5.769,
     'L0_ffn_down_b': 31.025,
     'L0_ffn_up_b': 25.123,
     'L0_ffn_conv_b': 6.231,
     'L1_attn_bq': 3.37,
     'L1_attn_bv': 4.517,
     'L1_attn_hyperplanes': 14.403}
    for name, (base, spread) in spreads.items():
        noise = np.random.default_rng([zlib.crc32(name.encode()), seed]).standard_normal(out[name].shape)
        drawn = base * np.exp(spread * noise) if base else spread * noise
        out[name] = jnp.asarray(drawn.astype(out[name].dtype))
    for name, factor in factors.items():
        out[name] = (out[name] * factor).astype(out[name].dtype)
    return out
```

```python
from contextlib import ExitStack

import concourse.bass as bass
import numpy as np
from concourse import mybir

F32 = mybir.dt.float32
U32 = mybir.dt.uint32
U8 = mybir.dt.uint8
BF16 = mybir.dt.bfloat16
ALU = mybir.AluOpType
ACT = mybir.ActivationFunctionType
AX = mybir.AxisListType.X

P = 128
NB, T, D = 16, 100, 256
KD = D // P
NH = 16
DH = D // NH
HG = P // DH
NBR = 4
SC = 361
EPS = 1e-5
BIG = 1e30


class Chain:

    def __init__(self, eng, sem, per):
        self.eng, self.sem, self.per = eng, sem, per

    def start(self, i):
        self.base, self.n = i * self.per, 0

    def after(self, ins):
        ins.then_inc(self.sem, 1)
        self.n += 1
        self.eng.wait_ge(self.sem, self.base + self.n)

    def end(self):
        assert self.n == self.per, (self.sem, self.n)


class Stage:

    def __init__(self, nc, name):
        self.nc, self.name, self.ctx, self.sems = nc, name, ExitStack(), []

    def __enter__(self):
        self.ctx.__enter__()
        return self

    def __exit__(self, *a):
        if self.sems and a[0] is None:
            self.nc.clear_and_free_semaphores(self.sems)
            self.nc.all_engine_barrier()
        return self.ctx.__exit__(*a)

    def sb(self, name, shape, dt=F32):
        return self.ctx.enter_context(self.nc.sbuf_tensor(f"{self.name}_{name}", shape, dt))

    def ps(self, name, shape):
        return self.ctx.enter_context(self.nc.psum_tensor(f"{self.name}_{name}", shape, F32))

    def sem(self, name):
        self.sems.append(self.nc.alloc_semaphore(f"{self.name}_{name}"))
        return self.sems[-1]


def rows(w):
    return w.rearrange("(k p) n -> p k n", p=P)


def bcast(v, parts):
    n = v.shape[0]
    return v.rearrange("(a n) -> a n", a=1).broadcast_to([parts, n])


class Side:

    def __init__(self, slots, filled, read):
        self.slots, self.filled, self.read = slots, filled, read
        names = [s for slot in slots for s in slot]
        self.fronts = [s for s in names if s[0] == "f"]
        self.backs = [s for s in names if s[0] == "b"]
        self.all = names

    def steps(self, i, m):
        first, last = isinstance(i, int) and i == 0, isinstance(i, int) and i == NB - 1
        keep = [s for s in self.all if not (first and s[0] == "b") and not (last and s[0] == "f")]
        if first:
            base = len(self.fronts)
        else:
            base = 2 * len(self.fronts) + (i - 1) * len(self.all)
        return [(s, base + keep.index(s)) for s in self.slots[m] if s in keep]

    def prologue(self):
        return [(s, n) for n, s in enumerate(self.fronts)]

    def epilogue(self):
        base = NB * len(self.fronts) + (NB - 1) * len(self.backs)
        return [(s, base + n) for n, s in enumerate(self.backs)]

    def read_of(self, i, name):
        if isinstance(i, int) and i == 0:
            return self.fronts.index(name) + 1
        m = next(m for m, slot in enumerate(self.slots) if name in slot)
        return dict(self.steps(i - 1, m))[name] + 1

    def front_done(self, i):
        if isinstance(i, int) and i == 0:
            return len(self.fronts)
        last = max(self.all.index(s) for s in self.fronts)
        off = sum(1 for s in self.all[:last + 1] if s[0] == "b") if isinstance(i, int) and i == 1 else 0
        if isinstance(i, int) and i == 1:
            return len(self.fronts) + last + 1 - off
        return 2 * len(self.fronts) + (i - 2) * len(self.all) + last + 1


def above(eng, sem, n):
    if not isinstance(n, int) or n > 0:
        eng.wait_ge(sem, n)


def over_batches(eng, body, apart=1):
    body(0, 0)
    with eng.Fori(0, (NB - 1 - apart) // 2) as j:
        body(2 * j + 1, 1)
        body(2 * j + 2, 0)
    for i in range(NB - apart, NB):
        body(i, i % 2)


def self_attention(nc, X, ident, d):
    CS = float(np.pi / np.sqrt(3.0))
    NU = HG * NBR * T
    st = Stage(nc, "sa")
    with st:
        sb, ps, sem = st.sb, st.ps, st.sem
        wq, wv = sb("wq", [P, KD, NBR * D]), sb("wv", [P, KD, NBR * D])
        wk, wo = sb("wk", [P, KD, D]), sb("wo", [P, KD, D])
        bq, bv = sb("bq", [T, NBR * D]), sb("bv", [T, NBR * D])
        bk, bo = sb("bk", [T, D]), sb("bo", [T, D])
        cos, sin = sb("cos", [T, DH // 2]), sb("sin", [T, DH // 2])
        causal = sb("causal", [T, T])
        hmask = sb("hmask", [P, HG])
        sink, csk = sb("sink", [T, NBR * NH]), sb("csk", [T, NBR * NH])
        csvn = sb("csvn", [T, NBR * D])
        xs = sb("xs", [T, D])
        xT = sb("xT", [P, KD, T])
        qn, qr = sb("qn", [T, NBR * D]), sb("qr", [T, NBR * D])
        qa, qb = sb("qa", [T, NBR * D // 2]), sb("qb", [T, NBR * D // 2])
        kn, kr = sb("kn", [T, D]), sb("kr", [T, D])
        ka, kb = sb("ka", [T, D // 2]), sb("kb", [T, D // 2])
        ksq, kss, kf = sb("ksq", [T, D]), sb("kss", [T, NH]), sb("kf", [T, NH])
        va = sb("va", [T, NBR * NH, 32])
        qT = sb("qT", [P, KD, NBR, T])
        kTm = sb("kTm", [P, KD, HG, T])
        sm = sb("sm", [T, KD, HG, NBR, T])
        L = sb("L", [T, KD, HG, NBR, T])
        avT = sb("avT", [P, 4, T])
        oN = sb("oN", [T, NBR, HG, 32])
        den, alpha = sb("den", [T, NBR, HG]), sb("alpha", [T, NBR, HG])
        num = sb("num", [T, NBR, P])
        cx = sb("cx", [T, D])
        cxT = sb("cxT", [P, KD, T])
        xb, y = sb("xb", [T, D]), sb("y", [T, D])
        stats, mv, rs = sb("stats", [T, 6]), sb("mv", [T, 2]), sb("rs", [T, 2])
        eps = sb("eps", [T, 1])
        gap = sb("gap", [T, 1])
        pS = ps("pS", [P, 4, 512])
        pq = ps("pq", [P, 2, 512])
        pk = ps("pk", [P, 512])
        pb = ps("pb", [P, 512])

        s_w, s_c = sem("weights_loaded"), sem("consts_ready")
        s_xs, s_xTp, s_xT = sem("xs_staged"), sem("xT_in_psum"), sem("xT_ready")
        s_kp, s_kn, s_kr = sem("k_in_psum"), sem("k_read"), sem("k_roped")
        s_ks, s_kf = sem("k_square_sums"), sem("k_factors")
        s_kTp, s_kT = sem("kT_in_psum"), sem("kT_ready")
        s_qp, s_qn, s_qr = sem("q_in_psum"), sem("q_read"), sem("q_roped")
        s_qTp, s_qT = sem("qT_in_psum"), sem("qT_ready")
        s_vp, s_v = sem("v_in_psum"), sem("v_ready")
        s_S, s_sm = sem("scores_in_psum"), sem("scores_masked")
        s_L, s_W, s_G = sem("logs_ready"), sem("softplus_ready"), sem("gated_ready")
        s_av, s_avT = sem("av_in_psum"), sem("av_read")
        s_oNp, s_oN, s_nm = sem("out_in_psum"), sem("out_read"), sem("normed")
        s_cTp, s_cT, s_y, s_yr = sem("ctxT_in_psum"), sem("ctxT_ready"), sem("y_in_psum"), sem("y_read")
        s_mv, s_rs, s_x = sem("ln_stats"), sem("ln_rstd"), sem("x_done")
        s_xb = sem("x_plus_bias")
        s_dv, s_ac, s_po = sem("dve_chain"), sem("act_chain"), sem("pool_chain")
        NW = 14

        with nc.Block() as block:
            @block.sync
            def _(sp):
                for dst, src in ((wk[:], rows(d["L0_attn_Wk"])), (wq[:], rows(d["L0_attn_Wq"])),
                                 (wv[:], rows(d["L0_attn_Wv"])), (wo[:], rows(d["L0_attn_Wo"])),
                                 (bk[:], bcast(d["L0_attn_bk"], T)), (bq[:], bcast(d["L0_attn_bq"], T)),
                                 (bv[:], bcast(d["L0_attn_bv"], T)), (bo[:], bcast(d["L0_attn_bo"], T)),
                                 (cos[:], d["c_cos"]), (sin[:], d["c_sin"]),
                                 (causal[:], d["c_causal"]), (hmask[:], d["c_hmask"]),
                                 (sink[:], bcast(d["L0_attn_sink_scalars"].rearrange("a b c -> (a b c)"), T)),
                                 (csvn[:], bcast(d["L0_attn_v_nulls"].rearrange("a b -> (a b)"), T))):
                    sp.dma_start(dst, src).then_inc(s_w, 16)

            @block.tensor
            def _(pe):
                def front_k(i):
                    pe.wait_ge(s_xs, i + 1)
                    pe.wait_ge(s_kT, i)
                    for k in range(KD):
                        last = nc.tensor.transpose(pk[:, k * T:(k + 1) * T], xs[:, k * P:(k + 1) * P],
                                                   ident[0:T, 0:T])
                    last.then_inc(s_xTp, 1)
                    pe.wait_ge(s_xT, i + 1)
                    for k in range(KD):
                        last = nc.tensor.matmul(pk[0:T, 256:512], xT[:, k, :], wk[:, k, :],
                                                start=k == 0, stop=k == KD - 1)
                    last.then_inc(s_kp, 1)
                    pe.wait_ge(s_v, i)
                    for n in range(2):
                        for k in range(KD):
                            last = nc.tensor.matmul(pq[0:T, n, :], xT[:, k, :], wq[:, k, n * 512:(n + 1) * 512],
                                                    start=k == 0, stop=k == KD - 1)
                    last.then_inc(s_qp, 1)

                def front_t(i):
                    pe.wait_ge(s_kr, i + 1)
                    for k in range(KD):
                        last = nc.tensor.transpose(pk[:, k * T:(k + 1) * T], kr[:, k * P:(k + 1) * P],
                                                   ident[0:T, 0:T])
                    last.then_inc(s_kTp, 1)
                    pe.wait_ge(s_qr, i + 1)
                    pe.wait_ge(s_qn, i + 1)
                    for k in range(KD):
                        for r in range(NBR):
                            last = nc.tensor.transpose(pq[:, k, r * T:(r + 1) * T],
                                                       qr[:, r * D + k * P:r * D + (k + 1) * P], ident[0:T, 0:T])
                    last.then_inc(s_qTp, 1)

                def front_v(i):
                    pe.wait_ge(s_qT, i + 1)
                    for n in range(2):
                        for k in range(KD):
                            last = nc.tensor.matmul(pq[0:T, n, :], xT[:, k, :], wv[:, k, n * 512:(n + 1) * 512],
                                                    start=k == 0, stop=k == KD - 1)
                    last.then_inc(s_vp, 1)

                def scores(i, g):
                    if g == 0:
                        pe.wait_ge(s_kT, i + 1)
                        pe.wait_ge(s_qT, i + 1)
                    for m in range(HG // 2):
                        n = i * 8 + (g * 4 + m)
                        if not isinstance(n, int) or n > 1:
                            pe.wait_ge(s_sm, n - 1)
                        for e in range(2):
                            last = nc.tensor.matmul(pS[0:T, 2 * (m % 2) + e, 0:NBR * T], kTm[:, g, 2 * m + e, :],
                                                    qT[:, g, :, :], start=True, stop=True)
                        last.then_inc(s_S, 1)

                def values(i, g):
                    pe.wait_ge(s_G, i * 2 + (g + 1))
                    pe.wait_ge(s_v, i + 1)
                    for c in range(2):
                        n = i * 4 + (g * 2 + c)
                        pe.wait_ge(s_oN, n)
                        if c == 0 and g == 0:
                            pe.wait_ge(s_yr, i)
                        for rr in range(2):
                            r = 2 * c + rr
                            for m in range(2):
                                for j in range(4):
                                    hh = 4 * m + j
                                    last = nc.tensor.matmul(
                                        pb[32 * j:32 * j + 32, (2 * rr + m) * T:(2 * rr + m + 1) * T],
                                        va[:, r * NH + g * HG + hh, :], L[:, g, hh, r, :], start=True, stop=True)
                        last.then_inc(s_av, 1)
                        pe.wait_ge(s_avT, n + 1)
                        for q in range(4):
                            last = nc.tensor.transpose(pb[0:T, q * P:(q + 1) * P], avT[:, q, :], ident[:, :])
                        last.then_inc(s_oNp, 1)

                def out(i):
                    pe.wait_ge(s_nm, i * 2 + 2)
                    pe.wait_ge(s_oN, i * 4 + 4)
                    for k in range(KD):
                        last = nc.tensor.transpose(pb[:, k * T:(k + 1) * T], cx[:, k * P:(k + 1) * P],
                                                   ident[0:T, 0:T])
                    last.then_inc(s_cTp, 1)
                    pe.wait_ge(s_cT, i + 1)
                    for k in range(KD):
                        last = nc.tensor.matmul(pb[0:T, 256:512], cxT[:, k, :], wo[:, k, :],
                                                start=k == 0, stop=k == KD - 1)
                    last.then_inc(s_y, 1)

                def body(i, more):
                    scores(i, 0)
                    scores(i, 1)
                    if more:
                        front_k(i + 1)
                    values(i, 0)
                    if more:
                        front_t(i + 1)
                    values(i, 1)
                    if more:
                        front_v(i + 1)
                    out(i)

                pe.wait_ge(s_w, 16 * NW)
                front_k(0)
                front_t(0)
                front_v(0)
                body(0, True)
                with pe.Fori(1, NB - 1) as i:
                    body(i, True)
                body(NB - 1, False)

            @block.vector
            def _(dv):
                ch = Chain(dv, s_dv, 0)

                def front_a(i):
                    dv.wait_ge(s_kp, i)
                    dv.wait_ge(s_qp, i)
                    dv.wait_ge(s_xTp, i)
                    if not isinstance(i, int) or i:
                        dv.wait_ge(s_vp, i)
                    nc.vector.tensor_copy(xs[:], X[0:T, i, :]).then_inc(s_xs, 1)
                    dv.wait_ge(s_xTp, i + 1)
                    nc.vector.tensor_copy(xT[:, :, :].rearrange("p k t -> p (k t)"), pk[:, 0:KD * T])\
                        .then_inc(s_xT, 1)

                def front_b(i):
                    dv.wait_ge(s_kp, i + 1)
                    ch.after(nc.vector.tensor_tensor(kn[:], pk[0:T, 256:512], bk[:], ALU.add))
                    h = kn[:, :].rearrange("p (h c two) -> p h c two", h=NH, two=2)
                    x1, x2 = h[:, :, :, 0], h[:, :, :, 1]
                    o = kr[:, :].rearrange("p (h c) -> p h c", h=NH)
                    c = cos[:, :].unsqueeze(1).broadcast_to([T, NH, DH // 2])
                    s = sin[:, :].unsqueeze(1).broadcast_to([T, NH, DH // 2])
                    A = ka[:, :].rearrange("p (h c) -> p h c", h=NH)
                    B = kb[:, :].rearrange("p (h c) -> p h c", h=NH)
                    dv.wait_ge(s_kTp, i)
                    nc.vector.tensor_tensor(A, x1, c, ALU.mult).then_inc(s_dv, 1)
                    ch.n += 1
                    ch.after(nc.vector.tensor_tensor(B, x2, s, ALU.mult))
                    ch.after(nc.vector.tensor_tensor(o[:, :, 0:DH // 2], A, B, ALU.subtract))
                    nc.vector.tensor_tensor(A, x1, s, ALU.mult).then_inc(s_dv, 1)
                    ch.n += 1
                    ch.after(nc.vector.tensor_tensor(B, x2, c, ALU.mult))
                    ch.after(nc.vector.tensor_tensor(o[:, :, DH // 2:DH], A, B, ALU.add))
                    ch.after(nc.vector.tensor_tensor(ksq[:], kr[:], kr[:], ALU.mult))
                    ch.after(nc.vector.reduce_sum(kss[:], ksq[:, :].rearrange("p (h c) -> p h c", h=NH), AX))
                    nc.vector.tensor_scalar(kss[:], kss[:], 1e-6, None, ALU.max).then_inc(s_ks, 1)
                    dv.wait_ge(s_qp, i + 1)
                    dv.wait_ge(s_qr, i)
                    nc.vector.tensor_tensor(qn[:, :].rearrange("p (n c) -> p n c", n=2), pq[0:T, :, :],
                                            bq[:, :].rearrange("p (n c) -> p n c", n=2), ALU.add).then_inc(s_qn, 1)
                    dv.wait_ge(s_kf, i + 1)
                    nc.vector.tensor_tensor(o, o, kf[:, :].unsqueeze(2).broadcast_to([T, NH, DH]), ALU.mult)\
                        .then_inc(s_kr, 1)

                def front_c(i):
                    dv.wait_ge(s_kTp, i + 1)
                    kk = pk[:, 0:KD * T].rearrange("p (k t) -> p k t", k=KD)
                    for k in range(KD):
                        ins = nc.vector.tensor_tensor(kTm[:, k, :, :], kk[:, k, :].unsqueeze(1).broadcast_to([P, HG, T]),
                                                      hmask[:, :].unsqueeze(2).broadcast_to([P, HG, T]), ALU.mult)
                        if k == KD - 1:
                            ins.then_inc(s_kT, 1)
                        else:
                            ch.after(ins)

                def front_d(i):
                    dv.wait_ge(s_vp, i + 1)
                    nc.vector.tensor_tensor(va[:, :, 0:DH],
                                            pq[0:T, :, :].rearrange("p n (h c) -> p (n h) c", c=DH),
                                            bv[:, :].rearrange("p (h c) -> p h c", c=DH), ALU.add).then_inc(s_v, 1)

                def masked(i, g):
                    if g == 0:
                        dv.wait_ge(s_G, i * 2)
                        dv.wait_ge(s_av, i * 4)
                    for m in range(HG // 2):
                        n = i * 8 + (g * 4 + m)
                        dv.wait_ge(s_S, n + 1)
                        cm = causal[:, :].unsqueeze(1).broadcast_to([T, NBR, T])
                        for e in range(2):
                            ins = nc.vector.tensor_tensor(
                                sm[:, g, 2 * m + e, :, :],
                                pS[0:T, 2 * (m % 2) + e, 0:NBR * T].rearrange("p (r t) -> p r t", r=NBR), cm, ALU.add)
                            if e:
                                ch.after(ins)
                        nc.vector.tensor_scalar(
                            L[:, g, 2 * m:2 * m + 2, :, :].rearrange("p h r t -> p (h r t)"),
                            sm[:, g, 2 * m:2 * m + 2, :, :].rearrange("p h r t -> p (h r t)"),
                            30.0, None, ALU.min).then_inc(s_sm, 1)

                def softplus(i, g):
                    dv.wait_ge(s_L, i * 2 + (g + 1))
                    nc.vector.tensor_tensor(L[:, g].rearrange("p h r t -> p (h r t)"),
                                            L[:, g].rearrange("p h r t -> p (h r t)"),
                                            sm[:, g].rearrange("p h r t -> p (h r t)"), ALU.max).then_inc(s_W, 1)

                def norm(i, g):
                    dv.wait_ge(s_oN, i * 4 + (g + 1) * 2)
                    k3 = csk[:, :].rearrange("p (r g h) -> p r g h", r=NBR, g=KD)[:, :, g, :]
                    v4 = csvn[:, :].rearrange("p (r g c) -> p r g c", r=NBR, g=KD)[:, :, g, :]
                    ch.after(nc.vector.tensor_tensor(den[:], oN[:, :, :, DH], k3, ALU.add))
                    ch.after(nc.vector.reciprocal(alpha[:], den[:]))
                    for r in range(NBR):
                        ins = nc.vector.tensor_tensor(num[:, r, :].rearrange("p (h c) -> p h c", c=DH),
                                                      oN[:, r, :, 0:DH],
                                                      v4[:, r, :].rearrange("p (h c) -> p h c", c=DH), ALU.add)
                        ins.then_inc(s_dv, 1)
                        ch.n += 1
                    dv.wait_ge(s_dv, ch.base + ch.n)
                    n3 = num[:, :, :].rearrange("p r (h c) -> p (r h) c", c=DH)
                    ch.after(nc.vector.tensor_tensor(
                        n3, n3, alpha[:, :, :].rearrange("p r h -> p (r h)").unsqueeze(2)
                        .broadcast_to([T, NBR * HG, DH]), ALU.mult))
                    if g == 0:
                        dv.wait_ge(s_cTp, i)
                    nc.vector.reduce_sum(cx[:, g * P:(g + 1) * P], num[:, :, :].rearrange("p r c -> p c r"), AX)\
                        .then_inc(s_nm, 1)

                def finish(i):
                    dv.wait_ge(s_cTp, i + 1)
                    nc.vector.tensor_copy(cxT[:, :, :].rearrange("p k t -> p (k t)"), pb[:, 0:KD * T])\
                        .then_inc(s_cT, 1)
                    dv.wait_ge(s_y, i + 1)
                    dv.wait_ge(s_xb, i + 1)
                    nc.vector.scalar_tensor_tensor(out=y[:], in0=pb[0:T, 256:512], scalar=1.0 / NBR, in1=xb[:],
                                                   op0=ALU.mult, op1=ALU.add).then_inc(s_yr, 1)
                    dv.wait_ge(s_yr, i + 1)
                    ch.after(nc.vector.bn_stats(stats[:], y[:]))
                    nc.vector.memset(gap[:], 0.0)
                    nc.vector.bn_aggr(mv[:], stats[:]).then_inc(s_mv, 1)
                    dv.wait_ge(s_rs, i + 1)
                    nc.vector.tensor_scalar(X[0:T, i, :], y[:], mv[:, 0:1], rs[:, 1:2], ALU.subtract, ALU.mult)\
                        .then_inc(s_x, 1)

                def body(i, more):
                    ch.start(i)
                    ch.base = PRE + i * PER
                    masked(i, 0)
                    masked(i, 1)
                    if more:
                        front_a(i + 1)
                    softplus(i, 0)
                    if more:
                        front_b(i + 1)
                    softplus(i, 1)
                    norm(i, 0)
                    if more:
                        front_c(i + 1)
                    norm(i, 1)
                    if more:
                        front_d(i + 1)
                    finish(i)
                    assert ch.n == (PER if more else PER - FR), ch.n

                FR, SET = 10, 7
                PRE, PER = SET + FR, FR + 8 + 2 * 7 + 1
                ch.base, ch.n = 0, 0
                ch.after(nc.vector.memset(va[:], 0.0))
                ch.after(nc.vector.memset(va[:, :, DH:DH + 1], 1.0))
                ch.after(nc.vector.memset(eps[:], EPS))
                dv.wait_ge(s_w, 16 * NW)
                dv.wait_ge(s_c, 1)
                ch.after(nc.vector.tensor_scalar(sink[:], sink[:], 1e-6, None, ALU.add))
                ch.after(nc.vector.tensor_scalar(csk[:], sink[:], 1e-6, CS, ALU.add, ALU.mult))
                v3 = csvn[:, :].rearrange("p (h c) -> p h c", c=DH)
                ch.after(nc.vector.tensor_tensor(v3, v3, sink[:, :].unsqueeze(2).broadcast_to([T, NBR * NH, DH]),
                                                 ALU.mult))
                ch.after(nc.vector.tensor_scalar(csvn[:], csvn[:], CS, None, ALU.mult))
                assert ch.n == SET
                front_a(0)
                front_b(0)
                front_c(0)
                front_d(0)
                assert ch.n == PRE, ch.n
                body(0, True)
                with dv.Fori(1, NB - 1) as i:
                    body(i, True)
                body(NB - 1, False)

            @block.scalar
            def _(ac):
                def factors(i):
                    ac.wait_ge(s_ks, i + 1)
                    nc.scalar.activation(kf[:], kss[:], ACT.Ln).then_inc(s_ac, 1)
                    n = i * 5 if not isinstance(i, int) or i else 1
                    ac.wait_ge(s_ac, n)
                    nc.scalar.activation(kf[:], kf[:], ACT.Exp, scale=-0.5).then_inc(s_ac, 1)
                    ac.wait_ge(s_ac, n + 1)
                    nc.scalar.mul(kf[:], kf[:], DH ** -0.5).then_inc(s_kf, 1)

                def front(i):
                    ac.wait_ge(s_qTp, i + 1)
                    nc.scalar.copy(qT[:, :, :, :].rearrange("p k r t -> p k (r t)"), pq[:, :, 0:NBR * T])\
                        .then_inc(s_qT, 1)

                def logs(i, g):
                    for m in range(HG // 2):
                        ac.wait_ge(s_sm, i * 8 + (g * 4 + m + 1))
                        v = L[:, g, 2 * m:2 * m + 2].rearrange("p h r t -> p (h r t)")
                        ins = nc.scalar.activation(v, v, ACT.Exp)
                    ins.then_inc(s_ac, 1)
                    ac.wait_ge(s_ac, i * 5 + (3 + g))
                    v = L[:, g].rearrange("p h r t -> p (h r t)")
                    nc.scalar.activation(v, v, ACT.Ln, bias=1.0).then_inc(s_L, 1)

                def gate(i, g):
                    ac.wait_ge(s_W, i * 2 + (g + 1))
                    v = L[:, g].rearrange("p h r t -> p (h r t)")
                    nc.scalar.activation(v, v, ACT.Silu, scale=CS).then_inc(s_G, 1)

                def evacs(i, g):
                    for c in range(2):
                        n = i * 4 + (g * 2 + c)
                        ac.wait_ge(s_av, n + 1)
                        ac.wait_ge(s_oNp, n)
                        nc.scalar.copy(avT[:, :, :].rearrange("p q t -> p (q t)"), pb[:, 0:4 * T]).then_inc(s_avT, 1)
                        ac.wait_ge(s_oNp, n + 1)
                        if c == 0:
                            ac.wait_ge(s_nm, i * 2 + g)
                        nc.scalar.copy(oN[:, 2 * c:2 * c + 2, :, :].rearrange("p r h c -> p (r h c)"), pb[0:T, :])\
                            .then_inc(s_oN, 1)

                def rstd(i, last=False):
                    ac.wait_ge(s_mv, i + 1)
                    nc.scalar.activation(rs[:, 0:1], mv[:, 1:2], ACT.Ln, bias=eps[:, 0:1]).then_inc(s_ac, 1)
                    ac.wait_ge(s_ac, i * 5 + (5 if last else 7))
                    nc.scalar.activation(rs[:, 1:2], rs[:, 0:1], ACT.Exp, scale=-0.5).then_inc(s_rs, 1)

                def body(i, more):
                    logs(i, 0)
                    logs(i, 1)
                    if more:
                        factors(i + 1)
                    gate(i, 0)
                    gate(i, 1)
                    evacs(i, 0)
                    if more:
                        front(i + 1)
                    evacs(i, 1)
                    rstd(i, not more)

                ac.wait_ge(s_w, 16 * NW)
                nc.scalar.activation(sink[:], sink[:], ACT.Tanh).then_inc(s_c, 1)
                factors(0)
                front(0)
                body(0, True)
                with ac.Fori(1, NB - 1) as i:
                    body(i, True)
                body(NB - 1, False)

            @block.gpsimd
            def _(po):
                def rope_q(i):
                    po.wait_ge(s_qn, i + 1)
                    h = qn[:, :].rearrange("p (h c two) -> p h c two", two=2, c=DH // 2)
                    x1, x2 = h[:, :, :, 0], h[:, :, :, 1]
                    o = qr[:, :].rearrange("p (h c) -> p h c", c=DH)
                    c = cos[:, :].unsqueeze(1).broadcast_to([T, NBR * NH, DH // 2])
                    s = sin[:, :].unsqueeze(1).broadcast_to([T, NBR * NH, DH // 2])
                    A = qa[:, :].rearrange("p (h c) -> p h c", c=DH // 2)
                    B = qb[:, :].rearrange("p (h c) -> p h c", c=DH // 2)
                    b = i * 5
                    nc.gpsimd.tensor_tensor(A, x1, c, ALU.mult).then_inc(s_po, 1)
                    nc.gpsimd.tensor_tensor(B, x2, s, ALU.mult).then_inc(s_po, 1)
                    po.wait_ge(s_po, b + 2)
                    po.wait_ge(s_qTp, i)
                    nc.gpsimd.tensor_tensor(o[:, :, 0:DH // 2], A, B, ALU.subtract).then_inc(s_po, 1)
                    po.wait_ge(s_po, b + 3)
                    nc.gpsimd.tensor_tensor(A, x1, s, ALU.mult).then_inc(s_po, 1)
                    nc.gpsimd.tensor_tensor(B, x2, c, ALU.mult).then_inc(s_po, 1)
                    po.wait_ge(s_po, b + 5)
                    nc.gpsimd.tensor_tensor(o[:, :, DH // 2:DH], A, B, ALU.add).then_inc(s_qr, 1)

                def residual(i):
                    po.wait_ge(s_yr, i)
                    nc.gpsimd.tensor_tensor(xb[:], X[0:T, i, :], bo[:], ALU.add).then_inc(s_xb, 1)

                def body(i, more):
                    residual(i)
                    if more:
                        rope_q(i + 1)

                po.wait_ge(s_w, 16 * NW)
                rope_q(0)
                body(0, True)
                with po.Fori(1, NB - 1) as i:
                    body(i, True)
                body(NB - 1, False)


def turned(nc, st, names, d, ident):
    nat = [st.sb(f"{n}_nat", [P, KD, D]) for n in names]
    res = [st.sb(f"{n}_T", [P, KD, D]) for n in names]
    bank = Stage(nc, st.name + "t")
    s_l, s_p, s_r = st.sem("turn_loaded"), st.sem("turn_filled"), st.sem("turn_read")
    with bank, nc.Block() as block:
        pt = bank.ps("turn", [P, 512])

        @block.sync
        def _(sp):
            for n, t in zip(names, nat):
                sp.dma_start(t[:], rows(d[n])).then_inc(s_l, 16)

        @block.tensor
        def _(pe):
            pe.wait_ge(s_l, 16 * len(names))
            for w, t in enumerate(nat):
                above(pe, s_r, w)
                for k in range(KD):
                    for o in range(KD):
                        last = nc.tensor.transpose(pt[:, k * D + o * P:k * D + (o + 1) * P],
                                                   t[:, o, k * P:(k + 1) * P], ident[:, :])
                last.then_inc(s_p, 1)

        @block.scalar
        def _(ac):
            for w, r in enumerate(res):
                ac.wait_ge(s_p, w + 1)
                nc.scalar.copy(r[:, :, :].rearrange("p k n -> p (k n)"), pt[:, :]).then_inc(s_r, 1)
            ac.wait_ge(s_r, len(names))
    return res


def cross_attention(nc, X, ident, d):
    NC, KP_ = 3, 3 * P
    MP = NH // 2
    SCALE = DH ** -0.5
    keys = [P, P, SC - 2 * P]
    SLOTS = [["fx"], ["fc0", "fc1"], ["bo", "fk0"], ["fk1", "fq"], ["bp", "fv0"], ["by", "fv1"], [], []]
    st = Stage(nc, "ca")
    with st:
        sb, ps, sem = st.sb, st.ps, st.sem
        wqT, wkT, wvT, woT = turned(nc, st, ["L0_xattn_Wq", "L0_xattn_Wk", "L0_xattn_Wv", "L0_xattn_Wo"], d, ident)
        bq, bk = sb("bq", [P, KD]), sb("bk", [P, KD])
        bv, bo = sb("bv", [P, D]), sb("bo", [T, D])
        hmask = sb("hmask", [P, HG])
        xs, xT = sb("xs", [T, D]), sb("xT", [P, KD, T])
        cn = sb("cn", [P, NC, D])
        cT = sb("cT", [P, KD, SC])
        kT = [sb(f"kT{b}", [P, KD, SC]) for b in range(2)]
        qTm = [sb(f"qTm{b}", [P, KD, HG, T]) for b in range(2)]
        va = [sb(f"va{b}", [P, NC, NH, 32]) for b in range(2)]
        nm = [sb(f"nm{b}", [T, 2]) for b in range(2)]
        pr = [sb(f"pr{b}", [T, 2, KP_]) for b in range(2)]
        pT = [sb(f"pT{b}", [P, 2, NC * T]) for b in range(2)]
        avT = sb("avT", [P, 4, T])
        rc = sb("rc", [T, NH])
        o, oT = sb("o", [T, D]), sb("oT", [P, KD, T])
        xb, y = sb("xb", [T, D]), sb("y", [T, D])
        stats, mv, rs, eps = sb("stats", [T, 6]), sb("mv", [T, 2]), sb("rs", [T, 2]), sb("eps", [T, 1])
        gap = sb("gap", [T, 1])
        pS = ps("pS", [P, 4, 512])
        pPT = ps("pPT", [P, 2, 512])
        pav = ps("pav", [P, 512])
        pf = ps("side", [P, 512])

        s_w, s_z = sem("weights_loaded"), sem("padding_zeroed")
        s_cn = sem("context_loaded")
        s_xs = sem("xs_staged")
        s_F, s_R = sem("side_filled"), sem("side_read")
        s_S, s_mx, s_P = sem("scores_in_psum"), sem("max_ready"), sem("exp_ready")
        s_PTp, s_PT, s_AV = sem("probsT_in_psum"), sem("probsT_ready"), sem("values_summed")
        s_av = sem("sums_read")
        s_xb, s_y, s_mv, s_ln, s_rs, s_x = (sem(n) for n in ("x_plus_bias", "y_ready", "ln_stats", "ln_log",
                                                             "ln_rstd", "x_done"))
        s_dv = sem("dve_chain")
        side = Side(SLOTS, s_F, s_R)
        NW = 5

        with nc.Block() as block:
            @block.sync
            def _(sp):
                for dst, src in ((bq[:], d["L0_xattn_bq"].rearrange("(k p) -> p k", p=P)),
                                 (bk[:], d["L0_xattn_bk"].rearrange("(k p) -> p k", p=P)),
                                 (bv[:], bcast(d["L0_xattn_bv"], P)), (bo[:], bcast(d["L0_xattn_bo"], T)),
                                 (hmask[:], d["c_hmask"])):
                    with nc.allow_non_contiguous_dma("a bias by partition"):
                        sp.dma_start(dst, src).then_inc(s_w, 16)

                def load(i):
                    if not isinstance(i, int) or i:
                        sp.wait_ge(s_R, side.read_of(i - 1, "fc1"))
                    sp.dma_start(cn[:, 0:2, :], d["ctx_1024"][i, 0:2 * P, :].rearrange("(c p) n -> p c n", p=P))\
                        .then_inc(s_cn, 16)
                    sp.dma_start(cn[0:keys[2], 2, :], d["ctx_1024"][i, 2 * P:SC, :]).then_inc(s_cn, 16)
                for i in range(3):
                    load(i)
                with sp.Fori(3, NB) as i:
                    load(i)

            @block.tensor
            def _(pe):
                def step(name, n, i, b):
                    if name == "fx":
                        pe.wait_ge(s_xs, i + 1)
                    if name == "fc0":
                        pe.wait_ge(s_cn, 32 * i + 32)
                    above(pe, s_R, n)
                    if name == "fx":
                        for k in range(KD):
                            last = nc.tensor.transpose(pf[:, k * T:(k + 1) * T], xs[:, k * P:(k + 1) * P],
                                                       ident[0:T, 0:T])
                    elif name in ("fc0", "fc1"):
                        k = int(name[-1])
                        for c in range(NC):
                            last = nc.tensor.transpose(pf[:, c * P:c * P + keys[c]],
                                                       cn[0:keys[c], c, k * P:(k + 1) * P],
                                                       ident[0:keys[c], 0:keys[c]])
                    elif name in ("fk0", "fk1"):
                        e = int(name[-1])
                        for k in range(KD):
                            last = nc.tensor.matmul(pf[:, 0:SC], wkT[:, k, e * P:(e + 1) * P], cT[:, k, :],
                                                    start=k == 0, stop=k == KD - 1)
                    elif name == "fq":
                        for e in range(KD):
                            for k in range(KD):
                                last = nc.tensor.matmul(pf[:, e * T:(e + 1) * T], wqT[:, k, e * P:(e + 1) * P],
                                                        xT[:, k, :], start=k == 0, stop=k == KD - 1)
                    elif name in ("fv0", "fv1"):
                        for c in ((0, 1) if name == "fv0" else (2,)):
                            for k in range(KD):
                                last = nc.tensor.matmul(pf[0:keys[c], (c % 2) * D:(c % 2 + 1) * D],
                                                        cT[:, k, c * P:c * P + keys[c]], wvT[:, k, :],
                                                        start=k == 0, stop=k == KD - 1)
                    elif name == "bo":
                        pe.wait_ge(s_av, i + 1)
                        for q in range(4):
                            last = nc.tensor.transpose(pf[0:T, q * P:(q + 1) * P], avT[:, q, :], ident[:, :])
                    elif name == "bp":
                        for k in range(KD):
                            last = nc.tensor.transpose(pf[:, k * T:(k + 1) * T], o[:, k * P:(k + 1) * P],
                                                       ident[0:T, 0:T])
                    elif name == "by":
                        for k in range(KD):
                            last = nc.tensor.matmul(pf[0:T, 0:D], oT[:, k, :], woT[:, k, :],
                                                    start=k == 0, stop=k == KD - 1)
                    last.then_inc(s_F, 1)

                def scores(i, b, m):
                    n = i * MP + m
                    if m == 0:
                        pe.wait_ge(s_R, side.front_done(i))
                    above(pe, s_P, n - 1)
                    for e in range(2):
                        h = 2 * m + e
                        last = nc.tensor.matmul(pS[0:T, 2 * (m % 2) + e, 0:SC], qTm[b][:, h // HG, h % HG, :],
                                                kT[b][:, h // HG, :], start=True, stop=True)
                    last.then_inc(s_S, 1)

                def turn(n, m):
                    pe.wait_ge(s_P, n + 1)
                    above(pe, s_PT, n)
                    for e in range(2):
                        for c in range(NC):
                            last = nc.tensor.transpose(pPT[:, e, c * T:(c + 1) * T],
                                                       pr[m % 2][:, e, c * P:(c + 1) * P], ident[0:T, 0:T])
                    last.then_inc(s_PTp, 1)

                def values(n, i, b, m):
                    pe.wait_ge(s_PT, n + 1)
                    if m == 0:
                        above(pe, s_av, i)
                    for e in range(2):
                        h = 2 * m + e
                        j = h % 4
                        for c in range(NC):
                            last = nc.tensor.matmul(pav[32 * j:32 * j + 32, (h // 4) * T:(h // 4 + 1) * T],
                                                    va[b][:, c, h, :], pT[m % 2][:, e, c * T:(c + 1) * T],
                                                    start=c == 0, stop=c == NC - 1)
                    last.then_inc(s_AV, 1)

                def behind(i, b, m):
                    first = isinstance(i, int) and i == 0
                    n = i * MP + m
                    if m >= 1 or not first:
                        turn(n - 1, (m - 1) % MP)
                    if m >= 2:
                        values(n - 2, i, b, m - 2)
                    elif not first:
                        values(n - 2, i - 1, 1 - b, MP - 2 + m)

                def body(i, b):
                    for m in range(MP):
                        scores(i, b, m)
                        behind(i, b, m)
                        for name, n in side.steps(i, m):
                            step(name, n, i + 1 if name[0] == "f" else i - 1, 1 - b)

                pe.wait_ge(s_w, 16 * NW)
                pe.wait_ge(s_z, 1)
                for name, n in side.prologue():
                    step(name, n, 0, 0)
                over_batches(pe, body)
                n = NB * MP
                turn(n - 1, MP - 1)
                values(n - 2, NB - 1, 1, MP - 2)
                values(n - 1, NB - 1, 1, MP - 1)
                for name, k in side.epilogue():
                    step(name, k, NB - 1, 0)

            @block.vector
            def _(dv):
                ch = Chain(dv, s_dv, 0)
                SET = 9

                def step(name, n, i, b):
                    if name == "fx":
                        return
                    if name == "fq":
                        dv.wait_ge(s_F, n + 1)
                        for e in range(KD):
                            ins = nc.vector.scalar_tensor_tensor(
                                out=qTm[b][:, e, :, :],
                                in0=pf[:, e * T:(e + 1) * T].unsqueeze(1).broadcast_to([P, HG, T]),
                                scalar=bq[:, e:e + 1], in1=hmask[:, :].unsqueeze(2).broadcast_to([P, HG, T]),
                                op0=ALU.add, op1=ALU.mult)
                        ins.then_inc(s_R, 1)
                    elif name in ("fv0", "fv1"):
                        dv.wait_ge(s_F, n + 1)
                        for c in ((0, 1) if name == "fv0" else (2,)):
                            ins = nc.vector.tensor_tensor(
                                va[b][0:keys[c], c, :, 0:DH],
                                pf[0:keys[c], (c % 2) * D:(c % 2 + 1) * D].rearrange("p (h c) -> p h c", c=DH),
                                bv[0:keys[c], :].rearrange("p (h c) -> p h c", c=DH), ALU.add)
                        ins.then_inc(s_R, 1)
                    elif name == "bo":
                        dv.wait_ge(s_F, n + 1)
                        o4 = pf[0:T, :].rearrange("p (h c) -> p h c", c=32)
                        nc.vector.reciprocal(rc[:], o4[:, :, DH]).then_inc(s_dv, 1)
                        dv.wait_ge(s_dv, SET + 2 * i + 1)
                        nc.vector.tensor_tensor(o[:, :].rearrange("p (h c) -> p h c", c=DH), o4[:, :, 0:DH],
                                                rc[:, :].unsqueeze(2).broadcast_to([T, NH, DH]), ALU.mult)\
                            .then_inc(s_R, 1)
                    elif name == "by":
                        dv.wait_ge(s_F, n + 1)
                        dv.wait_ge(s_xb, i + 1)
                        nc.vector.tensor_tensor(y[:], pf[0:T, 0:D], xb[:], ALU.add).then_inc(s_R, 1)
                        dv.wait_ge(s_R, n + 1)
                        nc.vector.bn_stats(stats[:], y[:]).then_inc(s_dv, 1)
                        dv.wait_ge(s_dv, SET + 2 * i + 2)
                        nc.vector.memset(gap[:], 0.0)
                        nc.vector.bn_aggr(mv[:], stats[:]).then_inc(s_mv, 1)
                        dv.wait_ge(s_rs, i + 1)
                        nc.vector.tensor_scalar(X[0:T, i, :], y[:], mv[:, 0:1], rs[:, 1:2], ALU.subtract, ALU.mult)\
                            .then_inc(s_x, 1)

                def maxima(i, m):
                    n = i * MP + m
                    dv.wait_ge(s_S, n + 1)
                    above(dv, s_P, n - 1)
                    nc.vector.reduce_max(nm[m % 2][:], pS[0:T, 2 * (m % 2):2 * (m % 2) + 2, 0:SC], AX)\
                        .then_inc(s_mx, 1)
                    dv.wait_ge(s_mx, 2 * n + 1)
                    nc.vector.tensor_scalar(nm[m % 2][:], nm[m % 2][:], -SCALE, None, ALU.mult).then_inc(s_mx, 1)

                def evac(n, m):
                    dv.wait_ge(s_PTp, n + 1)
                    above(dv, s_AV, n - 1)
                    nc.vector.tensor_copy(pT[m % 2][:], pPT[:, :, 0:NC * T]).then_inc(s_PT, 1)

                def body(i, b):
                    for m in range(MP):
                        maxima(i, m)
                        if m or not (isinstance(i, int) and i == 0):
                            evac(i * MP + m - 1, (m - 1) % MP)
                        for name, n in side.steps(i, m):
                            step(name, n, i + 1 if name[0] == "f" else i - 1, 1 - b)

                ch.base, ch.n = 0, 0
                for b in range(2):
                    ch.after(nc.vector.memset(va[b][:], 0.0))
                    ch.after(nc.vector.memset(va[b][:, 0:2, :, DH:DH + 1], 1.0))
                    ch.after(nc.vector.memset(va[b][0:keys[2], 2, :, DH:DH + 1], 1.0))
                    ch.after(nc.vector.memset(pr[b][:], 0.0))
                ch.after(nc.vector.memset(eps[:], EPS))
                assert ch.n == SET
                nc.vector.memset(rc[:], 0.0).then_inc(s_z, 1)
                dv.wait_ge(s_z, 1)
                dv.wait_ge(s_w, 16 * NW)
                for name, n in side.prologue():
                    step(name, n, 0, 0)
                over_batches(dv, body)
                evac(NB * MP - 1, MP - 1)
                for name, n in side.epilogue():
                    step(name, n, NB - 1, 0)

            @block.scalar
            def _(ac):
                def step(name, n, i, b):
                    if name in ("fx", "bp"):
                        ac.wait_ge(s_F, n + 1)
                        dst = xT if name == "fx" else oT
                        nc.scalar.copy(dst[:, :, :].rearrange("p k t -> p (k t)"), pf[:, 0:KD * T]).then_inc(s_R, 1)
                    elif name in ("fc0", "fc1"):
                        ac.wait_ge(s_F, n + 1)
                        nc.scalar.copy(cT[:, int(name[-1]), :], pf[:, 0:SC]).then_inc(s_R, 1)
                    elif name in ("fk0", "fk1"):
                        e = int(name[-1])
                        ac.wait_ge(s_F, n + 1)
                        nc.scalar.activation(kT[b][:, e, :], pf[:, 0:SC], ACT.Identity, bias=bk[:, e:e + 1])\
                            .then_inc(s_R, 1)
                    elif name == "by":
                        ac.wait_ge(s_mv, i + 1)
                        nc.scalar.activation(rs[:, 0:1], mv[:, 1:2], ACT.Ln, bias=eps[:, 0:1]).then_inc(s_ln, 1)
                        ac.wait_ge(s_ln, i + 1)
                        nc.scalar.activation(rs[:, 1:2], rs[:, 0:1], ACT.Exp, scale=-0.5).then_inc(s_rs, 1)

                def exps(i, m):
                    n = i * MP + m
                    ac.wait_ge(s_mx, 2 * n + 2)
                    above(ac, s_PTp, n - 1)
                    for e in range(2):
                        ins = nc.scalar.activation(pr[m % 2][:, e, 0:SC], pS[0:T, 2 * (m % 2) + e, 0:SC], ACT.Exp,
                                                   bias=nm[m % 2][:, e:e + 1], scale=SCALE)
                    ins.then_inc(s_P, 1)

                def sums(i):
                    ac.wait_ge(s_AV, i * MP + MP)
                    nc.scalar.copy(avT[:, :, :].rearrange("p q t -> p (q t)"), pav[:, 0:4 * T]).then_inc(s_av, 1)

                def body(i, b):
                    for m in range(MP):
                        exps(i, m)
                        if m == 1 and not (isinstance(i, int) and i == 0):
                            sums(i - 1)
                        for name, n in side.steps(i, m):
                            step(name, n, i + 1 if name[0] == "f" else i - 1, 1 - b)

                ac.wait_ge(s_w, 16 * NW)
                ac.wait_ge(s_z, 1)
                for name, n in side.prologue():
                    step(name, n, 0, 0)
                over_batches(ac, body)
                sums(NB - 1)
                for name, n in side.epilogue():
                    step(name, n, NB - 1, 0)

            @block.gpsimd
            def _(po):
                def stage(i):
                    if not isinstance(i, int) or i:
                        po.wait_ge(s_R, side.read_of(i - 1, "fx"))
                    nc.gpsimd.tensor_copy(xs[:], X[0:T, i, :]).then_inc(s_xs, 1)

                def residual(i):
                    above(po, s_x, i)
                    nc.gpsimd.tensor_tensor(xb[:], X[0:T, i, :], bo[:], ALU.add).then_inc(s_xb, 1)

                po.wait_ge(s_w, 16 * NW)
                stage(0)
                stage(1)
                residual(0)
                stage(2)
                residual(1)
                with po.Fori(2, NB - 1) as i:
                    stage(i + 1)
                    residual(i)
                residual(NB - 1)


def expert_adapter(nc, X, ident, d):
    E, R = 8, 64
    st = Stage(nc, "ea")
    with st:
        sb, ps, sem = st.sb, st.ps, st.sem
        wb, wbT = sb("wb", [P, KD, D]), sb("wbT", [P, KD, D])
        wc, wcT = sb("wc", [P, E, KD, D]), sb("wcT", [P, E, KD, D])
        wd, wu = sb("wd", [P, E, KD, R]), sb("wu", [P, E, D])
        bd, bu, bc = sb("bd", [T, E, R]), sb("bu", [T, E, D]), sb("bc", [T, E, D])
        bb = sb("bb", [T, D])
        sel = sb("sel", [T, NB, NB])
        xsq = sb("xsq", [T, NB, D])
        mu, sg = sb("mu", [E, D]), sb("sg", [E, D])
        tab = sb("tab", [E, 3, D])
        tabT = sb("tabT", [P, 3 * KD, E])
        mom, momT = sb("mom", [NB, 2 * D]), sb("momT", [P, 2 * KD, NB])
        ones = sb("ones", [P, NB])
        nl, top = sb("nl", [NB, E]), sb("top", [NB, E])
        ix, ixr = sb("ix", [NB, E], U32), sb("ixr", [1, NB], U32)
        xs = [sb(f"xs{l}", [T, D]) for l in range(2)]
        xT = [sb(f"xT{l}", [P, KD, T]) for l in range(2)]
        hn = [sb(f"hn{l}", [T, P]) for l in range(2)]
        hT = [sb(f"hT{l}", [P, T]) for l in range(2)]
        an = [sb(f"an{l}", [T, D]) for l in range(2)]
        aT = [sb(f"aT{l}", [P, KD, T]) for l in range(2)]
        xb = [sb(f"xb{l}", [T, D]) for l in range(2)]
        y0 = [sb(f"y0{l}", [T, D]) for l in range(2)]
        y = [sb(f"y{l}", [T, D]) for l in range(2)]
        stats = [sb(f"stats{l}", [T, 6]) for l in range(2)]
        mv = [sb(f"mv{l}", [T, 2]) for l in range(2)]
        rs = [sb(f"rs{l}", [T, 2]) for l in range(2)]
        eps = sb("eps", [T, 1])
        gap = sb("gap", [T, 1])
        pt = [ps(f"pt{l}", [P, 512]) for l in range(2)]
        pm, pl = ps("pm", [P, 512]), ps("pl", [P, 512])

        s_w, s_t, s_tr = sem("weights_loaded"), sem("turn_filled"), sem("turn_read")
        s_sq, s_tab, s_tabT, s_tabTr = sem("squares_ready"), sem("tables_ready"), sem("tablesT_in_psum"), sem("tablesT_read")
        s_m, s_mr, s_mT, s_mTr = sem("moments_in_psum"), sem("moments_read"), sem("momentsT_in_psum"), sem("momentsT_read")
        s_l, s_ix, s_ixr, s_dv = sem("losses_in_psum"), sem("indices_ready"), sem("indices_in_a_row"), sem("setup_chain")
        with nc.Block() as block:
            @block.sync
            def _(sp):
                for dst, src in ((wb[:], rows(d["L0_ffn_base_W"])),
                                 (wc[:], d["L0_ffn_conv_W"].rearrange("e (k p) n -> p e k n", p=P)),
                                 (sel[:], d["c_sel"]), (mu[:], d["L0_ffn_disc_mu"]), (sg[:], d["L0_ffn_disc_sigma"]),
                                 (wd[:], d["L0_ffn_down_W"].rearrange("e (k p) n -> p e k n", p=P)),
                                 (wu[0:R], d["L0_ffn_up_W"].rearrange("e r n -> r e n")),
                                 (bd[:], bcast(d["L0_ffn_down_b"].rearrange("e r -> (e r)"), T)),
                                 (bu[:], bcast(d["L0_ffn_up_b"].rearrange("e r -> (e r)"), T)),
                                 (bc[:], bcast(d["L0_ffn_conv_b"].rearrange("e r -> (e r)"), T)),
                                 (bb[:], bcast(d["L0_ffn_base_b"], T))):
                    v = dst if len(dst.shape) == len(src.shape) else dst.rearrange("p e r -> p (e r)")
                    sp.dma_start(v, src).then_inc(s_w, 16)
                sp.wait_ge(s_w, 16 * 11)
                sp.wait_ge(s_ix, 1)
                with nc.allow_non_contiguous_dma("16 indices to one row"):
                    sp.dma_start(ixr[:], ix[:, 0:1]).then_inc(s_ixr, 16)
                sp.wait_ge(s_ixr, 16)

            @block.tensor
            def _(pe):
                pe.wait_ge(s_w, 16 * 11)
                for part, src in ((0, X), (1, xsq)):
                    if part:
                        pe.wait_ge(s_sq, 1)
                    for b in range(NB):
                        last = nc.tensor.matmul(pm[0:NB, part * D:(part + 1) * D], sel[:, b, :], src[0:T, b, :],
                                                start=b == 0, stop=b == NB - 1)
                last.then_inc(s_m, 1)
                pe.wait_ge(s_tab, 1)
                for j in range(3):
                    for k in range(KD):
                        last = nc.tensor.transpose(pl[:, (j * KD + k) * E:(j * KD + k + 1) * E],
                                                   tab[:, j, k * P:(k + 1) * P], ident[0:E, 0:E])
                last.then_inc(s_tabT, 1)
                pe.wait_ge(s_mr, 1)
                for k in range(2 * KD):
                    last = nc.tensor.transpose(pm[:, k * NB:(k + 1) * NB], mom[:, k * P:(k + 1) * P],
                                               ident[0:NB, 0:NB])
                last.then_inc(s_mT, 1)
                pe.wait_ge(s_mTr, 1)
                pe.wait_ge(s_tabTr, 1)
                n = 0
                for j, lhs in ((0, 1), (1, 0), (2, None)):
                    for k in range(KD):
                        a = ones[:, :] if lhs is None else momT[:, lhs * KD + k, :]
                        last = nc.tensor.matmul(pl[0:NB, 256:256 + E], a, tabT[:, j * KD + k, :],
                                                start=n == 0, stop=n == 3 * KD - 1)
                        n += 1
                last.then_inc(s_l, 1)
                for w in range(E + 1):
                    above(pe, s_tr, w - 1)
                    src = wb if w == E else wc[:, w]
                    for k in range(KD):
                        for o in range(KD):
                            last = nc.tensor.transpose(pt[w % 2][:, k * D + o * P:k * D + (o + 1) * P],
                                                       src[:, o, k * P:(k + 1) * P], ident[:, :])
                    last.then_inc(s_t, 1)

            @block.scalar
            def _(ac):
                for w in range(E + 1):
                    ac.wait_ge(s_t, w + 1)
                    dst = wbT[:, :, :] if w == E else wcT[:, w, :, :]
                    nc.scalar.copy(dst.rearrange("p k n -> p (k n)"), pt[w % 2][:, :]).then_inc(s_tr, 1)
                ac.wait_ge(s_tr, E + 1)

            @block.vector
            def _(dv):
                ch = Chain(dv, s_dv, 0)
                ch.base, ch.n = 0, 0
                nc.vector.tensor_tensor(xsq[:], X[0:T, :, :], X[0:T, :, :], ALU.mult).then_inc(s_sq, 1)
                nc.vector.memset(eps[:], EPS)
                nc.vector.memset(ones[:], 1.0)
                for l in range(2):
                    nc.vector.memset(hn[l][:, R:P], 0.0)
                dv.wait_ge(s_w, 16 * 11)
                ch.after(nc.vector.tensor_tensor(sg[:], sg[:], sg[:], ALU.mult))
                ch.after(nc.vector.reciprocal(tab[:, 0, :], sg[:]))
                ch.after(nc.vector.tensor_tensor(sg[:], mu[:], tab[:, 0, :], ALU.mult))
                ch.after(nc.vector.tensor_scalar(tab[:, 1, :], sg[:], -2.0, None, ALU.mult))
                nc.vector.tensor_tensor(tab[:, 2, :], mu[:], sg[:], ALU.mult).then_inc(s_tab, 1)
                dv.wait_ge(s_m, 1)
                nc.vector.tensor_scalar(mom[:], pm[0:NB, :], 1.0 / T, None, ALU.mult).then_inc(s_mr, 1)
                dv.wait_ge(s_tabT, 1)
                nc.vector.tensor_copy(tabT[:, :, :].rearrange("p j e -> p (j e)"), pl[:, 0:3 * KD * E])\
                    .then_inc(s_tabTr, 1)
                dv.wait_ge(s_mT, 1)
                nc.vector.tensor_copy(momT[:, :, :].rearrange("p j e -> p (j e)"), pm[:, 0:2 * KD * NB])\
                    .then_inc(s_mTr, 1)
                dv.wait_ge(s_l, 1)
                ch.after(nc.vector.tensor_scalar(nl[:], pl[0:NB, 256:256 + E], -1.0, None, ALU.mult))
                ch.after(nc.vector.max(top[:], nl[:]))
                nc.vector.max_index(ix[:], top[:], nl[:]).then_inc(s_ix, 1)
                dv.wait_ge(s_ix, 1)

        pc = [ps(f"pc{l}", [P, 512]) for l in range(2)]

        def over_pairs(eng, body):
            body(0)
            with eng.Fori(1, NB // 2) as j:
                body(j)

        s_xs = [sem(f"xs_staged{l}") for l in range(2)]
        s_F = [sem(f"step_filled{l}") for l in range(2)]
        s_R = [sem(f"step_read{l}") for l in range(2)]
        s_xb = [sem(f"x_plus_bias{l}") for l in range(2)]
        s_ch = [sem(f"ln_chain{l}") for l in range(2)]
        s_mv, s_ln, s_rs, s_x = ([sem(f"{n}{l}") for l in range(2)] for n in ("ln_stats", "ln_log", "ln_rstd", "x_done"))
        NS = 6
        with nc.Block() as block:
            @block.gpsimd
            def _(po):
                def body(j):
                    for l in range(2):
                        above(po, s_x[l], j)
                        nc.gpsimd.tensor_copy(xs[l][:], X[0:T, 2 * j + l, :]).then_inc(s_xs[l], 1)
                        nc.gpsimd.tensor_tensor(xb[l][:], X[0:T, 2 * j + l, :], bb[:], ALU.add).then_inc(s_xb[l], 1)
                over_pairs(po, body)

            @block.tensor
            def _(pe):
                def body(j):
                    e = [pe.value_load(ixr[0:1, bass.ds(2 * j + l, 1)], min_val=0, max_val=E - 1) for l in range(2)]
                    for s in range(NS):
                        for l in range(2):
                            if s == 0:
                                pe.wait_ge(s_xs[l], j + 1)
                            above(pe, s_R[l], NS * j + s)
                            if s == 0:
                                for k in range(KD):
                                    last = nc.tensor.transpose(pt[l][:, k * T:(k + 1) * T], xs[l][:, k * P:(k + 1) * P],
                                                               ident[0:T, 0:T])
                            elif s == 1:
                                for k in range(KD):
                                    last = nc.tensor.matmul(pt[l][0:T, 256:256 + R], xT[l][:, k, :], wd[:, e[l], k, :],
                                                            start=k == 0, stop=k == KD - 1)
                            elif s == 2:
                                last = nc.tensor.transpose(pt[l][:, 384:384 + T], hn[l][:, :], ident[0:T, 0:T])
                            elif s == 3:
                                last = nc.tensor.matmul(pt[l][0:T, 0:D], hT[l][0:R, :], wu[0:R, e[l], :],
                                                        start=True, stop=True)
                            elif s == 4:
                                for k in range(KD):
                                    last = nc.tensor.transpose(pt[l][:, 256 + k * T:256 + (k + 1) * T],
                                                               an[l][:, k * P:(k + 1) * P], ident[0:T, 0:T])
                            else:
                                for k in range(KD):
                                    nc.tensor.matmul(pc[l][0:T, 0:D], xT[l][:, k, :], wbT[:, k, :],
                                                     start=k == 0, stop=False)
                                for k in range(KD):
                                    last = nc.tensor.matmul(pc[l][0:T, 0:D], aT[l][:, k, :], wcT[:, e[l], k, :],
                                                            start=False, stop=k == KD - 1)
                            last.then_inc(s_F[l], 1)
                over_pairs(pe, body)

            @block.scalar
            def _(ac):
                with ac.Fori(0, NB // 2) as j:
                    for s in (0, 2, 4):
                        for l in range(2):
                            ac.wait_ge(s_F[l], NS * j + (s + 1))
                            if s == 2:
                                nc.scalar.activation(hT[l][0:R, :], pt[l][0:R, 384:384 + T], ACT.Relu)\
                                    .then_inc(s_R[l], 1)
                            else:
                                o, dst = (0, xT[l]) if s == 0 else (256, aT[l])
                                nc.scalar.copy(dst[:, :, :].rearrange("p k t -> p (k t)"),
                                               pt[l][:, o:o + KD * T]).then_inc(s_R[l], 1)
                    for l in range(2):
                        ac.wait_ge(s_mv[l], j + 1)
                        nc.scalar.activation(rs[l][:, 0:1], mv[l][:, 1:2], ACT.Ln, bias=eps[:, 0:1]).then_inc(s_ln[l], 1)
                        ac.wait_ge(s_ln[l], j + 1)
                        nc.scalar.activation(rs[l][:, 1:2], rs[l][:, 0:1], ACT.Exp, scale=-0.5).then_inc(s_rs[l], 1)

            @block.vector
            def _(dv):
                with dv.Fori(0, NB // 2) as j:
                    e = [dv.value_load(ixr[0:1, bass.ds(2 * j + l, 1)], min_val=0, max_val=E - 1) for l in range(2)]
                    for l in range(2):
                        dv.wait_ge(s_F[l], NS * j + 2)
                        nc.vector.tensor_tensor(hn[l][:, 0:R], pt[l][0:T, 256:256 + R], bd[:, e[l], :], ALU.add)\
                            .then_inc(s_R[l], 1)
                    for l in range(2):
                        dv.wait_ge(s_F[l], NS * j + 4)
                        nc.vector.tensor_tensor(an[l][:], pt[l][0:T, 0:D], bu[:, e[l], :], ALU.add).then_inc(s_R[l], 1)
                    for l in range(2):
                        dv.wait_ge(s_F[l], NS * j + 6)
                        nc.vector.tensor_tensor(y0[l][:], pc[l][0:T, 0:D], bc[:, e[l], :], ALU.add).then_inc(s_R[l], 1)
                        dv.wait_ge(s_R[l], NS * j + 6)
                        dv.wait_ge(s_xb[l], j + 1)
                        nc.vector.tensor_tensor(y[l][:], y0[l][:], xb[l][:], ALU.add).then_inc(s_ch[l], 1)
                        dv.wait_ge(s_ch[l], 2 * j + 1)
                        nc.vector.bn_stats(stats[l][:], y[l][:]).then_inc(s_ch[l], 1)
                        dv.wait_ge(s_ch[l], 2 * j + 2)
                        nc.vector.memset(gap[:], 0.0)
                        nc.vector.bn_aggr(mv[l][:], stats[l][:]).then_inc(s_mv[l], 1)
                    for l in range(2):
                        dv.wait_ge(s_rs[l], j + 1)
                        nc.vector.tensor_scalar(X[0:T, 2 * j + l, :], y[l][:], mv[l][:, 0:1], rs[l][:, 1:2],
                                                ALU.subtract, ALU.mult).then_inc(s_x[l], 1)


def bucket_attention(nc, X, ident, d):
    NQ, HQ, NHP = 4, 4, 6
    NBK = 2 ** NHP
    SCALE = D ** -0.5
    SLOTS = [["fx"], ["fq"], ["bo", "fh"], ["fv"]]
    st = Stage(nc, "ba")
    with st:
        sb, ps, sem = st.sb, st.ps, st.sem
        wqT, wvT = turned(nc, st, ["L1_attn_Wq", "L1_attn_Wv"], d, ident)
        bq, bv = sb("bq", [P, KD]), sb("bv", [T, D])
        hmask = sb("hmask", [P, HG])
        hyp, hb = sb("hyp", [P, HG * NHP]), sb("hb", [T, NHP])
        pw = sb("pw", [T, NH * NHP])
        xs, xT = sb("xs", [T, D]), sb("xT", [P, KD, T])
        qT = [sb(f"qT{b}", [P, KD, T]) for b in range(2)]
        qTm = [sb(f"qTm{b}", [P, KD, HG, T]) for b in range(2)]
        va = [sb(f"va{b}", [T, NH, 32]) for b in range(2)]
        pj, bk = sb("pj", [T, NH * NHP]), [sb(f"bk{b}", [T, NH]) for b in range(2)]
        dg = [sb(f"dg{b}", [T, NH, T], BF16) for b in range(2)]
        ones = sb("ones", [T, P], BF16)
        same = sb("same", [T, HQ, T])
        A = [sb(f"A{b}", [T, HQ, T]) for b in range(2)]
        mx = [sb(f"mx{b}", [T, HQ]) for b in range(2)]
        pr = [sb(f"pr{b}", [T, HQ, T]) for b in range(2)]
        pT = [sb(f"pT{b}", [T, HQ * T]) for b in range(2)]
        avT = sb("avT", [P, NQ, T])
        rc, o, y = sb("rc", [T, NH]), sb("o", [T, D]), sb("y", [T, D])
        stats, mv, rs, eps = sb("stats", [T, 6]), sb("mv", [T, 2]), sb("rs", [T, 2]), sb("eps", [T, 1])
        gap = sb("gap", [T, 1])
        pS = [ps(f"pS{b}", [P, 512]) for b in range(2)]
        pB = [ps(f"pB{b}", [P, 512]) for b in range(2)]
        pPT = [ps(f"pPT{b}", [P, 512]) for b in range(2)]
        pav, pf = ps("pav", [P, 512]), ps("side", [P, 512])

        s_w, s_z, s_z1 = sem("weights_loaded"), sem("padding_zeroed"), sem("hyperplanes_zeroed")
        s_xs, s_F, s_R = sem("xs_staged"), sem("side_filled"), sem("side_read")
        s_qm, s_dg = sem("masked_q_ready"), sem("diagonals_ready")
        s_S, s_mx, s_A, s_P = sem("scores_in_psum"), sem("max_ready"), sem("scores_shifted"), sem("exp_ready")
        s_PTp, s_PT, s_AV, s_av = (sem(n) for n in ("probsT_in_psum", "probsT_ready", "values_summed", "sums_read"))
        s_mv, s_ln, s_rs, s_x = (sem(n) for n in ("ln_stats", "ln_log", "ln_rstd", "x_done"))
        s_dv, s_dq, s_df, s_pl = sem("setup_chain"), sem("quad_chain"), sem("step_chain"), sem("pool_chain")
        side = Side(SLOTS, s_F, s_R)
        NW = 5 + HG

        with nc.Block() as block:
            @block.sync
            def _(sp):
                with nc.allow_non_contiguous_dma("small constants"):
                    for dst, src in ((bq[:], d["L1_attn_bq"].rearrange("(k p) -> p k", p=P)),
                                     (bv[:], bcast(d["L1_attn_bv"], T)), (hmask[:], d["c_hmask"]),
                                     (pw[:], d["c_pow2"]),
                                     (hb[:], d["L1_attn_hyperplanes"][DH:DH + 1, :].broadcast_to([T, NHP]))):
                        sp.dma_start(dst, src).then_inc(s_w, 16)
                    sp.wait_ge(s_z1, 1)
                    for h in range(HG):
                        sp.dma_start(hyp[h * DH:(h + 1) * DH, h * NHP:(h + 1) * NHP],
                                     d["L1_attn_hyperplanes"][0:DH, :]).then_inc(s_w, 16)

            @block.tensor
            def _(pe):
                def step(name, n, i, b):
                    if name == "fx":
                        pe.wait_ge(s_xs, i + 1)
                    if name == "bo":
                        pe.wait_ge(s_av, i + 1)
                    above(pe, s_R, n)
                    if name == "fx":
                        for k in range(KD):
                            last = nc.tensor.transpose(pf[:, k * T:(k + 1) * T], xs[:, k * P:(k + 1) * P],
                                                       ident[0:T, 0:T])
                    elif name == "fq":
                        for e in range(KD):
                            for k in range(KD):
                                last = nc.tensor.matmul(pf[:, e * T:(e + 1) * T], wqT[:, k, e * P:(e + 1) * P],
                                                        xT[:, k, :], start=k == 0, stop=k == KD - 1)
                    elif name == "fh":
                        W = HG * NHP
                        for e in range(KD):
                            last = nc.tensor.matmul(pf[0:T, e * W:(e + 1) * W], qT[b][:, e, :], hyp[:, :],
                                                    start=True, stop=True)
                    elif name == "fv":
                        for k in range(KD):
                            last = nc.tensor.matmul(pf[0:T, 0:D], xT[:, k, :], wvT[:, k, :],
                                                    start=k == 0, stop=k == KD - 1)
                    else:
                        for q in range(NQ):
                            last = nc.tensor.transpose(pf[0:T, q * P:(q + 1) * P], avT[:, q, :], ident[:, :])
                    last.then_inc(s_F, 1)

                def scores(i, b, m):
                    n = i * NQ + m
                    if m == 0:
                        pe.wait_ge(s_R, side.front_done(i))
                        pe.wait_ge(s_qm, i + 1)
                        pe.wait_ge(s_dg, i + 1)
                    above(pe, s_mx, 2 * (n - 1))
                    h = HQ * m
                    nc.tensor.matmul(pB[m % 2][:, 0:HQ * T], ones[:, :], dg[b][:, h:h + HQ, :], start=True, stop=True)
                    nc.tensor.matmul(pS[m % 2][0:T, 0:HQ * T], qT[b][:, h // HG, :],
                                     qTm[b][:, h // HG, h % HG:h % HG + HQ, :], start=True, stop=True)\
                        .then_inc(s_S, 1)

                def turn(n, m):
                    pe.wait_ge(s_P, n + 1)
                    above(pe, s_PT, n - 1)
                    for e in range(HQ):
                        last = nc.tensor.transpose(pPT[m % 2][0:T, e * T:(e + 1) * T], pr[m % 2][:, e, :],
                                                   ident[0:T, 0:T])
                    last.then_inc(s_PTp, 1)

                def values(n, i, b, m):
                    pe.wait_ge(s_PT, n + 1)
                    if m == 0:
                        above(pe, s_av, i)
                    for j in range(HQ):
                        last = nc.tensor.matmul(pav[32 * j:32 * j + 32, m * T:(m + 1) * T], va[b][:, HQ * m + j, :],
                                                pT[m % 2][:, j * T:(j + 1) * T], start=True, stop=True)
                    last.then_inc(s_AV, 1)

                def body(i, b):
                    first = isinstance(i, int) and i == 0
                    for m in range(NQ):
                        n = i * NQ + m
                        scores(i, b, m)
                        if m >= 1 or not first:
                            turn(n - 1, (m - 1) % NQ)
                        if m >= 2:
                            values(n - 2, i, b, m - 2)
                        elif not first:
                            values(n - 2, i - 1, 1 - b, NQ - 2 + m)
                        for name, k in side.steps(i, m):
                            step(name, k, i + 1 if name[0] == "f" else i - 1, 1 - b)

                pe.wait_ge(s_w, 16 * NW)
                pe.wait_ge(s_z, 1)
                for name, n in side.prologue():
                    step(name, n, 0, 0)
                over_batches(pe, body)
                n = NB * NQ
                turn(n - 1, NQ - 1)
                values(n - 2, NB - 1, 1, NQ - 2)
                values(n - 1, NB - 1, 1, NQ - 1)
                for name, k in side.epilogue():
                    step(name, k, NB - 1, 0)

            @block.vector
            def _(dv):
                SET = 6

                def step(name, n, i, b):
                    if name == "fq":
                        dv.wait_ge(s_F, n + 1)
                        for e in range(KD):
                            ins = nc.vector.tensor_scalar(qT[b][:, e, :], pf[:, e * T:(e + 1) * T], bq[:, e:e + 1],
                                                          None, ALU.add)
                        ins.then_inc(s_R, 1)
                    elif name == "fh":
                        dv.wait_ge(s_F, n + 1)
                        p3 = pj[:, :].rearrange("p (h n) -> p h n", n=NHP)
                        nc.vector.tensor_tensor(p3, pf[0:T, 0:NH * NHP].rearrange("p (h n) -> p h n", n=NHP),
                                                hb[:, :].unsqueeze(1).broadcast_to([T, NH, NHP]), ALU.add)\
                            .then_inc(s_df, 1)
                        dv.wait_ge(s_df, 2 * i + 1)
                        nc.vector.scalar_tensor_tensor(out=pj[:], in0=pj[:], scalar=0.0, in1=pw[:], op0=ALU.is_ge,
                                                       op1=ALU.mult).then_inc(s_df, 1)
                        dv.wait_ge(s_df, 2 * i + 2)
                        nc.vector.reduce_sum(bk[b][:], p3, AX).then_inc(s_R, 1)
                    elif name == "fv":
                        dv.wait_ge(s_F, n + 1)
                        nc.vector.tensor_tensor(va[b][:, :, 0:DH], pf[0:T, 0:D].rearrange("p (h c) -> p h c", c=DH),
                                                bv[:, :].rearrange("p (h c) -> p h c", c=DH), ALU.add).then_inc(s_R, 1)
                    elif name == "bo":
                        dv.wait_ge(s_F, n + 1)
                        o4 = pf[0:T, :].rearrange("p (h c) -> p h c", c=32)
                        nc.vector.reciprocal(rc[:], o4[:, :, DH]).then_inc(s_dv, 1)
                        dv.wait_ge(s_dv, SET + 3 * i + 1)
                        nc.vector.tensor_tensor(o[:, :].rearrange("p (h c) -> p h c", c=DH), o4[:, :, 0:DH],
                                                rc[:, :].unsqueeze(2).broadcast_to([T, NH, DH]), ALU.mult)\
                            .then_inc(s_R, 1)
                        dv.wait_ge(s_R, n + 1)
                        nc.vector.tensor_tensor(y[:], o[:], X[0:T, i, :], ALU.add).then_inc(s_dv, 1)
                        dv.wait_ge(s_dv, SET + 3 * i + 2)
                        nc.vector.bn_stats(stats[:], y[:]).then_inc(s_dv, 1)
                        dv.wait_ge(s_dv, SET + 3 * i + 3)
                        nc.vector.memset(gap[:], 0.0)
                        nc.vector.bn_aggr(mv[:], stats[:]).then_inc(s_mv, 1)
                        dv.wait_ge(s_rs, i + 1)
                        nc.vector.tensor_scalar(X[0:T, i, :], y[:], mv[:, 0:1], rs[:, 1:2], ALU.subtract, ALU.mult)\
                            .then_inc(s_x, 1)

                def weigh(i, b, m):
                    n = i * NQ + m
                    h = HQ * m
                    dv.wait_ge(s_S, n + 1)
                    above(dv, s_P, n - 1)
                    nc.vector.tensor_tensor(same[:], pB[m % 2][0:T, 0:HQ * T].rearrange("p (h t) -> p h t", h=HQ),
                                            bk[b][:, h:h + HQ].unsqueeze(2).broadcast_to([T, HQ, T]), ALU.is_equal)\
                        .then_inc(s_dq, 1)
                    dv.wait_ge(s_dq, n + 1)
                    nc.vector.scalar_tensor_tensor(
                        out=A[m % 2][:, :, :].rearrange("p h t -> p (h t)"),
                        in0=same[:, :, :].rearrange("p h t -> p (h t)"), scalar=float(NBK - 2),
                        in1=pS[m % 2][0:T, 0:HQ * T], op0=ALU.add, op1=ALU.mult).then_inc(s_mx, 1)
                    dv.wait_ge(s_mx, 2 * n + 1)
                    nc.vector.reduce_max(mx[m % 2][:], A[m % 2][:], AX).then_inc(s_mx, 1)

                def body(i, b):
                    for m in range(NQ):
                        weigh(i, b, m)
                        for name, n in side.steps(i, m):
                            step(name, n, i + 1 if name[0] == "f" else i - 1, 1 - b)

                ch = Chain(dv, s_dv, 0)
                ch.base, ch.n = 0, 0
                ch.after(nc.vector.memset(hyp[:], 0.0))
                nc.vector.memset(rc[:], 0.0).then_inc(s_z1, 1)
                for b in range(2):
                    ch.after(nc.vector.memset(va[b][:], 0.0))
                    ch.after(nc.vector.memset(va[b][:, :, DH:DH + 1], 1.0))
                ch.after(nc.vector.memset(eps[:], EPS))
                assert ch.n == SET
                nc.vector.memset(ones[:], 1.0).then_inc(s_z, 1)
                dv.wait_ge(s_z, 1)
                dv.wait_ge(s_w, 16 * NW)
                for name, n in side.prologue():
                    step(name, n, 0, 0)
                over_batches(dv, body)
                for name, n in side.epilogue():
                    step(name, n, NB - 1, 0)

            @block.scalar
            def _(ac):
                def step(name, n, i, b):
                    if name == "fx":
                        ac.wait_ge(s_F, n + 1)
                        nc.scalar.copy(xT[:, :, :].rearrange("p k t -> p (k t)"), pf[:, 0:KD * T]).then_inc(s_R, 1)
                    elif name == "bo":
                        ac.wait_ge(s_mv, i + 1)
                        nc.scalar.activation(rs[:, 0:1], mv[:, 1:2], ACT.Ln, bias=eps[:, 0:1]).then_inc(s_ln, 1)
                        ac.wait_ge(s_ln, i + 1)
                        nc.scalar.activation(rs[:, 1:2], rs[:, 0:1], ACT.Exp, scale=-0.5).then_inc(s_rs, 1)

                def exps(i, m):
                    n = i * NQ + m
                    ac.wait_ge(s_A, n + 1)
                    above(ac, s_PTp, n - 1)
                    nc.scalar.activation(pr[m % 2][:, :, :].rearrange("p h t -> p (h t)"),
                                         A[m % 2][:, :, :].rearrange("p h t -> p (h t)"), ACT.Exp, scale=SCALE)\
                        .then_inc(s_P, 1)

                def evac(n, m):
                    ac.wait_ge(s_PTp, n + 1)
                    above(ac, s_AV, n - 1)
                    nc.scalar.copy(pT[m % 2][:], pPT[m % 2][0:T, 0:HQ * T]).then_inc(s_PT, 1)

                def sums(i):
                    ac.wait_ge(s_AV, i * NQ + NQ)
                    nc.scalar.copy(avT[:, :, :].rearrange("p q t -> p (q t)"), pav[:, 0:NQ * T]).then_inc(s_av, 1)

                def body(i, b):
                    first = isinstance(i, int) and i == 0
                    for m in range(NQ):
                        if m or not first:
                            evac(i * NQ + m - 1, (m - 1) % NQ)
                        if m == 1 and not first:
                            sums(i - 1)
                        exps(i, m)
                        for name, n in side.steps(i, m):
                            step(name, n, i + 1 if name[0] == "f" else i - 1, 1 - b)

                ac.wait_ge(s_z, 1)
                for name, n in side.prologue():
                    step(name, n, 0, 0)
                over_batches(ac, body)
                evac(NB * NQ - 1, NQ - 1)
                sums(NB - 1)
                for name, n in side.epilogue():
                    step(name, n, NB - 1, 0)

            @block.gpsimd
            def _(po):
                def stage(i):
                    if not isinstance(i, int) or i:
                        po.wait_ge(s_R, side.read_of(i - 1, "fx"))
                    nc.gpsimd.tensor_copy(xs[:], X[0:T, i, :]).then_inc(s_xs, 1)

                def masks(i, b):
                    po.wait_ge(s_R, side.read_of(i, "fq"))
                    for e in range(KD):
                        ins = nc.gpsimd.tensor_tensor(qTm[b][:, e, :, :],
                                                      qT[b][:, e, :].unsqueeze(1).broadcast_to([P, HG, T]),
                                                      hmask[:, :].unsqueeze(2).broadcast_to([P, HG, T]), ALU.mult)
                    ins.then_inc(s_qm, 1)

                def diagonals(i, b):
                    po.wait_ge(s_R, side.read_of(i, "fh"))
                    nc.gpsimd.tensor_tensor(dg[b][:], ident[0:T, 0:T].unsqueeze(1).broadcast_to([T, NH, T]),
                                            bk[b][:, :].unsqueeze(2).broadcast_to([T, NH, T]), ALU.mult)\
                        .then_inc(s_dg, 1)

                def shift(i, m):
                    n = i * NQ + m
                    po.wait_ge(s_mx, 2 * n + 2)
                    nc.gpsimd.tensor_tensor(A[m % 2][:], A[m % 2][:],
                                            mx[m % 2][:, :].unsqueeze(2).broadcast_to([T, HQ, T]), ALU.subtract)\
                        .then_inc(s_A, 1)

                def body(i, b):
                    last = isinstance(i, int) and i == NB - 1
                    for m in range(NQ):
                        if m == 0 and not last:
                            stage(i + 1)
                        shift(i, m)
                        if m == 2 and not last:
                            masks(i + 1, 1 - b)
                        if m == 3 and not last:
                            diagonals(i + 1, 1 - b)

                po.wait_ge(s_w, 16 * NW)
                stage(0)
                masks(0, 0)
                diagonals(0, 0)
                over_batches(po, body)


def latent_attention(nc, X, ident, d):
    DX = 64
    NE = NH * DX // P
    NC, SK = 4, SC + T
    KP_ = NC * P
    MP = NH // 2
    SCALE = DX ** -0.5
    ckeys = [P, P, SC - 2 * P]
    keys = [min(P, SK - c * P) for c in range(NC)]
    SLOTS = [["fl", "fc0", "fc1"], ["fk0", "fk1", "fk2"], ["by", "fk3", "fk4"], ["fk5", "fk6", "fk7"],
             ["fq0", "fq1", "fv00"], ["fv01", "fv10", "fv11"], ["fv20", "fv21", "fv30"], ["fv31"]]
    st = Stage(nc, "la")
    with st:
        sb, ps, sem = st.sb, st.ps, st.sem
        wq, wkv = sb("wq", [P, KD, NH * DX]), sb("wkv", [P, KD, 2 * NH * DX])
        wo = sb("wo", [P, NE, D])
        gx, bx, gl, bl = (sb(n, [P, KD]) for n in ("gx", "bx", "gl", "bl"))
        go, bo = sb("go", [T, D]), sb("bo", [T, D])
        half = sb("half", [P, 2])
        mk = sb("mk", [1, NB * SC], U8)
        mb = [sb(f"mb{b}", [P, SC + T + 1], BF16) for b in range(2)]
        row0 = sb("row0", [P, P], BF16)
        xs, cn = sb("xs", [T, D]), sb("cn", [P, 3, D])
        inT = sb("inT", [P, KD, SK])
        kT = [sb(f"kT{b}", [P, NE, SK]) for b in range(2)]
        v = [sb(f"v{b}", [P, NC, NH * DX]) for b in range(2)]
        qTm = [sb(f"qTm{b}", [P, NE, 2, T]) for b in range(2)]
        nm = [sb(f"nm{b}", [T, 2]) for b in range(2)]
        zs = [sb(f"zs{b}", [T, 4]) for b in range(2)]
        pr = [sb(f"pr{b}", [T, 2, KP_]) for b in range(2)]
        pT = [sb(f"pT{b}", [P, 2, NC * T]) for b in range(2)]
        oT = [sb(f"oT{b}", [P, NE, T]) for b in range(2)]
        xb, y0, y1, y2, y3 = (sb(n, [T, D]) for n in ("xb", "y0", "y1", "y2", "y3"))
        cst, cmv, crs = sb("cst", [P, 4, 6]), sb("cmv", [P, 4, 2]), sb("crs", [P, 2, 4])
        stats, mv, rs, eps = sb("stats", [T, 6]), sb("mv", [T, 2]), sb("rs", [T, 2]), sb("eps", [P, 1])
        gap = sb("gap", [T, 1])
        pS = ps("pS", [P, 4, 512])
        pPT = ps("pPT", [P, 2, 512])
        pav, pf = ps("pav", [P, 4, T]), ps("side", [P, 512])

        s_w, s_z = sem("weights_loaded"), sem("padding_zeroed")
        s_cn = sem("context_loaded")
        s_xs, s_F, s_R = sem("xs_staged"), sem("side_filled"), sem("side_read")
        s_cmv, s_cln, s_crs, s_n = (sem(n) for n in ("input_stats", "input_log", "input_rstd", "inputs_normed"))
        s_mb = sem("mask_ready")
        s_S, s_mx, s_P, s_Z = sem("scores_in_psum"), sem("max_ready"), sem("exp_ready"), sem("probs_ready")
        s_PTp, s_PT, s_AV, s_av = (sem(n) for n in ("probsT_in_psum", "probsT_ready", "values_summed", "sums_read"))
        s_xb, s_mv, s_ln, s_rs, s_x = (sem(n) for n in ("x_plus_bias", "ln_stats", "ln_log", "ln_rstd", "x_done"))
        s_nn = sem("input_applied")
        s_dv, s_dn, s_dy, s_dz = sem("setup_chain"), sem("input_chain"), sem("out_chain"), sem("norm_chain")
        side = Side(SLOTS, s_F, s_R)
        NW = 11

        with nc.Block() as block:
            @block.sync
            def _(sp):
                col = lambda n: d[n].rearrange("(k p) -> p k", p=P)
                with nc.allow_non_contiguous_dma("small constants"):
                    for dst, src in ((wq[:], rows(d["L1_xattn_Wq"])), (wkv[:], rows(d["L1_xattn_Wkv"])),
                                     (wo[:], rows(d["L1_xattn_Wout"])), (gx[:], col("L1_xattn_g_x")),
                                     (bx[:], col("L1_xattn_b_x")), (gl[:], col("L1_xattn_g_l")),
                                     (bl[:], col("L1_xattn_b_l")), (go[:], bcast(d["L1_xattn_g_o"], T)),
                                     (bo[:], bcast(d["L1_xattn_b_o"], T)), (half[:], d["c_half"]),
                                     (mk[:], d["mask_BxS2_bf1"].rearrange("(a b) s -> a (b s)", a=1))):
                        sp.dma_start(dst, src).then_inc(s_w, 16)

                def load(i):
                    if not isinstance(i, int) or i:
                        sp.wait_ge(s_R, side.read_of(i - 1, "fc1"))
                    sp.dma_start(cn[:, 0:2, :], d["ctx_1024"][i, 0:2 * P, :].rearrange("(c p) n -> p c n", p=P))\
                        .then_inc(s_cn, 16)
                    sp.dma_start(cn[0:ckeys[2], 2, :], d["ctx_1024"][i, 2 * P:SC, :]).then_inc(s_cn, 16)
                for i in range(3):
                    load(i)
                with sp.Fori(3, NB) as i:
                    load(i)

            @block.tensor
            def _(pe):
                def step(name, n, i, b):
                    if name == "fl":
                        pe.wait_ge(s_n, i + 1)
                    above(pe, s_R, n)
                    if name == "fl":
                        for k in range(KD):
                            last = nc.tensor.transpose(pf[:, k * T:(k + 1) * T], xs[:, k * P:(k + 1) * P],
                                                       ident[0:T, 0:T])
                    elif name in ("fc0", "fc1"):
                        k = int(name[-1])
                        for c in range(3):
                            last = nc.tensor.transpose(pf[:, c * P:c * P + ckeys[c]],
                                                       cn[0:ckeys[c], c, k * P:(k + 1) * P],
                                                       ident[0:ckeys[c], 0:ckeys[c]])
                    elif name[:2] == "fk":
                        e = int(name[2])
                        for k in range(KD):
                            last = nc.tensor.matmul(pf[:, 0:SK], wkv[:, k, e * P:(e + 1) * P], inT[:, k, :],
                                                    start=k == 0, stop=k == KD - 1)
                    elif name[:2] == "fq":
                        for q in range(4):
                            e = 4 * int(name[2]) + q
                            for k in range(KD):
                                last = nc.tensor.matmul(pf[:, q * T:(q + 1) * T], wq[:, k, e * P:(e + 1) * P],
                                                        inT[:, k, SC:SK], start=k == 0, stop=k == KD - 1)
                    elif name[:2] == "fv":
                        c, h = int(name[2]), int(name[3])
                        for k in range(KD):
                            o = NH * DX + h * 512
                            last = nc.tensor.matmul(pf[0:keys[c], :], inT[:, k, c * P:c * P + keys[c]],
                                                    wkv[:, k, o:o + 512], start=k == 0, stop=k == KD - 1)
                    else:
                        for e in range(NE):
                            last = nc.tensor.matmul(pf[0:T, 0:D], oT[1 - b][:, e, :], wo[:, e, :],
                                                    start=e == 0, stop=e == NE - 1)
                    last.then_inc(s_F, 1)

                def scores(i, b, m):
                    n = i * MP + m
                    if m == 0:
                        pe.wait_ge(s_R, side.front_done(i))
                        pe.wait_ge(s_mb, i + 1)
                    above(pe, s_P, n - 1)
                    for e in range(2):
                        o = pS[0:T, 2 * (m % 2) + e, 0:SK]
                        nc.tensor.matmul(o, row0[:, 0:T], mb[b][:, 0:SK], start=True, stop=False)
                        last = nc.tensor.matmul(o, qTm[b][:, m, e, :], kT[b][:, m, :], start=False, stop=True)
                    last.then_inc(s_S, 1)

                def turn(n, m):
                    pe.wait_ge(s_Z, n + 1)
                    above(pe, s_PT, n)
                    for e in range(2):
                        for c in range(NC):
                            last = nc.tensor.transpose(pPT[:, e, c * T:(c + 1) * T],
                                                       pr[m % 2][:, e, c * P:(c + 1) * P], ident[0:T, 0:T])
                    last.then_inc(s_PTp, 1)

                def values(n, b, m):
                    pe.wait_ge(s_PT, n + 1)
                    above(pe, s_av, n)
                    for e in range(2):
                        for c in range(NC):
                            last = nc.tensor.matmul(pav[DX * e:DX * (e + 1), m % 4, :],
                                                    v[b][:, c, (2 * m + e) * DX:(2 * m + e + 1) * DX],
                                                    pT[m % 2][:, e, c * T:(c + 1) * T], start=c == 0, stop=c == NC - 1)
                    last.then_inc(s_AV, 1)

                def body(i, b):
                    first = isinstance(i, int) and i == 0
                    for m in range(MP):
                        n = i * MP + m
                        small = side.steps(i, m) + [None] * 3

                        def between(s):
                            if s and s[0] == "by":
                                pe.wait_ge(s_av, i * MP)
                                step(*s, i - 1, b)
                            elif s:
                                step(*s, i + 1, 1 - b)
                        scores(i, b, m)
                        between(small[0])
                        if m >= 1 or not first:
                            turn(n - 1, (m - 1) % MP)
                        between(small[1])
                        if m >= 2:
                            values(n - 2, b, m - 2)
                        elif not first:
                            values(n - 2, 1 - b, MP - 2 + m)
                        between(small[2])

                pe.wait_ge(s_w, 16 * NW)
                pe.wait_ge(s_z, 1)
                for name, n in side.prologue():
                    step(name, n, 0, 0)
                over_batches(pe, body)
                n = NB * MP
                turn(n - 1, MP - 1)
                values(n - 2, 1, MP - 2)
                values(n - 1, 1, MP - 1)
                pe.wait_ge(s_av, n)
                for name, k in side.epilogue():
                    step(name, k, NB - 1, 0)

            @block.vector
            def _(dv):
                SET = 6
                NLN = 8

                def inputs(i):
                    dv.wait_ge(s_cn, 32 * i + 32)
                    dv.wait_ge(s_xs, i + 1)
                    if not isinstance(i, int) or i:
                        dv.wait_ge(s_crs, i)
                    srcs = [cn[:, 0, :], cn[:, 1, :], cn[0:ckeys[2], 2, :], xs[:, :]]
                    for c, src in enumerate(srcs):
                        r = src.shape[0]
                        nc.vector.bn_stats(cst[0:r, c, :], src).then_inc(s_dn, 1)
                    dv.wait_ge(s_dn, i * 4 + 4)
                    nc.vector.memset(gap[:], 0.0)
                    for c, src in enumerate(srcs):
                        r = src.shape[0]
                        nc.vector.bn_aggr(cmv[0:r, c, :], cst[0:r, c, :]).then_inc(s_cmv, 1)

                def apply_inputs(i):
                    dv.wait_ge(s_crs, i + 1)
                    srcs = [cn[:, 0, :], cn[:, 1, :], cn[0:ckeys[2], 2, :], xs[:, :]]
                    for c, src in enumerate(srcs):
                        r = src.shape[0]
                        nc.vector.tensor_scalar(src, src, cmv[0:r, c, 0:1], crs[0:r, 1, c:c + 1],
                                                ALU.subtract, ALU.mult).then_inc(s_nn, 1)
                    dv.wait_ge(s_nn, i * 4 + 8)
                    nc.vector.memset(gap[:], 0.0).then_inc(s_n, 1)

                def mask(i, b):
                    above(dv, s_S, (i - 1) * MP)
                    nc.vector.tensor_scalar(mb[b][0:1, 0:SC], mk[0:1, bass.ds(i * SC, SC)], -1.0, BIG, ALU.add,
                                            ALU.mult).then_inc(s_mb, 1)

                def step(name, n, i, b):
                    if name[:2] == "fq":
                        dv.wait_ge(s_F, n + 1)
                        for e in range(2):
                            ins = nc.vector.tensor_scalar(qTm[b][:, 4 * int(name[2]):4 * int(name[2]) + 4, e, :],
                                                          pf[:, 0:4 * T].rearrange("p (q t) -> p q t", q=4),
                                                          half[:, e:e + 1], None, ALU.mult)
                        ins.then_inc(s_R, 1)
                    elif name[:2] == "fv":
                        c, h = int(name[2]), int(name[3])
                        dv.wait_ge(s_F, n + 1)
                        nc.vector.tensor_copy(v[b][0:keys[c], c, h * 512:(h + 1) * 512], pf[0:keys[c], :])\
                            .then_inc(s_R, 1)
                    elif name == "by":
                        dv.wait_ge(s_F, n + 1)
                        nc.vector.tensor_copy(y0[:], pf[0:T, 0:D]).then_inc(s_R, 1)
                        dv.wait_ge(s_R, n + 1)
                        link(nc.vector.bn_stats(stats[:], y0[:]), i, 1)
                        nc.vector.memset(gap[:], 0.0)
                        nc.vector.bn_aggr(mv[:], stats[:]).then_inc(s_mv, 1)

                def link(ins, i, k):
                    ins.then_inc(s_dy, 1)
                    dv.wait_ge(s_dy, 5 * i + k)

                def out_norm(i):
                        dv.wait_ge(s_rs, 2 * i + 1)
                        link(nc.vector.tensor_scalar(y1[:], y0[:], mv[:, 0:1], rs[:, 1:2], ALU.subtract, ALU.mult), i, 2)
                        link(nc.vector.tensor_tensor(y2[:], y1[:], go[:], ALU.mult), i, 3)
                        dv.wait_ge(s_xb, i + 1)
                        link(nc.vector.tensor_tensor(y3[:], y2[:], xb[:], ALU.add), i, 4)
                        link(nc.vector.bn_stats(stats[:], y3[:]), i, 5)
                        nc.vector.memset(gap[:], 0.0)
                        nc.vector.bn_aggr(mv[:], stats[:]).then_inc(s_mv, 1)

                def x_norm(i):
                        dv.wait_ge(s_rs, 2 * i + 2)
                        nc.vector.tensor_scalar(X[0:T, i, :], y3[:], mv[:, 0:1], rs[:, 1:2], ALU.subtract, ALU.mult)\
                            .then_inc(s_x, 1)

                def maxima(i, m):
                    n = i * MP + m
                    dv.wait_ge(s_S, n + 1)
                    above(dv, s_P, n - 1)
                    nc.vector.reduce_max(nm[m % 2][:], pS[0:T, 2 * (m % 2):2 * (m % 2) + 2, 0:SK], AX)\
                        .then_inc(s_mx, 1)
                    dv.wait_ge(s_mx, 2 * n + 1)
                    nc.vector.tensor_scalar(nm[m % 2][:], nm[m % 2][:], -SCALE, None, ALU.mult).then_inc(s_mx, 1)

                def norm(n, m):
                    dv.wait_ge(s_P, n + 1)
                    nc.vector.reciprocal(zs[m % 2][:, 2:4], zs[m % 2][:, 0:2]).then_inc(s_dz, 1)
                    dv.wait_ge(s_dz, n + 1)
                    for e in range(2):
                        ins = nc.vector.tensor_scalar(pr[m % 2][:, e, 0:SK], pr[m % 2][:, e, 0:SK],
                                                      zs[m % 2][:, 2 + e:3 + e], None, ALU.mult)
                    ins.then_inc(s_Z, 1)

                def body(i, b):
                    first = isinstance(i, int) and i == 0
                    ahead = not isinstance(i, int) or i + 2 < NB
                    for m in range(MP):
                        if m or not first:
                            norm(i * MP + m - 1, (m - 1) % MP)
                        maxima(i, m)
                        if m == 3 and not first:
                            out_norm(i - 1)
                        if m == 4 and not first:
                            x_norm(i - 1)
                        if m == 5 and ahead:
                            inputs(i + 2)
                        if m == 6 and ahead:
                            apply_inputs(i + 2)
                        if m == 7 and (not isinstance(i, int) or i + 1 < NB):
                            mask(i + 1, 1 - b)
                        for name, n in side.steps(i, m):
                            step(name, n, i + 1 if name[0] == "f" else i - 1, 1 - b)

                ch = Chain(dv, s_dv, 0)
                ch.base, ch.n = 0, 0
                for b in range(2):
                    ch.after(nc.vector.memset(v[b][:, NC - 1, :], 0.0))
                    ch.after(nc.vector.memset(pr[b][:], 0.0))
                    ch.after(nc.vector.memset(mb[b][:], 0.0))
                nc.vector.memset(eps[:], EPS)
                nc.vector.memset(cmv[:], 1.0)
                nc.vector.memset(row0[:], 0.0).then_inc(s_nn, 4)
                dv.wait_ge(s_nn, 4)
                nc.vector.memset(row0[0:1, :], 1.0).then_inc(s_z, 1)
                dv.wait_ge(s_z, 1)
                dv.wait_ge(s_w, 16 * NW)
                inputs(0)
                apply_inputs(0)
                mask(0, 0)
                for name, n in side.prologue():
                    step(name, n, 0, 0)
                    if name == "fc1":
                        inputs(1)
                        apply_inputs(1)
                over_batches(dv, body, 3)
                norm(NB * MP - 1, MP - 1)
                for name, n in side.epilogue():
                    step(name, n, NB - 1, 0)
                out_norm(NB - 1)
                x_norm(NB - 1)

            @block.scalar
            def _(ac):
                def inputs(i):
                    ac.wait_ge(s_cmv, 4 * i + 4)
                    if not isinstance(i, int) or i:
                        ac.wait_ge(s_n, i)
                    nc.scalar.activation(crs[:, 0, :], cmv[:, :, 1], ACT.Ln, bias=eps[:, 0:1]).then_inc(s_cln, 1)
                    ac.wait_ge(s_cln, i + 1)
                    nc.scalar.activation(crs[:, 1, :], crs[:, 0, :], ACT.Exp, scale=-0.5).then_inc(s_crs, 1)

                def step(name, n, i, b):
                    if name == "fl":
                        ac.wait_ge(s_F, n + 1)
                        for k in range(KD):
                            ins = nc.scalar.activation(inT[:, k, SC:SK], pf[:, k * T:(k + 1) * T], ACT.Identity,
                                                       bias=bl[:, k:k + 1], scale=gl[:, k:k + 1])
                        ins.then_inc(s_R, 1)
                    elif name in ("fc0", "fc1"):
                        k = int(name[-1])
                        ac.wait_ge(s_F, n + 1)
                        nc.scalar.activation(inT[:, k, 0:SC], pf[:, 0:SC], ACT.Identity, bias=bx[:, k:k + 1],
                                             scale=gx[:, k:k + 1]).then_inc(s_R, 1)
                    elif name[:2] == "fk":
                        ac.wait_ge(s_F, n + 1)
                        nc.scalar.copy(kT[b][:, int(name[2]), :], pf[:, 0:SK]).then_inc(s_R, 1)

                def rstd(i, r):
                    ac.wait_ge(s_mv, 2 * i + (r + 1))
                    nc.scalar.activation(rs[:, 0:1], mv[:, 1:2], ACT.Ln, bias=eps[0:T, 0:1]).then_inc(s_ln, 1)
                    ac.wait_ge(s_ln, 2 * i + (r + 1))
                    nc.scalar.activation(rs[:, 1:2], rs[:, 0:1], ACT.Exp, scale=-0.5).then_inc(s_rs, 1)

                def exps(i, m):
                    n = i * MP + m
                    ac.wait_ge(s_mx, 2 * n + 2)
                    above(ac, s_PTp, n - 1)
                    for e in range(2):
                        ins = nc.scalar.activation(pr[m % 2][:, e, 0:SK], pS[0:T, 2 * (m % 2) + e, 0:SK], ACT.Exp,
                                                   bias=nm[m % 2][:, e:e + 1], scale=SCALE,
                                                   accum_out=zs[m % 2][:, e:e + 1])
                    ins.then_inc(s_P, 1)

                def evac(n, m):
                    ac.wait_ge(s_PTp, n + 1)
                    above(ac, s_AV, n - 1)
                    nc.scalar.copy(pT[m % 2][:], pPT[:, :, 0:NC * T]).then_inc(s_PT, 1)

                def sums(n, b, m):
                    ac.wait_ge(s_AV, n + 1)
                    nc.scalar.copy(oT[b][:, m, :], pav[:, m % 4, :]).then_inc(s_av, 1)

                def body(i, b):
                    first = isinstance(i, int) and i == 0
                    ahead = not isinstance(i, int) or i + 2 < NB
                    for m in range(MP):
                        n = i * MP + m
                        small = side.steps(i, m) + [None] * 3

                        def between(s):
                            if s:
                                step(*s, i + 1 if s[0][0] == "f" else i - 1, 1 - b)
                        if m == 3 and not first:
                            rstd(i - 1, 0)
                        if m == 4 and not first:
                            rstd(i - 1, 1)
                        if m == 6 and ahead:
                            inputs(i + 2)
                        between(small[0])
                        exps(i, m)
                        between(small[1])
                        if m or not first:
                            evac(n - 1, (m - 1) % MP)
                        if m >= 2:
                            sums(n - 2, b, m - 2)
                        elif not first:
                            sums(n - 2, 1 - b, MP - 2 + m)
                        between(small[2])

                ac.wait_ge(s_w, 16 * NW)
                ac.wait_ge(s_z, 1)
                nc.scalar.preload_act_table_set("natural_log_exp_and_others")
                inputs(0)
                for name, n in side.prologue():
                    step(name, n, 0, 0)
                    if name == "fc1":
                        inputs(1)
                over_batches(ac, body, 3)
                n = NB * MP
                evac(n - 1, MP - 1)
                sums(n - 2, 1, MP - 2)
                sums(n - 1, 1, MP - 1)
                for name, k in side.epilogue():
                    step(name, k, NB - 1, 0)
                rstd(NB - 1, 0)
                rstd(NB - 1, 1)

            @block.gpsimd
            def _(po):
                def stage(i):
                    if not isinstance(i, int) or i:
                        po.wait_ge(s_R, side.read_of(i - 1, "fl"))
                    nc.gpsimd.tensor_copy(xs[:], X[0:T, i, :]).then_inc(s_xs, 1)

                def residual(i):
                    above(po, s_x, i)
                    nc.gpsimd.tensor_tensor(xb[:], X[0:T, i, :], bo[:], ALU.add).then_inc(s_xb, 1)

                po.wait_ge(s_w, 16 * NW)
                stage(0)
                stage(1)
                residual(0)
                stage(2)
                residual(1)
                with po.Fori(2, NB - 1) as i:
                    stage(i + 1)
                    residual(i)
                residual(NB - 1)


NBK = (NB * T + 8 * (P - 1)) // P
NTH = -(-NB * T // P)


def routed_ffn(nc, X, ident, d, out, rows_in, rows_out, s_zero):
    E, F = 8, 1024
    KF = F // P
    st = Stage(nc, "rf")
    with st:
        sb, ps, sem = st.sb, st.ps, st.sem
        w1, w2 = sb("w1", [P, E, KD, F]), sb("w2", [P, E, KF, D])
        gate = sb("gate", [T, NB])
        slot = sb("slot", [T, NB], U32)
        ebu = sb("ebu", [1, NBK], U32)
        s_we = [sem(f"weights_loaded{e}") for e in range(E)]
        s_wr = sem("experts_ready")
        s_sc, s_rt = sem("rows_scattered"), sem("routing_ready")

        rt = Stage(nc, "rr")
        with rt:
            wr, br = rt.sb("wr", [P, KD, E]), rt.sb("br", [T, E])
            tri, ones = rt.sb("tri", [T, T]), rt.sb("ones", [T, T])
            ie = rt.sb("ie", [T, NB, E])
            thr, blk = rt.sb("thr", [T, E, NTH]), rt.sb("blk", [1, NBK, E])
            xs, xT = rt.sb("xs", [T, D]), rt.sb("xT", [P, KD, T])
            lg, ex, route, eq, oh, pos = (rt.sb(n, [T, NB, E]) for n in ("lg", "ex", "route", "eq", "oh", "pos"))
            sc = [rt.sb(f"sc{n}", [T, NB, E]) for n in range(2)]
            tot = rt.sb("tot", [T, NB, E])
            ixe, slf = rt.sb("ixe", [T, NB]), rt.sb("slf", [T, NB])
            gt, nb_ = rt.sb("gt", [T, E, NTH]), rt.sb("nb", [T, E])
            be = [rt.sb(f"be{n}", [T, E]) for n in range(2)]
            ge, eb = rt.sb("ge", [1, NBK, E]), rt.sb("eb", [1, NBK])
            pt = rt.ps("pt", [P, 512])
            pl, pp = rt.ps("pl", [P, 512]), rt.ps("pp", [P, 512])
            s_c, s_xs, s_xTp, s_xT = rt.sem("consts"), rt.sem("xs_staged"), rt.sem("xT_in_psum"), rt.sem("xT_ready")
            s_l, s_lg, s_ex = rt.sem("logits_in_psum"), rt.sem("logits_ready"), rt.sem("exp_ready")
            s_oh, s_pp, s_ch = rt.sem("onehot_ready"), rt.sem("prefixes_in_psum"), rt.sem("dve_chain")
            NC_ = 6
            with nc.Block() as block:
                @block.sync
                def _(sp):
                    with nc.allow_non_contiguous_dma("small constants"):
                        for dst, src in ((wr[:], rows(d["L1_ffn_Wr"])), (br[:], bcast(d["L1_ffn_br"], T)),
                                         (tri[:], d["c_tri"]), (ie[:], d["c_experts"]), (thr[:], d["c_thresholds"]),
                                         (blk[:], d["c_blocks"])):
                            sp.dma_start(dst, src).then_inc(s_c, 16)
                    for e in range(E):
                        sp.dma_start(w1[:, e], rows(d["L1_ffn_W1"][e])).then_inc(s_we[e], 16)
                        sp.dma_start(w2[:, e], rows(d["L1_ffn_W2"][e])).then_inc(s_we[e], 16)

                @block.tensor
                def _(pe):
                    pe.wait_ge(s_c, 16 * NC_)
                    with pe.Fori(0, NB) as i:
                        pe.wait_ge(s_xs, i + 1)
                        for k in range(KD):
                            last = nc.tensor.transpose(pt[:, k * T:(k + 1) * T], xs[:, k * P:(k + 1) * P],
                                                       ident[0:T, 0:T])
                        last.then_inc(s_xTp, 1)
                        pe.wait_ge(s_xT, i + 1)
                        for k in range(KD):
                            last = nc.tensor.matmul(pl[0:T, bass.ds(i * E, E)], xT[:, k, :], wr[:, k, :],
                                                    start=k == 0, stop=k == KD - 1)
                        last.then_inc(s_l, 1)
                    pe.wait_ge(s_oh, 1)
                    o = oh[:, :, :].rearrange("p b e -> p (b e)")
                    nc.tensor.matmul(pp[0:T, 0:NB * E], tri[:, :], o, start=True, stop=True)
                    nc.tensor.matmul(pp[0:T, 256:256 + NB * E], ones[:, :], o, start=True, stop=True)\
                        .then_inc(s_pp, 1)

                @block.scalar
                def _(ac):
                    ac.wait_ge(s_lg, 1)
                    nc.scalar.activation(ex[:], lg[:], ACT.Exp, scale=-1.0).then_inc(s_ex, 1)
                    ac.wait_ge(s_ex, 1)

                @block.vector
                def _(dv):
                    ch = Chain(dv, s_ch, 0)
                    ch.base, ch.n = 0, 0
                    tt = nc.vector.tensor_tensor
                    ch.after(nc.vector.memset(ones[:], 1.0))
                    def take(i):
                        above(dv, s_xTp, i)
                        nc.vector.tensor_copy(xs[:], X[0:T, i, :]).then_inc(s_xs, 1)
                        dv.wait_ge(s_xTp, i + 1)
                        above(dv, s_l, i)
                        nc.vector.tensor_copy(xT[:, :, :].rearrange("p k t -> p (k t)"), pt[:, 0:KD * T])\
                            .then_inc(s_xT, 1)
                    take(0)
                    with dv.Fori(1, NB) as i:
                        take(i)
                    dv.wait_ge(s_l, NB)
                    dv.wait_ge(s_c, 16 * NC_)
                    tt(lg[:], pl[0:T, 0:NB * E].rearrange("p (b e) -> p b e", e=E),
                       br[:, :].unsqueeze(1).broadcast_to([T, NB, E]), ALU.add).then_inc(s_lg, 1)
                    dv.wait_ge(s_ex, 1)
                    ch.after(nc.vector.tensor_scalar(ex[:], ex[:], 1.0, None, ALU.add))
                    ch.after(nc.vector.reciprocal(route[:], ex[:]))
                    ch.after(nc.vector.reduce_max(gate[:], route[:], AX))
                    ch.after(tt(eq[:], route[:], gate[:, :].unsqueeze(2).broadcast_to([T, NB, E]), ALU.is_equal))
                    ch.after(nc.vector.scalar_tensor_tensor(out=eq[:], in0=eq[:], scalar=-float(E), in1=ie[:],
                                                            op0=ALU.mult, op1=ALU.add))
                    ch.after(nc.vector.tensor_reduce(ixe[:], eq[:], AX, ALU.min))
                    ch.after(nc.vector.tensor_scalar(ixe[:], ixe[:], float(E), None, ALU.add))
                    tt(oh[:], ie[:], ixe[:, :].unsqueeze(2).broadcast_to([T, NB, E]), ALU.is_equal).then_inc(s_oh, 1)
                    dv.wait_ge(s_pp, 1)
                    ch.after(nc.vector.tensor_copy(tot[:], pp[0:T, 256:256 + NB * E].rearrange("p (b e) -> p b e", e=E)))
                    src, n = tot, 0
                    for s in (1, 2, 4, 8):
                        dst = sc[n % 2]
                        ch.after(nc.vector.tensor_copy(dst[:, 0:s, :], src[:, 0:s, :]))
                        ch.after(tt(dst[:, s:NB, :], src[:, s:NB, :], src[:, 0:NB - s, :], ALU.add))
                        src, n = dst, n + 1
                    ch.after(tt(gt[:], src[:, NB - 1, :].unsqueeze(2).broadcast_to([T, E, NTH]), thr[:], ALU.is_gt))
                    ch.after(nc.vector.reduce_sum(nb_[:], gt[:], AX))
                    bsrc, n = nb_, 0
                    for s in (1, 2, 4):
                        dst = be[n % 2]
                        ch.after(nc.vector.tensor_copy(dst[:, 0:s], bsrc[:, 0:s]))
                        ch.after(tt(dst[:, s:E], bsrc[:, s:E], bsrc[:, 0:E - s], ALU.add))
                        bsrc, n = dst, n + 1
                    ch.after(tt(ge[:], blk[:], bsrc[0:1, :].unsqueeze(1).broadcast_to([1, NBK, E]), ALU.is_ge))
                    ch.after(nc.vector.reduce_sum(eb[:], ge[:], AX))
                    ch.after(nc.vector.tensor_scalar(eb[:], eb[:], float(E - 1), None, ALU.min))
                    ch.after(nc.vector.tensor_copy(ebu[:], eb[:]))
                    ch.after(tt(be[n % 2][:], bsrc[:], nb_[:], ALU.subtract))
                    st_ = be[n % 2]
                    ch.after(nc.vector.tensor_scalar(st_[:], st_[:], float(P), None, ALU.mult))
                    ch.after(tt(pos[:], src[:], tot[:], ALU.subtract))
                    ch.after(tt(pos[:], pos[:], pp[0:T, 0:NB * E].rearrange("p (b e) -> p b e", e=E), ALU.add))
                    ch.after(tt(pos[:], pos[:], st_[:, :].unsqueeze(1).broadcast_to([T, NB, E]), ALU.add))
                    ch.after(tt(pos[:], pos[:], oh[:], ALU.mult))
                    ch.after(nc.vector.reduce_sum(slf[:], pos[:], AX))
                    nc.vector.tensor_copy(slot[:], slf[:]).then_inc(s_rt, 1)
                    dv.wait_ge(s_rt, 1)

                @block.gpsimd
                def _(po):
                    po.wait_ge(s_rt, 1)
                    po.wait_ge(s_zero, 16 * NBK)
                    for b in range(NB):
                        po.indirect_dma_start(rows_in[:, :], bass.IndirectOffsetOnAxis(ap=slot[:, b:b + 1], axis=0),
                                              X[0:T, b, :], None).then_inc(s_sc, 16)
                    po.wait_ge(s_sc, 16 * NB)

        bk = Stage(nc, "rb")
        with bk:
            xr = [bk.sb(f"xr{l}", [P, D]) for l in range(2)]
            xT = [bk.sb(f"xT{l}", [P, KD, P]) for l in range(2)]
            g, gT = bk.sb("g", [P, F]), bk.sb("gT", [P, KF, P])
            yr = [bk.sb(f"yr{l}", [P, D]) for l in range(2)]
            px, py = bk.ps("px", [P, 512]), bk.ps("py", [P, 512])
            ph, pg = bk.ps("ph", [P, 2, 512]), bk.ps("pg", [P, 2, 512])
            s_xr = [bk.sem(f"block_loaded{l}") for l in range(2)]
            s_st = [bk.sem(f"block_stored{l}") for l in range(2)]
            s_xTp, s_xT, s_h, s_g = (bk.sem(n) for n in ("xT_in_psum", "xT_ready", "h_in_psum", "gelu_ready"))
            s_gp, s_gT, s_y, s_yr = (bk.sem(n) for n in ("gT_in_psum", "gT_ready", "y_in_psum", "y_ready"))

            with nc.Block() as block:
                @block.sync
                def _(sp):
                    for e in range(E):
                        sp.wait_ge(s_we[e], 32)
                        sp.sem_inc(s_wr, 1)

                    def store(k, l):
                        sp.wait_ge(s_yr, k + 1)
                        sp.dma_start(rows_out[bass.ds(k * P, P), :], yr[l][:]).then_inc(s_st[l], 16)
                    with sp.Fori(0, NBK // 2) as j:
                        store(2 * j, 0)
                        store(2 * j + 1, 1)
                    for l in range(2):
                        sp.wait_ge(s_st[l], 16 * (NBK // 2))

                @block.gpsimd
                def _(po):
                    def body(k, l, n):
                        above(po, s_xTp, k - 1)
                        po.dma_start(xr[l][:], rows_in[bass.ds(k * P, P), :]).then_inc(s_xr[l], 16)
                    for k in range(2):
                        body(k, k, 0)
                    with po.Fori(1, NBK // 2) as j:
                        body(2 * j, 0, j)
                        body(2 * j + 1, 1, j)

                @block.tensor
                def _(pe):
                    def turn_x(k, l, n):
                        pe.wait_ge(s_xr[l], 16 * n + 16)
                        above(pe, s_xT, k)
                        for c in range(KD):
                            last = nc.tensor.transpose(px[:, c * P:(c + 1) * P], xr[l][:, c * P:(c + 1) * P], ident[:, :])
                        last.then_inc(s_xTp, 1)

                    def up(k, l, e):
                        pe.wait_ge(s_wr, e + 1)
                        pe.wait_ge(s_xT, k + 1)
                        above(pe, s_g, k)
                        for n in range(2):
                            for c in range(KD):
                                last = nc.tensor.matmul(ph[:, n, :], xT[l][:, c, :], w1[:, e, c, n * 512:(n + 1) * 512],
                                                        start=c == 0, stop=c == KD - 1)
                        last.then_inc(s_h, 1)

                    def turn_g(k):
                        pe.wait_ge(s_g, k + 1)
                        above(pe, s_gT, k)
                        for f in range(KF):
                            last = nc.tensor.transpose(pg[:, f // 4, (f % 4) * P:(f % 4 + 1) * P],
                                                       g[:, f * P:(f + 1) * P], ident[:, :])
                        last.then_inc(s_gp, 1)

                    def down(k, e):
                        pe.wait_ge(s_gT, k + 1)
                        above(pe, s_yr, k)
                        for f in range(KF):
                            last = nc.tensor.matmul(py[:, 0:D], gT[:, f, :], w2[:, e, f, :],
                                                    start=f == 0, stop=f == KF - 1)
                        last.then_inc(s_y, 1)

                    def expert(k):
                        return pe.value_load(ebu[0:1, bass.ds(k, 1)], min_val=0, max_val=E - 1)

                    def two(j):
                        for m in range(2):
                            k = 2 * j + (m + 1)
                            turn_g(k - 1)
                            up(k, (m + 1) % 2, expert(k))
                            turn_x(k + 1, m % 2, j + 1)
                            down(k - 1, expert(k - 1))
                    turn_x(0, 0, 0)
                    up(0, 0, expert(0))
                    turn_x(1, 1, 0)
                    two(0)
                    with pe.Fori(1, NBK // 2 - 1) as j:
                        two(j)
                    turn_g(NBK - 2)
                    up(NBK - 1, 1, expert(NBK - 1))
                    down(NBK - 2, expert(NBK - 2))
                    turn_g(NBK - 1)
                    down(NBK - 1, expert(NBK - 1))

                @block.scalar
                def _(ac):
                    def body(k):
                        ac.wait_ge(s_h, k + 1)
                        above(ac, s_gp, k)
                        nc.scalar.activation(g[:], ph[:, :, :].rearrange("p n c -> p (n c)"), ACT.Gelu).then_inc(s_g, 1)
                    body(0)
                    with ac.Fori(1, NBK) as k:
                        body(k)

                @block.vector
                def _(dv):
                    def take_x(k, l):
                        dv.wait_ge(s_xTp, k + 1)
                        above(dv, s_h, k - 1)
                        nc.vector.tensor_copy(xT[l][:, :, :].rearrange("p k t -> p (k t)"), px[:, 0:D]).then_inc(s_xT, 1)

                    def take_g(k):
                        dv.wait_ge(s_gp, k + 1)
                        above(dv, s_y, k)
                        nc.vector.tensor_copy(gT[:, :, :].rearrange("p f t -> p (f t)"),
                                              pg[:, :, :].rearrange("p n c -> p (n c)")).then_inc(s_gT, 1)

                    def take_y(k, l, n):
                        dv.wait_ge(s_y, k + 1)
                        above(dv, s_st[l], 16 * n)
                        nc.vector.tensor_copy(yr[l][:], py[:, 0:D]).then_inc(s_yr, 1)

                    take_x(0, 0)
                    take_x(1, 1)
                    def two(j):
                        for m in range(2):
                            k = 2 * j + (m + 1)
                            take_g(k - 1)
                            take_x(k + 1, m % 2)
                            take_y(k - 1, m % 2, j)
                    two(0)
                    with dv.Fori(1, NBK // 2 - 1) as j:
                        two(j)
                    take_g(NBK - 2)
                    take_y(NBK - 2, 0, NBK // 2 - 1)
                    take_g(NBK - 1)
                    take_y(NBK - 1, 1, NBK // 2 - 1)


        fn = Stage(nc, "rn")
        with fn:
            y = fn.sb("y", [T, NB, D])
            st6, mv, rs, eps = fn.sb("st6", [T, NB, 6]), fn.sb("mv", [T, NB, 2]), fn.sb("rs", [T, 2, NB]), fn.sb("eps", [T, 1])
            s_ga, s_z, s_sm, s_mv = fn.sem("rows_gathered"), fn.sem("sums_ready"), fn.sem("stats_ready"), fn.sem("means_ready")
            s_ln, s_rs, s_x, s_out = fn.sem("log_ready"), fn.sem("rstd_ready"), fn.sem("x_done"), fn.sem("out_stored")
            s_gb = [fn.sem(f"gathered{b}") for b in range(4)]
            with nc.Block() as block:
                @block.gpsimd
                def _(po):
                    for b in range(NB):
                        po.indirect_dma_start(y[:, b, :], None, rows_out[:, :],
                                              bass.IndirectOffsetOnAxis(ap=slot[:, b:b + 1], axis=0))\
                            .then_inc(s_gb[b // 4], 16)

                @block.vector
                def _(dv):
                    nc.vector.memset(eps[:], EPS).then_inc(s_z, 1)
                    for b in range(NB):
                        if b % 4 == 0:
                            dv.wait_ge(s_gb[b // 4], 64)
                        nc.vector.scalar_tensor_tensor(out=X[0:T, b, :], in0=y[:, b, :], scalar=gate[:, b:b + 1],
                                                       in1=X[0:T, b, :], op0=ALU.mult, op1=ALU.add).then_inc(s_sm, 1)
                        if b:
                            dv.wait_ge(s_sm, b)
                            nc.vector.bn_stats(st6[:, b - 1, :], X[0:T, b - 1, :]).then_inc(s_mv, 1)
                    dv.wait_ge(s_sm, NB)
                    nc.vector.bn_stats(st6[:, NB - 1, :], X[0:T, NB - 1, :]).then_inc(s_mv, 1)
                    dv.wait_ge(s_mv, NB)
                    for b in range(NB):
                        nc.vector.bn_aggr(mv[:, b, :], st6[:, b, :]).then_inc(s_mv, 1)
                    dv.wait_ge(s_rs, 1)
                    for b in range(NB):
                        nc.vector.tensor_scalar(X[0:T, b, :], X[0:T, b, :], mv[:, b, 0:1], rs[:, 1, b:b + 1],
                                                ALU.subtract, ALU.mult).then_inc(s_x, 1)

                @block.scalar
                def _(ac):
                    ac.wait_ge(s_z, 1)
                    ac.wait_ge(s_mv, 2 * NB)
                    nc.scalar.activation(rs[:, 0, :], mv[:, :, 1], ACT.Ln, bias=eps[:, 0:1]).then_inc(s_ln, 1)
                    ac.wait_ge(s_ln, 1)
                    nc.scalar.activation(rs[:, 1, :], rs[:, 0, :], ACT.Exp, scale=-0.5).then_inc(s_rs, 1)

                @block.sync
                def _(sp):
                    o = out.rearrange("b t d -> t b d")
                    for b in range(0, NB, 4):
                        sp.wait_ge(s_x, b + 4)
                        sp.dma_start(o[:, b:b + 4, :], X[0:T, b:b + 4, :]).then_inc(s_out, 16)
                    sp.wait_ge(s_out, 16 * (NB // 4))


def build(nc, d, out, stages=6, start=0):
    rows_in = nc.dram_tensor("rows_in", (NBK * P, D), F32).ap()
    rows_out = nc.dram_tensor("rows_out", (NBK * P, D), F32).ap()
    st = Stage(nc, "io")
    with st:
        X = st.sb("X", [P, NB, D])
        ident, zero = st.sb("ident", [P, P]), st.sb("zero", [P, D])
        s_in, s_out = st.sem("x_loaded"), st.sem("out_stored")
        s_z, s_zero = st.sem("zero_ready"), st.sem("rows_zeroed")
        with nc.Block() as block:
            @block.vector
            def _(dv):
                nc.vector.memset(zero[:], 0.0).then_inc(s_z, 1)

            @block.sync
            def _(sp):
                sp.dma_start(ident[:], d["c_ident"]).then_inc(s_in, 16)
                sp.dma_start(X[0:T, :, :], d["x"].rearrange("b t d -> t b d")).then_inc(s_in, 16)
                sp.wait_ge(s_z, 1)
                for k in range(NBK):
                    sp.dma_start(rows_in[k * P:(k + 1) * P, :], zero[:]).then_inc(s_zero, 16)
                sp.wait_ge(s_in, 32)
        for n, stage in enumerate((self_attention, cross_attention, expert_adapter, bucket_attention,
                                   latent_attention)):
            if start <= n < stages:
                stage(nc, X, ident, d)
        if stages == 6:
            routed_ffn(nc, X, ident, d, out, rows_in, rows_out, s_zero)
            return
        with nc.Block() as block:
            @block.sync
            def _(sp):
                sp.wait_ge(s_zero, 16 * NBK)
                sp.dma_start(out.rearrange("b t d -> t b d"), X[0:T, :, :]).then_inc(s_out, 16)
                sp.wait_ge(s_out, 16)


def shape_constants():
    f = np.float32
    inv = (f(1.0) / (f(10000.0) ** (np.arange(0, DH, 2, dtype=f) / f(DH)))).astype(f)
    fr = (np.arange(T, dtype=f)[:, None] * inv[None, :]).astype(f)
    s, t = np.arange(T)[:, None], np.arange(T)[None, :]
    return {
        "c_cos": np.cos(fr).astype(f), "c_sin": np.sin(fr).astype(f),
        "c_causal": np.where(s <= t, 0.0, -BIG).astype(f),
        "c_hmask": (np.arange(P)[:, None] // DH == np.arange(HG)[None, :]).astype(f),
        "c_sel": np.broadcast_to(np.eye(NB, dtype=f), (T, NB, NB)).copy(),
        "c_pow2": np.tile((2.0 ** np.arange(6)).astype(f), (T, NH)),
        "c_half": (np.arange(P)[:, None] // (P // 2) == np.arange(2)[None, :]).astype(f),
        "c_tri": (s < t).astype(f), "c_experts": np.broadcast_to(np.arange(8, dtype=f), (T, NB, 8)).copy(),
        "c_thresholds": np.broadcast_to(P * np.arange(NTH, dtype=f), (T, 8, NTH)).copy(),
        "c_blocks": np.broadcast_to(np.arange(NBK, dtype=f)[None, :, None], (1, NBK, 8)).copy(),
        "c_ident": np.eye(P, dtype=f),
    }


def kernel(**inputs):
    import concourse.bacc as bacc
    from concourse.bass_utils import run_bass_kernel_spmd

    nc = bacc.Bacc("TRN2", target_bir_lowering=False, num_devices=1)
    arrays, d = {}, {}
    for name, a in {**inputs, **shape_constants()}.items():
        a = np.ascontiguousarray(a)
        if a.dtype == np.bool_:
            a = a.view(np.uint8)
        arrays[f"in_{name}"] = a
        d[name] = nc.dram_tensor(f"in_{name}", a.shape, mybir.dt.from_np(a.dtype), kind="ExternalInput").ap()
    out = nc.dram_tensor("out", (NB, T, D), F32, kind="ExternalOutput").ap()
    build(nc, d, out)
    r = run_bass_kernel_spmd(nc, [arrays], core_ids=[0])
    return r.results[0]["out"]
```

```python
from contextlib import ExitStack

import concourse.bass as bass
import numpy as np
from concourse import mybir

F32 = mybir.dt.float32
U32 = mybir.dt.uint32
U8 = mybir.dt.uint8
BF16 = mybir.dt.bfloat16
ALU = mybir.AluOpType
ACT = mybir.ActivationFunctionType
AX = mybir.AxisListType.X

P = 128
NB, T, D = 16, 100, 256
KD = D // P
NH = 16
DH = D // NH
HG = P // DH
NBR = 4
SC = 361
EPS = 1e-5
BIG = 1e30


class Chain:

    def __init__(self, eng, sem, per):
        self.eng, self.sem, self.per = eng, sem, per

    def start(self, i):
        self.base, self.n = i * self.per, 0

    def after(self, ins):
        ins.then_inc(self.sem, 1)
        self.n += 1
        self.eng.wait_ge(self.sem, self.base + self.n)

    def end(self):
        assert self.n == self.per, (self.sem, self.n)


class Stage:

    def __init__(self, nc, name):
        self.nc, self.name, self.ctx, self.sems = nc, name, ExitStack(), []

    def __enter__(self):
        self.ctx.__enter__()
        return self

    def __exit__(self, *a):
        if self.sems and a[0] is None:
            self.nc.clear_and_free_semaphores(self.sems)
            self.nc.all_engine_barrier()
        return self.ctx.__exit__(*a)

    def sb(self, name, shape, dt=F32):
        return self.ctx.enter_context(self.nc.sbuf_tensor(f"{self.name}_{name}", shape, dt))

    def ps(self, name, shape):
        return self.ctx.enter_context(self.nc.psum_tensor(f"{self.name}_{name}", shape, F32))

    def sem(self, name):
        self.sems.append(self.nc.alloc_semaphore(f"{self.name}_{name}"))
        return self.sems[-1]


def rows(w):
    return w.rearrange("(k p) n -> p k n", p=P)


def bcast(v, parts):
    n = v.shape[0]
    return v.rearrange("(a n) -> a n", a=1).broadcast_to([parts, n])


class Side:

    def __init__(self, slots, filled, read):
        self.slots, self.filled, self.read = slots, filled, read
        names = [s for slot in slots for s in slot]
        self.fronts = [s for s in names if s[0] == "f"]
        self.backs = [s for s in names if s[0] == "b"]
        self.all = names

    def steps(self, i, m):
        first, last = isinstance(i, int) and i == 0, isinstance(i, int) and i == NB - 1
        keep = [s for s in self.all if not (first and s[0] == "b") and not (last and s[0] == "f")]
        if first:
            base = len(self.fronts)
        else:
            base = 2 * len(self.fronts) + (i - 1) * len(self.all)
        return [(s, base + keep.index(s)) for s in self.slots[m] if s in keep]

    def prologue(self):
        return [(s, n) for n, s in enumerate(self.fronts)]

    def epilogue(self):
        base = NB * len(self.fronts) + (NB - 1) * len(self.backs)
        return [(s, base + n) for n, s in enumerate(self.backs)]

    def read_of(self, i, name):
        if isinstance(i, int) and i == 0:
            return self.fronts.index(name) + 1
        m = next(m for m, slot in enumerate(self.slots) if name in slot)
        return dict(self.steps(i - 1, m))[name] + 1

    def front_done(self, i):
        if isinstance(i, int) and i == 0:
            return len(self.fronts)
        last = max(self.all.index(s) for s in self.fronts)
        off = sum(1 for s in self.all[:last + 1] if s[0] == "b") if isinstance(i, int) and i == 1 else 0
        if isinstance(i, int) and i == 1:
            return len(self.fronts) + last + 1 - off
        return 2 * len(self.fronts) + (i - 2) * len(self.all) + last + 1


def above(eng, sem, n):
    if not isinstance(n, int) or n > 0:
        eng.wait_ge(sem, n)


def over_batches(eng, body, apart=1):
    body(0, 0)
    with eng.Fori(0, (NB - 1 - apart) // 2) as j:
        body(2 * j + 1, 1)
        body(2 * j + 2, 0)
    for i in range(NB - apart, NB):
        body(i, i % 2)


def parts(o):
    return [not isinstance(o, int) or 0 <= o + n < NB for n in (3, 2, 1, 0)]


def four_in_flight(eng, body):
    for o in range(-3, 1):
        body(o, o % 2)
    with eng.Fori(0, (NB - 4) // 2) as j:
        body(2 * j + 1, 1)
        body(2 * j + 2, 0)
    for o in range(NB - 3, NB):
        body(o, o % 2)


def self_attention(nc, X, ident, d):
    CS = float(np.pi / np.sqrt(3.0))
    NU = HG * NBR * T
    st = Stage(nc, "sa")
    with st:
        sb, ps, sem = st.sb, st.ps, st.sem
        wq, wv = sb("wq", [P, KD, NBR * D]), sb("wv", [P, KD, NBR * D])
        wk, wo = sb("wk", [P, KD, D]), sb("wo", [P, KD, D])
        bq, bv = sb("bq", [T, NBR * D]), sb("bv", [T, NBR * D])
        bk, bo = sb("bk", [T, D]), sb("bo", [T, D])
        cos, sin = sb("cos", [T, DH // 2]), sb("sin", [T, DH // 2])
        causal = sb("causal", [T, T])
        hmask = sb("hmask", [P, HG])
        sink, csk = sb("sink", [T, NBR * NH]), sb("csk", [T, NBR * NH])
        csvn = sb("csvn", [T, NBR * D])
        xs = sb("xs", [T, D])
        xT = sb("xT", [P, KD, T])
        qn, qr = sb("qn", [T, NBR * D]), sb("qr", [T, NBR * D])
        qa, qb = sb("qa", [T, NBR * D // 2]), sb("qb", [T, NBR * D // 2])
        kn, kr = sb("kn", [T, D]), sb("kr", [T, D])
        ka = sb("ka", [T, 4, D // 2])
        ksq, kss, kf = sb("ksq", [T, D]), sb("kss", [T, NH]), sb("kf", [T, NH])
        va = sb("va", [T, 2, NBR * NH, 32])
        qT = sb("qT", [P, KD, NBR, T])
        kTm = sb("kTm", [P, KD, HG, T])
        sm = sb("sm", [T, KD, HG, NBR, T])
        L = sb("L", [T, 2, KD, HG, NBR, T])
        avT = sb("avT", [P, 4, T])
        oN = sb("oN", [T, KD, NBR, HG, 32])
        den, alpha = sb("den", [T, NBR, HG]), sb("alpha", [T, NBR, HG])
        num = sb("num", [T, NBR, P])
        cx = sb("cx", [T, D])
        cxT = sb("cxT", [P, KD, T])
        xb, y = sb("xb", [T, D]), sb("y", [T, D])
        stats, mv, rs = sb("stats", [T, 6]), sb("mv", [T, 2]), sb("rs", [T, 2])
        eps = sb("eps", [T, 1])
        gap = sb("gap", [T, 1])
        pS = ps("pS", [P, 4, 512])
        pq = ps("pq", [P, 2, 512])
        pk = ps("pk", [P, 512])
        pb = ps("pb", [P, 512])

        s_w, s_c = sem("weights_loaded"), sem("consts_ready")
        s_xs, s_xTp, s_xT = sem("xs_staged"), sem("xT_in_psum"), sem("xT_ready")
        s_kp, s_kr = sem("k_in_psum"), sem("k_roped")
        s_ks, s_kf = sem("k_square_sums"), sem("k_factors")
        s_kTp, s_kT = sem("kT_in_psum"), sem("kT_ready")
        s_qp, s_qn, s_qr = sem("q_in_psum"), sem("q_read"), sem("q_roped")
        s_qTp, s_qT = sem("qT_in_psum"), sem("qT_ready")
        s_vp, s_v = sem("v_in_psum"), sem("v_ready")
        s_S, s_sm = sem("scores_in_psum"), sem("scores_masked")
        s_L, s_W, s_G = sem("logs_ready"), sem("softplus_ready"), sem("gated_ready")
        s_av, s_avT = sem("av_in_psum"), sem("av_read")
        s_oNp, s_oN, s_nm = sem("out_in_psum"), sem("out_read"), sem("normed")
        s_cTp, s_cT, s_y, s_yr = sem("ctxT_in_psum"), sem("ctxT_ready"), sem("y_in_psum"), sem("y_read")
        s_mv, s_rs, s_x = sem("ln_stats"), sem("ln_rstd"), sem("x_done")
        s_xb = sem("x_plus_bias")
        s_d1, s_d2 = sem("setup_chain"), sem("k_rope_chain")
        s_d4, s_d5, s_d6 = sem("mask_chain"), sem("norm_chain"), sem("ln_chain")
        s_a1, s_a2, s_a3, s_po = sem("k_factor_chain"), sem("exps_done"), sem("rstd_chain"), sem("q_rope_chain")
        NW = 14

        with nc.Block() as block:
            @block.sync
            def _(sp):
                for dst, src in ((wk[:], rows(d["L0_attn_Wk"])), (wq[:], rows(d["L0_attn_Wq"])),
                                 (wv[:], rows(d["L0_attn_Wv"])), (wo[:], rows(d["L0_attn_Wo"])),
                                 (bk[:], bcast(d["L0_attn_bk"], T)), (bq[:], bcast(d["L0_attn_bq"], T)),
                                 (bv[:], bcast(d["L0_attn_bv"], T)), (bo[:], bcast(d["L0_attn_bo"], T)),
                                 (cos[:], d["c_cos"]), (sin[:], d["c_sin"]),
                                 (causal[:], d["c_causal"]), (hmask[:], d["c_hmask"]),
                                 (sink[:], bcast(d["L0_attn_sink_scalars"].rearrange("a b c -> (a b c)"), T)),
                                 (csvn[:], bcast(d["L0_attn_v_nulls"].rearrange("a b -> (a b)"), T))):
                    sp.dma_start(dst, src).then_inc(s_w, 16)


            @block.tensor
            def _(pe):
                def x_turned(f):
                    pe.wait_ge(s_xs, f + 1)
                    above(pe, s_kT, f)
                    for k in range(KD):
                        last = nc.tensor.transpose(pk[:, k * T:(k + 1) * T], xs[:, k * P:(k + 1) * P],
                                                   ident[0:T, 0:T])
                    last.then_inc(s_xTp, 1)

                def k_projected(f):
                    pe.wait_ge(s_xT, f + 1)
                    for k in range(KD):
                        last = nc.tensor.matmul(pk[0:T, 256:512], xT[:, k, :], wk[:, k, :],
                                                start=k == 0, stop=k == KD - 1)
                    last.then_inc(s_kp, 1)

                def q_projected(f):
                    above(pe, s_v, f)
                    for n in range(2):
                        for k in range(KD):
                            last = nc.tensor.matmul(pq[0:T, n, :], xT[:, k, :], wq[:, k, n * 512:(n + 1) * 512],
                                                    start=k == 0, stop=k == KD - 1)
                    last.then_inc(s_qp, 1)

                def k_turned(f):
                    pe.wait_ge(s_kr, f + 1)
                    for k in range(KD):
                        last = nc.tensor.transpose(pk[:, k * T:(k + 1) * T], kr[:, k * P:(k + 1) * P],
                                                   ident[0:T, 0:T])
                    last.then_inc(s_kTp, 1)

                def q_turned(f):
                    pe.wait_ge(s_qr, f + 1)
                    pe.wait_ge(s_qn, f + 1)
                    for k in range(KD):
                        for r in range(NBR):
                            last = nc.tensor.transpose(pq[:, k, r * T:(r + 1) * T],
                                                       qr[:, r * D + k * P:r * D + (k + 1) * P], ident[0:T, 0:T])
                    last.then_inc(s_qTp, 1)

                def v_projected(f):
                    pe.wait_ge(s_qT, f + 1)
                    for n in range(2):
                        for k in range(KD):
                            last = nc.tensor.matmul(pq[0:T, n, :], xT[:, k, :], wv[:, k, n * 512:(n + 1) * 512],
                                                    start=k == 0, stop=k == KD - 1)
                    last.then_inc(s_vp, 1)

                def scores(s, m):
                    if m == 0:
                        pe.wait_ge(s_kT, s + 1)
                        pe.wait_ge(s_qT, s + 1)
                    above(pe, s_sm, s * HG + (m - 1))
                    g, h = m // 4, 2 * (m % 4)
                    for e in range(2):
                        last = nc.tensor.matmul(pS[0:T, 2 * (m % 2) + e, 0:NBR * T], kTm[:, g, h + e, :],
                                                qT[:, g, :, :], start=True, stop=True)
                    last.then_inc(s_S, 1)

                def values(v, par, c):
                    g = c // 2
                    if c % 2 == 0:
                        pe.wait_ge(s_G, v * 2 + (g + 1))
                    if c == 0:
                        pe.wait_ge(s_v, v + 1)
                        above(pe, s_yr, v)
                    else:
                        pe.wait_ge(s_oN, v * 4 + c)
                    for rr in range(2):
                        r = 2 * (c % 2) + rr
                        for m in range(2):
                            for j in range(4):
                                hh = 4 * m + j
                                last = nc.tensor.matmul(
                                    pb[32 * j:32 * j + 32, (2 * rr + m) * T:(2 * rr + m + 1) * T],
                                    va[:, par, r * NH + g * HG + hh, :], L[:, par, g, hh, r, :],
                                    start=True, stop=True)
                    last.then_inc(s_av, 1)

                def values_turned(v, c):
                    pe.wait_ge(s_avT, v * 4 + (c + 1))
                    for q in range(4):
                        last = nc.tensor.transpose(pb[0:T, q * P:(q + 1) * P], avT[:, q, :], ident[:, :])
                    last.then_inc(s_oNp, 1)

                def context_turned(o):
                    pe.wait_ge(s_nm, o * 2 + 2)
                    pe.wait_ge(s_oN, o * 4 + 4)
                    for k in range(KD):
                        last = nc.tensor.transpose(pb[:, k * T:(k + 1) * T], cx[:, k * P:(k + 1) * P],
                                                   ident[0:T, 0:T])
                    last.then_inc(s_cTp, 1)

                def out_projected(o):
                    pe.wait_ge(s_cT, o + 1)
                    for k in range(KD):
                        last = nc.tensor.matmul(pb[0:T, 256:512], cxT[:, k, :], wo[:, k, :],
                                                start=k == 0, stop=k == KD - 1)
                    last.then_inc(s_y, 1)

                def body(o, par):
                    F, S, V, O = parts(o)
                    f, s, v = o + 3, o + 2, o + 1
                    vp = (par + 1) % 2
                    if O:
                        context_turned(o)
                    if S:
                        scores(s, 0)
                    if F:
                        x_turned(f)
                    if S:
                        scores(s, 1)
                    if O:
                        out_projected(o)
                    if S:
                        scores(s, 2)
                    if V:
                        values(v, vp, 0)
                    if F:
                        k_projected(f)
                    if S:
                        scores(s, 3)
                    if V:
                        values_turned(v, 0)
                    if S:
                        scores(s, 4)
                    if V:
                        values(v, vp, 1)
                    if F:
                        q_projected(f)
                    if V:
                        values_turned(v, 1)
                    if S:
                        scores(s, 5)
                    if V:
                        values(v, vp, 2)
                    if S:
                        scores(s, 6)
                    if V:
                        values_turned(v, 2)
                    if S:
                        scores(s, 7)
                    if F:
                        k_turned(f)
                    if V:
                        values(v, vp, 3)
                    if F:
                        q_turned(f)
                    if V:
                        values_turned(v, 3)
                    if F:
                        v_projected(f)

                pe.wait_ge(s_w, 16 * NW)
                four_in_flight(pe, body)

            @block.vector
            def _(dv):
                cs, ck, cm = Chain(dv, s_d1, 0), Chain(dv, s_d2, 5), Chain(dv, s_d4, HG)
                cn, cf = Chain(dv, s_d5, 2 * 4), Chain(dv, s_d6, 1)

                def xT_read(f):
                    dv.wait_ge(s_xTp, f + 1)
                    above(dv, s_vp, f)
                    nc.vector.tensor_copy(xT[:, :, :].rearrange("p k t -> p (k t)"), pk[:, 0:KD * T])\
                        .then_inc(s_xT, 1)

                def k_roped(f):
                    ck.start(f)
                    dv.wait_ge(s_kp, f + 1)
                    above(dv, s_kTp, f)
                    ck.after(nc.vector.tensor_tensor(kn[:], pk[0:T, 256:512], bk[:], ALU.add))
                    h = kn[:, :].rearrange("p (h c two) -> p h c two", h=NH, two=2)
                    o = kr[:, :].rearrange("p (h c) -> p h c", h=NH)
                    c = cos[:, :].unsqueeze(1).broadcast_to([T, NH, DH // 2])
                    s = sin[:, :].unsqueeze(1).broadcast_to([T, NH, DH // 2])
                    A = [ka[:, n].rearrange("p (h c) -> p h c", h=NH) for n in range(4)]
                    for n, (x, y_) in enumerate(((0, c), (1, s), (0, s), (1, c))):
                        ins = nc.vector.tensor_tensor(A[n], h[:, :, :, x], y_, ALU.mult)
                    ck.after(ins)
                    nc.vector.tensor_tensor(o[:, :, 0:DH // 2], A[0], A[1], ALU.subtract)
                    ck.after(nc.vector.tensor_tensor(o[:, :, DH // 2:DH], A[2], A[3], ALU.add))
                    ck.after(nc.vector.tensor_tensor(ksq[:], kr[:], kr[:], ALU.mult))
                    ck.after(nc.vector.reduce_sum(kss[:], ksq[:, :].rearrange("p (h c) -> p h c", h=NH), AX))
                    nc.vector.tensor_scalar(kss[:], kss[:], 1e-6, None, ALU.max).then_inc(s_ks, 1)

                def q_biased(f):
                    dv.wait_ge(s_qp, f + 1)
                    above(dv, s_qr, f)
                    nc.vector.tensor_tensor(qn[:, :].rearrange("p (n c) -> p n c", n=2), pq[0:T, :, :],
                                            bq[:, :].rearrange("p (n c) -> p n c", n=2), ALU.add).then_inc(s_qn, 1)

                def k_scaled(f):
                    dv.wait_ge(s_kf, f + 1)
                    o = kr[:, :].rearrange("p (h c) -> p h c", h=NH)
                    nc.vector.tensor_tensor(o, o, kf[:, :].unsqueeze(2).broadcast_to([T, NH, DH]), ALU.mult)\
                        .then_inc(s_kr, 1)

                def kT_read(f):
                    dv.wait_ge(s_kTp, f + 1)
                    kk = pk[:, 0:KD * T].rearrange("p (k t) -> p k t", k=KD)
                    nc.vector.tensor_tensor(
                        kTm[:, :, :, :], kk.unsqueeze(2).broadcast_to([P, KD, HG, T]),
                        hmask[:, :].unsqueeze(1).unsqueeze(3).broadcast_to([P, KD, HG, T]), ALU.mult).then_inc(s_kT, 1)

                def v_biased(f, par):
                    dv.wait_ge(s_vp, f + 1)
                    nc.vector.tensor_tensor(va[:, par, :, 0:DH],
                                            pq[0:T, :, :].rearrange("p n (h c) -> p (n h) c", c=DH),
                                            bv[:, :].rearrange("p (h c) -> p h c", c=DH), ALU.add).then_inc(s_v, 1)

                def masked(s, par, m, o):
                    g, h = m // 4, 2 * (m % 4)
                    if m == 0:
                        cm.start(s)
                        above(dv, s_av, o * 4 + 4)
                    dv.wait_ge(s_S, s * HG + (m + 1))
                    mask = causal[:, :].unsqueeze(1).unsqueeze(1).broadcast_to([T, 2, NBR, T])
                    two = pS[0:T, 2 * (m % 2):2 * (m % 2) + 2, 0:NBR * T].rearrange("p e (r t) -> p e r t", r=NBR)
                    cm.after(nc.vector.tensor_tensor(sm[:, g, h:h + 2, :, :], two, mask, ALU.add))
                    nc.vector.tensor_scalar(
                        L[:, par, g, h:h + 2, :, :].rearrange("p h r t -> p (h r t)"),
                        sm[:, g, h:h + 2, :, :].rearrange("p h r t -> p (h r t)"),
                        30.0, None, ALU.min).then_inc(s_sm, 1)

                def softplus(s, par, g):
                    dv.wait_ge(s_L, s * 2 + (g + 1))
                    nc.vector.tensor_tensor(L[:, par, g].rearrange("p h r t -> p (h r t)"),
                                            L[:, par, g].rearrange("p h r t -> p (h r t)"),
                                            sm[:, g].rearrange("p h r t -> p (h r t)"), ALU.max).then_inc(s_W, 1)

                def norm(v, g):
                    if g == 0:
                        cn.start(v)
                    dv.wait_ge(s_oN, v * 4 + (g + 1) * 2)
                    k3 = csk[:, :].rearrange("p (r g h) -> p r g h", r=NBR, g=KD)[:, :, g, :]
                    v4 = csvn[:, :].rearrange("p (r g c) -> p r g c", r=NBR, g=KD)[:, :, g, :]
                    cn.after(nc.vector.tensor_tensor(den[:], oN[:, g, :, :, DH], k3, ALU.add))
                    cn.after(nc.vector.reciprocal(alpha[:], den[:]))
                    cn.after(nc.vector.tensor_tensor(num[:, :, :].rearrange("p r (h c) -> p r h c", c=DH),
                                                     oN[:, g, :, :, 0:DH],
                                                     v4.rearrange("p r (h c) -> p r h c", c=DH), ALU.add))
                    n3 = num[:, :, :].rearrange("p r (h c) -> p (r h) c", c=DH)
                    cn.after(nc.vector.tensor_tensor(
                        n3, n3, alpha[:, :, :].rearrange("p r h -> p (r h)").unsqueeze(2)
                        .broadcast_to([T, NBR * HG, DH]), ALU.mult))
                    if g == 0:
                        above(dv, s_cTp, v)
                    nc.vector.reduce_sum(cx[:, g * P:(g + 1) * P], num[:, :, :].rearrange("p r c -> p c r"), AX)\
                        .then_inc(s_nm, 1)

                def context_read(o):
                    dv.wait_ge(s_cTp, o + 1)
                    nc.vector.tensor_copy(cxT[:, :, :].rearrange("p k t -> p (k t)"), pb[:, 0:KD * T])\
                        .then_inc(s_cT, 1)

                def residual(o):
                    dv.wait_ge(s_y, o + 1)
                    dv.wait_ge(s_xb, o + 1)
                    nc.vector.scalar_tensor_tensor(out=y[:], in0=pb[0:T, 256:512], scalar=1.0 / NBR, in1=xb[:],
                                                   op0=ALU.mult, op1=ALU.add).then_inc(s_yr, 1)
                    dv.wait_ge(s_yr, o + 1)
                    cf.start(o)
                    cf.after(nc.vector.bn_stats(stats[:], y[:]))
                    nc.vector.memset(gap[:], 0.0)
                    nc.vector.bn_aggr(mv[:], stats[:]).then_inc(s_mv, 1)

                def normed(o):
                    dv.wait_ge(s_rs, o + 1)
                    nc.vector.tensor_scalar(X[0:T, o, :], y[:], mv[:, 0:1], rs[:, 1:2], ALU.subtract, ALU.mult)\
                        .then_inc(s_x, 1)

                def body(o, par):
                    F, S, V, O = parts(o)
                    f, s, v = o + 3, o + 2, o + 1
                    if O:
                        context_read(o)
                    if S:
                        masked(s, par, 0, o)
                    if F:
                        xT_read(f)
                    if S:
                        masked(s, par, 1, o)
                    if O:
                        residual(o)
                    if S:
                        masked(s, par, 2, o)
                    if F:
                        k_roped(f)
                    if S:
                        masked(s, par, 3, o)
                    if O:
                        normed(o)
                    if S:
                        masked(s, par, 4, o)
                    if F:
                        q_biased(f)
                        k_scaled(f)
                    if S:
                        masked(s, par, 5, o)
                        softplus(s, par, 0)
                    if V:
                        norm(v, 0)
                    if S:
                        masked(s, par, 6, o)
                        masked(s, par, 7, o)
                    if F:
                        kT_read(f)
                    if V:
                        norm(v, 1)
                    if S:
                        softplus(s, par, 1)
                    if F:
                        v_biased(f, (par + 1) % 2)

                cs.start(0)
                cs.after(nc.vector.memset(va[:], 0.0))
                cs.after(nc.vector.memset(va[:, :, :, DH:DH + 1], 1.0))
                cs.after(nc.vector.memset(eps[:], EPS))
                dv.wait_ge(s_w, 16 * NW)
                dv.wait_ge(s_c, 1)
                cs.after(nc.vector.tensor_scalar(sink[:], sink[:], 1e-6, None, ALU.add))
                cs.after(nc.vector.tensor_scalar(csk[:], sink[:], 1e-6, CS, ALU.add, ALU.mult))
                v3 = csvn[:, :].rearrange("p (h c) -> p h c", c=DH)
                cs.after(nc.vector.tensor_tensor(v3, v3, sink[:, :].unsqueeze(2).broadcast_to([T, NBR * NH, DH]),
                                                 ALU.mult))
                cs.after(nc.vector.tensor_scalar(csvn[:], csvn[:], CS, None, ALU.mult))
                four_in_flight(dv, body)

            @block.scalar
            def _(ac):
                def k_factors(f):
                    ac.wait_ge(s_ks, f + 1)
                    above(ac, s_kr, f)
                    nc.scalar.activation(kf[:], kss[:], ACT.Ln).then_inc(s_a1, 1)
                    ac.wait_ge(s_a1, f * 2 + 1)
                    nc.scalar.activation(kf[:], kf[:], ACT.Exp, scale=-0.5).then_inc(s_a1, 1)
                    ac.wait_ge(s_a1, f * 2 + 2)
                    nc.scalar.mul(kf[:], kf[:], DH ** -0.5).then_inc(s_kf, 1)

                def qT_read(f):
                    ac.wait_ge(s_qTp, f + 1)
                    nc.scalar.copy(qT[:, :, :, :].rearrange("p k r t -> p k (r t)"), pq[:, :, 0:NBR * T])\
                        .then_inc(s_qT, 1)

                def exponential(s, par, m):
                    g, h = m // 4, 2 * (m % 4)
                    ac.wait_ge(s_sm, s * HG + (m + 1))
                    w = L[:, par, g, h:h + 2].rearrange("p h r t -> p (h r t)")
                    ins = nc.scalar.activation(w, w, ACT.Exp)
                    if m % 4 == 3:
                        ins.then_inc(s_a2, 1)

                def logarithm(s, par, g):
                    ac.wait_ge(s_a2, s * 2 + (g + 1))
                    w = L[:, par, g].rearrange("p h r t -> p (h r t)")
                    nc.scalar.activation(w, w, ACT.Ln, bias=1.0).then_inc(s_L, 1)

                def gate(v, par, g):
                    ac.wait_ge(s_W, v * 2 + (g + 1))
                    w = L[:, par, g].rearrange("p h r t -> p (h r t)")
                    nc.scalar.activation(w, w, ACT.Silu, scale=CS).then_inc(s_G, 1)

                def values_read(v, c):
                    n = v * 4 + c
                    ac.wait_ge(s_av, n + 1)
                    above(ac, s_oNp, n)
                    nc.scalar.copy(avT[:, :, :].rearrange("p q t -> p (q t)"), pb[:, 0:4 * T]).then_inc(s_avT, 1)

                def out_read(v, c, o):
                    g, n = c // 2, v * 4 + c
                    ac.wait_ge(s_oNp, n + 1)
                    if c % 2 == 0:
                        above(ac, s_nm, o * 2 + (g + 1))
                    nc.scalar.copy(oN[:, g, 2 * (c % 2):2 * (c % 2) + 2, :, :].rearrange("p r h c -> p (r h c)"),
                                   pb[0:T, :]).then_inc(s_oN, 1)

                def rstd(o):
                    ac.wait_ge(s_mv, o + 1)
                    above(ac, s_x, o)
                    nc.scalar.activation(rs[:, 0:1], mv[:, 1:2], ACT.Ln, bias=eps[:, 0:1]).then_inc(s_a3, 1)
                    ac.wait_ge(s_a3, o + 1)
                    nc.scalar.activation(rs[:, 1:2], rs[:, 0:1], ACT.Exp, scale=-0.5).then_inc(s_rs, 1)

                def body(o, par):
                    F, S, V, O = parts(o)
                    f, s, v = o + 3, o + 2, o + 1
                    vp = (par + 1) % 2
                    if V:
                        gate(v, vp, 0)
                        gate(v, vp, 1)
                    nc.scalar.preload_act_table_set("natural_log_exp_and_others")
                    if V:
                        values_read(v, 0)
                    if S:
                        exponential(s, par, 0)
                    if O:
                        rstd(o)
                    if S:
                        exponential(s, par, 1)
                    if V:
                        out_read(v, 0, o)
                    if S:
                        exponential(s, par, 2)
                    if V:
                        values_read(v, 1)
                    if F:
                        k_factors(f)
                    if V:
                        out_read(v, 1, o)
                    if S:
                        exponential(s, par, 3)
                        logarithm(s, par, 0)
                    if V:
                        values_read(v, 2)
                    if S:
                        exponential(s, par, 4)
                    if V:
                        out_read(v, 2, o)
                    if S:
                        exponential(s, par, 5)
                        exponential(s, par, 6)
                    if V:
                        values_read(v, 3)
                    if F:
                        qT_read(f)
                    if V:
                        out_read(v, 3, o)
                    if S:
                        exponential(s, par, 7)
                        logarithm(s, par, 1)

                ac.wait_ge(s_w, 16 * NW)
                nc.scalar.activation(sink[:], sink[:], ACT.Tanh).then_inc(s_c, 1)
                four_in_flight(ac, body)

            @block.gpsimd
            def _(po):
                def staged(f):
                    above(po, s_xTp, f)
                    nc.gpsimd.tensor_copy(xs[:], X[0:T, f, :]).then_inc(s_xs, 1)

                def q_roped(f):
                    po.wait_ge(s_qn, f + 1)
                    h = qn[:, :].rearrange("p (h c two) -> p h c two", two=2, c=DH // 2)
                    x1, x2 = h[:, :, :, 0], h[:, :, :, 1]
                    o = qr[:, :].rearrange("p (h c) -> p h c", c=DH)
                    c = cos[:, :].unsqueeze(1).broadcast_to([T, NBR * NH, DH // 2])
                    s = sin[:, :].unsqueeze(1).broadcast_to([T, NBR * NH, DH // 2])
                    A = qa[:, :].rearrange("p (h c) -> p h c", c=DH // 2)
                    B = qb[:, :].rearrange("p (h c) -> p h c", c=DH // 2)
                    b = f * 5
                    nc.gpsimd.tensor_tensor(A, x1, c, ALU.mult).then_inc(s_po, 1)
                    nc.gpsimd.tensor_tensor(B, x2, s, ALU.mult).then_inc(s_po, 1)
                    po.wait_ge(s_po, b + 2)
                    above(po, s_qTp, f)
                    nc.gpsimd.tensor_tensor(o[:, :, 0:DH // 2], A, B, ALU.subtract).then_inc(s_po, 1)
                    po.wait_ge(s_po, b + 3)
                    nc.gpsimd.tensor_tensor(A, x1, s, ALU.mult).then_inc(s_po, 1)
                    nc.gpsimd.tensor_tensor(B, x2, c, ALU.mult).then_inc(s_po, 1)
                    po.wait_ge(s_po, b + 5)
                    nc.gpsimd.tensor_tensor(o[:, :, DH // 2:DH], A, B, ALU.add).then_inc(s_qr, 1)

                def residual(o):
                    above(po, s_yr, o)
                    nc.gpsimd.tensor_tensor(xb[:], X[0:T, o, :], bo[:], ALU.add).then_inc(s_xb, 1)

                def body(o, par):
                    F, S, V, O = parts(o)
                    if O:
                        residual(o)
                    if F:
                        staged(o + 3)
                        q_roped(o + 3)

                po.wait_ge(s_w, 16 * NW)
                four_in_flight(po, body)


def turned(nc, st, names, d, ident):
    nat = [st.sb(f"{n}_nat", [P, KD, D]) for n in names]
    res = [st.sb(f"{n}_T", [P, KD, D]) for n in names]
    bank = Stage(nc, st.name + "t")
    s_l, s_p, s_r = st.sem("turn_loaded"), st.sem("turn_filled"), st.sem("turn_read")
    with bank, nc.Block() as block:
        pt = bank.ps("turn", [P, 512])

        @block.sync
        def _(sp):
            for n, t in zip(names, nat):
                sp.dma_start(t[:], rows(d[n])).then_inc(s_l, 16)

        @block.tensor
        def _(pe):
            pe.wait_ge(s_l, 16 * len(names))
            for w, t in enumerate(nat):
                above(pe, s_r, w)
                for k in range(KD):
                    for o in range(KD):
                        last = nc.tensor.transpose(pt[:, k * D + o * P:k * D + (o + 1) * P],
                                                   t[:, o, k * P:(k + 1) * P], ident[:, :])
                last.then_inc(s_p, 1)

        @block.scalar
        def _(ac):
            for w, r in enumerate(res):
                ac.wait_ge(s_p, w + 1)
                nc.scalar.copy(r[:, :, :].rearrange("p k n -> p (k n)"), pt[:, :]).then_inc(s_r, 1)
            ac.wait_ge(s_r, len(names))
    return res


def cross_attention(nc, X, ident, d):
    NC, KP_ = 3, 3 * P
    MP = NH // 2
    SCALE = DH ** -0.5
    keys = [P, P, SC - 2 * P]
    SLOTS = [["fx"], ["fc0", "fq"], ["fc1", "bo"], ["bp", "fv0"], ["fk0", "by"], ["fk1", "fv1"], [], []]
    NORM = 6
    st = Stage(nc, "ca")
    with st:
        sb, ps, sem = st.sb, st.ps, st.sem
        wqT, wkT, wvT, woT = turned(nc, st, ["L0_xattn_Wq", "L0_xattn_Wk", "L0_xattn_Wv", "L0_xattn_Wo"], d, ident)
        bq, bk = sb("bq", [P, KD]), sb("bk", [P, KD])
        bv, bo = sb("bv", [P, D]), sb("bo", [T, D])
        hmask = sb("hmask", [P, HG])
        qb = sb("qb", [P, KD, T])
        xs, xT = sb("xs", [T, D]), sb("xT", [P, KD, T])
        cn = sb("cn", [P, NC, D])
        cT = sb("cT", [P, KD, SC])
        kT = [sb(f"kT{b}", [P, KD, SC]) for b in range(2)]
        qTm = [sb(f"qTm{b}", [P, KD, HG, T]) for b in range(2)]
        va = [sb(f"va{b}", [P, NC, NH, 32]) for b in range(2)]
        nm = [sb(f"nm{b}", [T, 2]) for b in range(2)]
        pr = [sb(f"pr{b}", [T, 2, KP_]) for b in range(2)]
        pT = [sb(f"pT{b}", [P, 2, NC * T]) for b in range(2)]
        avT = sb("avT", [P, 4, T])
        rc = sb("rc", [T, NH])
        o, oT = sb("o", [T, D]), sb("oT", [P, KD, T])
        xb, y = [sb(f"xb{b}", [T, D]) for b in range(2)], sb("y", [T, D])
        stats, mv, rs, eps = sb("stats", [T, 6]), sb("mv", [T, 2]), sb("rs", [T, 2]), sb("eps", [T, 1])
        gap = sb("gap", [T, 1])
        pS = ps("pS", [P, 4, 512])
        pPT = ps("pPT", [P, 2, 512])
        pav = ps("pav", [P, 512])
        pf = ps("side", [P, 512])

        s_w, s_z = sem("weights_loaded"), sem("padding_zeroed")
        s_cn = sem("context_loaded")
        s_xs, s_qm = sem("xs_staged"), sem("q_masked")
        s_F, s_R = sem("side_filled"), sem("side_read")
        s_S, s_mx, s_P = sem("scores_in_psum"), sem("max_ready"), sem("exp_ready")
        s_PTp, s_PT, s_AV = sem("probsT_in_psum"), sem("probsT_ready"), sem("values_summed")
        s_av = sem("sums_read")
        s_xb, s_y, s_mv, s_ln, s_rs, s_x = (sem(n) for n in ("x_plus_bias", "y_ready", "ln_stats", "ln_log",
                                                             "ln_rstd", "x_done"))
        s_dv = sem("dve_chain")
        side = Side(SLOTS, s_F, s_R)
        NW = 5

        with nc.Block() as block:
            @block.sync
            def _(sp):
                for dst, src in ((bq[:], d["L0_xattn_bq"].rearrange("(k p) -> p k", p=P)),
                                 (bk[:], d["L0_xattn_bk"].rearrange("(k p) -> p k", p=P)),
                                 (bv[:], bcast(d["L0_xattn_bv"], P)), (bo[:], bcast(d["L0_xattn_bo"], T)),
                                 (hmask[:], d["c_hmask"])):
                    with nc.allow_non_contiguous_dma("a bias by partition"):
                        sp.dma_start(dst, src).then_inc(s_w, 16)

                def load(i):
                    if not isinstance(i, int) or i:
                        sp.wait_ge(s_R, side.read_of(i - 1, "fc1"))
                    sp.dma_start(cn[:, 0:2, :], d["ctx_1024"][i, 0:2 * P, :].rearrange("(c p) n -> p c n", p=P))\
                        .then_inc(s_cn, 16)
                    sp.dma_start(cn[0:keys[2], 2, :], d["ctx_1024"][i, 2 * P:SC, :]).then_inc(s_cn, 16)
                for i in range(3):
                    load(i)
                with sp.Fori(3, NB) as i:
                    load(i)

            @block.tensor
            def _(pe):
                def step(name, n, i, b):
                    if name == "fx":
                        pe.wait_ge(s_xs, i + 1)
                    if name == "fc0":
                        pe.wait_ge(s_cn, 32 * i + 32)
                    above(pe, s_R, n)
                    if name == "fx":
                        for k in range(KD):
                            last = nc.tensor.transpose(pf[:, k * T:(k + 1) * T], xs[:, k * P:(k + 1) * P],
                                                       ident[0:T, 0:T])
                    elif name in ("fc0", "fc1"):
                        k = int(name[-1])
                        for c in range(NC):
                            last = nc.tensor.transpose(pf[:, c * P:c * P + keys[c]],
                                                       cn[0:keys[c], c, k * P:(k + 1) * P],
                                                       ident[0:keys[c], 0:keys[c]])
                    elif name in ("fk0", "fk1"):
                        e = int(name[-1])
                        for k in range(KD):
                            last = nc.tensor.matmul(pf[:, 0:SC], wkT[:, k, e * P:(e + 1) * P], cT[:, k, :],
                                                    start=k == 0, stop=k == KD - 1)
                    elif name == "fq":
                        for e in range(KD):
                            for k in range(KD):
                                last = nc.tensor.matmul(pf[:, e * T:(e + 1) * T], wqT[:, k, e * P:(e + 1) * P],
                                                        xT[:, k, :], start=k == 0, stop=k == KD - 1)
                    elif name in ("fv0", "fv1"):
                        for c in ((0, 1) if name == "fv0" else (2,)):
                            for k in range(KD):
                                last = nc.tensor.matmul(pf[0:keys[c], (c % 2) * D:(c % 2 + 1) * D],
                                                        cT[:, k, c * P:c * P + keys[c]], wvT[:, k, :],
                                                        start=k == 0, stop=k == KD - 1)
                    elif name == "bo":
                        pe.wait_ge(s_av, i + 1)
                        for q in range(4):
                            last = nc.tensor.transpose(pf[0:T, q * P:(q + 1) * P], avT[:, q, :], ident[:, :])
                    elif name == "bp":
                        for k in range(KD):
                            last = nc.tensor.transpose(pf[:, k * T:(k + 1) * T], o[:, k * P:(k + 1) * P],
                                                       ident[0:T, 0:T])
                    elif name == "by":
                        for k in range(KD):
                            last = nc.tensor.matmul(pf[0:T, 0:D], oT[:, k, :], woT[:, k, :],
                                                    start=k == 0, stop=k == KD - 1)
                    last.then_inc(s_F, 1)

                def scores(i, b, m):
                    n = i * MP + m
                    if m == 0:
                        pe.wait_ge(s_R, side.front_done(i))
                        pe.wait_ge(s_qm, i + 1)
                    above(pe, s_P, n - 1)
                    for e in range(2):
                        h = 2 * m + e
                        last = nc.tensor.matmul(pS[0:T, 2 * (m % 2) + e, 0:SC], qTm[b][:, h // HG, h % HG, :],
                                                kT[b][:, h // HG, :], start=True, stop=True)
                    last.then_inc(s_S, 1)

                def turn(n, m):
                    pe.wait_ge(s_P, n + 1)
                    above(pe, s_PT, n)
                    for e in range(2):
                        for c in range(NC):
                            last = nc.tensor.transpose(pPT[:, e, c * T:(c + 1) * T],
                                                       pr[m % 2][:, e, c * P:(c + 1) * P], ident[0:T, 0:T])
                    last.then_inc(s_PTp, 1)

                def values(n, i, b, m):
                    pe.wait_ge(s_PT, n + 1)
                    if m == 0:
                        above(pe, s_av, i)
                    for e in range(2):
                        h = 2 * m + e
                        j = h % 4
                        for c in range(NC):
                            last = nc.tensor.matmul(pav[32 * j:32 * j + 32, (h // 4) * T:(h // 4 + 1) * T],
                                                    va[b][:, c, h, :], pT[m % 2][:, e, c * T:(c + 1) * T],
                                                    start=c == 0, stop=c == NC - 1)
                    last.then_inc(s_AV, 1)

                def turned_pair(i, b, m):
                    if m >= 1 or not (isinstance(i, int) and i == 0):
                        turn(i * MP + m - 1, (m - 1) % MP)

                def summed_pair(i, b, m):
                    if m >= 2:
                        values(i * MP + m - 2, i, b, m - 2)
                    elif not (isinstance(i, int) and i == 0):
                        values(i * MP + m - 2, i - 1, 1 - b, MP - 2 + m)

                def body(i, b):
                    for m in range(MP):
                        small = side.steps(i, m)
                        scores(i, b, m)
                        for part in (turned_pair, summed_pair, None):
                            if small:
                                name, n = small.pop(0)
                                step(name, n, i + 1 if name[0] == "f" else i - 1, 1 - b)
                            if part:
                                part(i, b, m)
                        assert not small

                pe.wait_ge(s_w, 16 * NW)
                pe.wait_ge(s_z, 1)
                for name, n in side.prologue():
                    step(name, n, 0, 0)
                over_batches(pe, body)
                n = NB * MP
                turn(n - 1, MP - 1)
                values(n - 2, NB - 1, 1, MP - 2)
                values(n - 1, NB - 1, 1, MP - 1)
                for name, k in side.epilogue():
                    step(name, k, NB - 1, 0)

            @block.vector
            def _(dv):
                ch = Chain(dv, s_dv, 0)
                SET = 9

                def step(name, n, i, b):
                    if name == "fx":
                        return
                    if name == "fq":
                        dv.wait_ge(s_F, n + 1)
                        above(dv, s_qm, i)
                        nc.vector.tensor_tensor(qb[:], pf[:, 0:KD * T].rearrange("p (k t) -> p k t", k=KD),
                                                bq[:, :].unsqueeze(2).broadcast_to([P, KD, T]), ALU.add)\
                            .then_inc(s_R, 1)
                    elif name in ("fv0", "fv1"):
                        dv.wait_ge(s_F, n + 1)
                        for c in ((0, 1) if name == "fv0" else (2,)):
                            ins = nc.vector.tensor_tensor(
                                va[b][0:keys[c], c, :, 0:DH],
                                pf[0:keys[c], (c % 2) * D:(c % 2 + 1) * D].rearrange("p (h c) -> p h c", c=DH),
                                bv[0:keys[c], :].rearrange("p (h c) -> p h c", c=DH), ALU.add)
                        ins.then_inc(s_R, 1)
                    elif name == "bo":
                        dv.wait_ge(s_F, n + 1)
                        o4 = pf[0:T, :].rearrange("p (h c) -> p h c", c=32)
                        nc.vector.reciprocal(rc[:], o4[:, :, DH]).then_inc(s_dv, 1)
                        dv.wait_ge(s_dv, SET + 2 * i + 1)
                        nc.vector.tensor_tensor(o[:, :].rearrange("p (h c) -> p h c", c=DH), o4[:, :, 0:DH],
                                                rc[:, :].unsqueeze(2).broadcast_to([T, NH, DH]), ALU.mult)\
                            .then_inc(s_R, 1)
                    elif name == "by":
                        dv.wait_ge(s_F, n + 1)
                        dv.wait_ge(s_xb, i + 1)
                        nc.vector.tensor_tensor(y[:], pf[0:T, 0:D], xb[b][:], ALU.add).then_inc(s_R, 1)
                        dv.wait_ge(s_R, n + 1)
                        nc.vector.bn_stats(stats[:], y[:]).then_inc(s_dv, 1)
                        dv.wait_ge(s_dv, SET + 2 * i + 2)
                        nc.vector.memset(gap[:], 0.0)
                        nc.vector.bn_aggr(mv[:], stats[:]).then_inc(s_mv, 1)

                def normed(i):
                    dv.wait_ge(s_rs, i + 1)
                    nc.vector.tensor_scalar(X[0:T, i, :], y[:], mv[:, 0:1], rs[:, 1:2], ALU.subtract, ALU.mult)\
                        .then_inc(s_x, 1)

                def maxima(i, m):
                    n = i * MP + m
                    dv.wait_ge(s_S, n + 1)
                    above(dv, s_P, n - 1)
                    nc.vector.reduce_max(nm[m % 2][:], pS[0:T, 2 * (m % 2):2 * (m % 2) + 2, 0:SC], AX)\
                        .then_inc(s_mx, 1)
                    dv.wait_ge(s_mx, 2 * n + 1)
                    nc.vector.tensor_scalar(nm[m % 2][:], nm[m % 2][:], -SCALE, None, ALU.mult).then_inc(s_mx, 1)

                def evac(n, m):
                    dv.wait_ge(s_PTp, n + 1)
                    above(dv, s_AV, n - 1)
                    nc.vector.tensor_copy(pT[m % 2][:], pPT[:, :, 0:NC * T]).then_inc(s_PT, 1)

                def body(i, b):
                    for m in range(MP):
                        small = side.steps(i, m)
                        maxima(i, m)
                        for turn in (False, True, False):
                            if small:
                                name, n = small.pop(0)
                                step(name, n, i + 1 if name[0] == "f" else i - 1, 1 - b)
                            if turn and (m or not (isinstance(i, int) and i == 0)):
                                evac(i * MP + m - 1, (m - 1) % MP)
                        if m == NORM and not (isinstance(i, int) and i == 0):
                            normed(i - 1)

                ch.base, ch.n = 0, 0
                for b in range(2):
                    ch.after(nc.vector.memset(va[b][:], 0.0))
                    ch.after(nc.vector.memset(va[b][:, 0:2, :, DH:DH + 1], 1.0))
                    ch.after(nc.vector.memset(va[b][0:keys[2], 2, :, DH:DH + 1], 1.0))
                    ch.after(nc.vector.memset(pr[b][:], 0.0))
                ch.after(nc.vector.memset(eps[:], EPS))
                assert ch.n == SET
                nc.vector.memset(rc[:], 0.0).then_inc(s_z, 1)
                dv.wait_ge(s_z, 1)
                dv.wait_ge(s_w, 16 * NW)
                for name, n in side.prologue():
                    step(name, n, 0, 0)
                over_batches(dv, body)
                evac(NB * MP - 1, MP - 1)
                for name, n in side.epilogue():
                    step(name, n, NB - 1, 1)
                normed(NB - 1)

            @block.scalar
            def _(ac):
                def step(name, n, i, b):
                    if name in ("fx", "bp"):
                        ac.wait_ge(s_F, n + 1)
                        dst = xT if name == "fx" else oT
                        nc.scalar.copy(dst[:, :, :].rearrange("p k t -> p (k t)"), pf[:, 0:KD * T]).then_inc(s_R, 1)
                    elif name in ("fc0", "fc1"):
                        ac.wait_ge(s_F, n + 1)
                        nc.scalar.copy(cT[:, int(name[-1]), :], pf[:, 0:SC]).then_inc(s_R, 1)
                    elif name in ("fk0", "fk1"):
                        e = int(name[-1])
                        ac.wait_ge(s_F, n + 1)
                        nc.scalar.activation(kT[b][:, e, :], pf[:, 0:SC], ACT.Identity, bias=bk[:, e:e + 1])\
                            .then_inc(s_R, 1)

                def rstd(i):
                    ac.wait_ge(s_mv, i + 1)
                    nc.scalar.activation(rs[:, 0:1], mv[:, 1:2], ACT.Ln, bias=eps[:, 0:1]).then_inc(s_ln, 1)
                    ac.wait_ge(s_ln, i + 1)
                    nc.scalar.activation(rs[:, 1:2], rs[:, 0:1], ACT.Exp, scale=-0.5).then_inc(s_rs, 1)

                def exps(i, m):
                    n = i * MP + m
                    ac.wait_ge(s_mx, 2 * n + 2)
                    above(ac, s_PTp, n - 1)
                    for e in range(2):
                        ins = nc.scalar.activation(pr[m % 2][:, e, 0:SC], pS[0:T, 2 * (m % 2) + e, 0:SC], ACT.Exp,
                                                   bias=nm[m % 2][:, e:e + 1], scale=SCALE)
                    ins.then_inc(s_P, 1)

                def sums(i):
                    ac.wait_ge(s_AV, i * MP + MP)
                    nc.scalar.copy(avT[:, :, :].rearrange("p q t -> p (q t)"), pav[:, 0:4 * T]).then_inc(s_av, 1)

                def body(i, b):
                    for m in range(MP):
                        behind = not (isinstance(i, int) and i == 0)
                        small = side.steps(i, m)
                        for name, n in small[:1]:
                            step(name, n, i + 1 if name[0] == "f" else i - 1, 1 - b)
                        if m == 2 and behind:
                            sums(i - 1)
                        exps(i, m)
                        if m == NORM and behind:
                            rstd(i - 1)
                        for name, n in small[1:]:
                            step(name, n, i + 1 if name[0] == "f" else i - 1, 1 - b)

                ac.wait_ge(s_w, 16 * NW)
                ac.wait_ge(s_z, 1)
                nc.scalar.preload_act_table_set("natural_log_exp_and_others")
                for name, n in side.prologue():
                    step(name, n, 0, 0)
                over_batches(ac, body)
                sums(NB - 1)
                for name, n in side.epilogue():
                    step(name, n, NB - 1, 1)
                rstd(NB - 1)

            @block.gpsimd
            def _(po):
                def stage(i):
                    if not isinstance(i, int) or i:
                        po.wait_ge(s_R, side.read_of(i - 1, "fx"))
                    nc.gpsimd.tensor_copy(xs[:], X[0:T, i, :]).then_inc(s_xs, 1)

                def residual(i, b):
                    nc.gpsimd.tensor_tensor(xb[b][:], X[0:T, i, :], bo[:], ALU.add).then_inc(s_xb, 1)

                def q_masked(i, b):
                    po.wait_ge(s_R, side.read_of(i, "fq"))
                    if not isinstance(i, int) or i > 1:
                        po.wait_ge(s_S, (i - 1) * MP)
                    for e in range(KD):
                        ins = nc.gpsimd.tensor_tensor(
                            qTm[b][:, e, :, :], qb[:, e, :].unsqueeze(1).broadcast_to([P, HG, T]),
                            hmask[:, :].unsqueeze(2).broadcast_to([P, HG, T]), ALU.mult)
                    ins.then_inc(s_qm, 1)

                def ahead(i, b):
                    stage(i)
                    q_masked(i, b)

                po.wait_ge(s_w, 16 * NW)
                ahead(0, 0)
                ahead(1, 1)
                residual(0, 0)
                ahead(2, 0)
                residual(1, 1)
                ahead(3, 1)
                residual(2, 0)
                with po.Fori(0, (NB - 4) // 2) as j:
                    ahead(2 * j + 4, 0)
                    residual(2 * j + 3, 1)
                    ahead(2 * j + 5, 1)
                    residual(2 * j + 4, 0)
                po.wait_ge(s_x, NB - 2)
                residual(NB - 1, 1)


def expert_adapter(nc, X, ident, d):
    E, R = 8, 64
    st = Stage(nc, "ea")
    with st:
        sb, ps, sem = st.sb, st.ps, st.sem
        wb, wbT = sb("wb", [P, KD, D]), sb("wbT", [P, KD, D])
        wc, wcT = sb("wc", [P, E, KD, D]), sb("wcT", [P, E, KD, D])
        wd, wu = sb("wd", [P, E, KD, R]), sb("wu", [P, E, D])
        bd, bu, bc = sb("bd", [T, E, R]), sb("bu", [T, E, D]), sb("bc", [T, E, D])
        bb = sb("bb", [T, D])
        sel = sb("sel", [T, NB, NB])
        xsq = sb("xsq", [T, NB, D])
        mu, sg = sb("mu", [E, D]), sb("sg", [E, D])
        tab = sb("tab", [E, 3, D])
        tabT = sb("tabT", [P, 3 * KD, E])
        mom, momT = sb("mom", [NB, 2 * D]), sb("momT", [P, 2 * KD, NB])
        ones = sb("ones", [P, NB])
        nl, top = sb("nl", [NB, E]), sb("top", [NB, E])
        ix, ixr = sb("ix", [NB, E], U32), sb("ixr", [1, NB], U32)
        xs = [sb(f"xs{l}", [T, D]) for l in range(2)]
        xT = [sb(f"xT{l}", [P, KD, T]) for l in range(2)]
        hn = [sb(f"hn{l}", [T, P]) for l in range(2)]
        hT = [sb(f"hT{l}", [P, T]) for l in range(2)]
        an = [sb(f"an{l}", [T, D]) for l in range(2)]
        aT = [sb(f"aT{l}", [P, KD, T]) for l in range(2)]
        y0 = [sb(f"y0{l}", [T, D]) for l in range(2)]
        y = [sb(f"y{l}", [T, D]) for l in range(2)]
        stats = [sb(f"stats{l}", [T, 6]) for l in range(2)]
        mv = [sb(f"mv{l}", [T, 2]) for l in range(2)]
        rs = [sb(f"rs{l}", [T, 2]) for l in range(2)]
        eps = sb("eps", [T, 1])
        gap = sb("gap", [T, 1])
        pt = [ps(f"pt{l}", [P, 512]) for l in range(2)]
        pm, pl = ps("pm", [P, 512]), ps("pl", [P, 512])

        s_rt = sem("routing_loaded")
        s_w, s_t, s_tr = sem("weights_loaded"), sem("turn_filled"), sem("turn_read")
        s_sq, s_tab, s_tabT, s_tabTr = sem("squares_ready"), sem("tables_ready"), sem("tablesT_in_psum"), sem("tablesT_read")
        s_m, s_mr, s_mT, s_mTr = sem("moments_in_psum"), sem("moments_read"), sem("momentsT_in_psum"), sem("momentsT_read")
        s_l, s_ix, s_ixr, s_dv = sem("losses_in_psum"), sem("indices_ready"), sem("indices_in_a_row"), sem("setup_chain")
        with nc.Block() as block:
            @block.sync
            def _(sp):
                for dst, src in ((sel[:], d["c_sel"]), (mu[:], d["L0_ffn_disc_mu"]), (sg[:], d["L0_ffn_disc_sigma"])):
                    sp.dma_start(dst, src).then_inc(s_rt, 16)
                for dst, src in ((wc[:], d["L0_ffn_conv_W"].rearrange("e (k p) n -> p e k n", p=P)),
                                 (wb[:], rows(d["L0_ffn_base_W"])),
                                 (wd[:], d["L0_ffn_down_W"].rearrange("e (k p) n -> p e k n", p=P)),
                                 (wu[0:R], d["L0_ffn_up_W"].rearrange("e r n -> r e n")),
                                 (bd[:], bcast(d["L0_ffn_down_b"].rearrange("e r -> (e r)"), T)),
                                 (bu[:], bcast(d["L0_ffn_up_b"].rearrange("e r -> (e r)"), T)),
                                 (bc[:], bcast(d["L0_ffn_conv_b"].rearrange("e r -> (e r)"), T)),
                                 (bb[:], bcast(d["L0_ffn_base_b"], T))):
                    v = dst if len(dst.shape) == len(src.shape) else dst.rearrange("p e r -> p (e r)")
                    sp.dma_start(v, src).then_inc(s_w, 16)
                sp.wait_ge(s_w, 16 * 8)
                sp.wait_ge(s_ix, 1)
                with nc.allow_non_contiguous_dma("16 indices to one row"):
                    sp.dma_start(ixr[:], ix[:, 0:1]).then_inc(s_ixr, 16)
                sp.wait_ge(s_ixr, 16)

            @block.tensor
            def _(pe):
                pe.wait_ge(s_rt, 16 * 3)
                for part, src in ((0, X), (1, xsq)):
                    if part:
                        pe.wait_ge(s_sq, 1)
                    for b in range(NB):
                        last = nc.tensor.matmul(pm[0:NB, part * D:(part + 1) * D], sel[:, b, :], src[0:T, b, :],
                                                start=b == 0, stop=b == NB - 1)
                last.then_inc(s_m, 1)
                pe.wait_ge(s_tab, 1)
                for j in range(3):
                    for k in range(KD):
                        last = nc.tensor.transpose(pl[:, (j * KD + k) * E:(j * KD + k + 1) * E],
                                                   tab[:, j, k * P:(k + 1) * P], ident[0:E, 0:E])
                last.then_inc(s_tabT, 1)
                pe.wait_ge(s_mr, 1)
                for k in range(2 * KD):
                    last = nc.tensor.transpose(pm[:, k * NB:(k + 1) * NB], mom[:, k * P:(k + 1) * P],
                                               ident[0:NB, 0:NB])
                last.then_inc(s_mT, 1)
                pe.wait_ge(s_mTr, 1)
                pe.wait_ge(s_tabTr, 1)
                n = 0
                for j, lhs in ((0, 1), (1, 0), (2, None)):
                    for k in range(KD):
                        a = ones[:, :] if lhs is None else momT[:, lhs * KD + k, :]
                        last = nc.tensor.matmul(pl[0:NB, 256:256 + E], a, tabT[:, j * KD + k, :],
                                                start=n == 0, stop=n == 3 * KD - 1)
                        n += 1
                last.then_inc(s_l, 1)
                pe.wait_ge(s_w, 16 * 8)
                for w in range(E + 1):
                    above(pe, s_tr, w - 1)
                    src = wb if w == E else wc[:, w]
                    for k in range(KD):
                        for o in range(KD):
                            last = nc.tensor.transpose(pt[w % 2][:, k * D + o * P:k * D + (o + 1) * P],
                                                       src[:, o, k * P:(k + 1) * P], ident[:, :])
                    last.then_inc(s_t, 1)

            @block.scalar
            def _(ac):
                for w in range(E + 1):
                    ac.wait_ge(s_t, w + 1)
                    dst = wbT[:, :, :] if w == E else wcT[:, w, :, :]
                    nc.scalar.copy(dst.rearrange("p k n -> p (k n)"), pt[w % 2][:, :]).then_inc(s_tr, 1)
                ac.wait_ge(s_tr, E + 1)

            @block.vector
            def _(dv):
                ch = Chain(dv, s_dv, 0)
                ch.base, ch.n = 0, 0
                nc.vector.tensor_tensor(xsq[:], X[0:T, :, :], X[0:T, :, :], ALU.mult).then_inc(s_sq, 1)
                nc.vector.memset(eps[:], EPS)
                nc.vector.memset(ones[:], 1.0)
                for l in range(2):
                    nc.vector.memset(hn[l][:, R:P], 0.0)
                dv.wait_ge(s_rt, 16 * 3)
                ch.after(nc.vector.tensor_tensor(sg[:], sg[:], sg[:], ALU.mult))
                ch.after(nc.vector.reciprocal(tab[:, 0, :], sg[:]))
                ch.after(nc.vector.tensor_tensor(sg[:], mu[:], tab[:, 0, :], ALU.mult))
                ch.after(nc.vector.tensor_scalar(tab[:, 1, :], sg[:], -2.0, None, ALU.mult))
                nc.vector.tensor_tensor(tab[:, 2, :], mu[:], sg[:], ALU.mult).then_inc(s_tab, 1)
                dv.wait_ge(s_m, 1)
                nc.vector.tensor_scalar(mom[:], pm[0:NB, :], 1.0 / T, None, ALU.mult).then_inc(s_mr, 1)
                dv.wait_ge(s_tabT, 1)
                nc.vector.tensor_copy(tabT[:, :, :].rearrange("p j e -> p (j e)"), pl[:, 0:3 * KD * E])\
                    .then_inc(s_tabTr, 1)
                dv.wait_ge(s_mT, 1)
                nc.vector.tensor_copy(momT[:, :, :].rearrange("p j e -> p (j e)"), pm[:, 0:2 * KD * NB])\
                    .then_inc(s_mTr, 1)
                dv.wait_ge(s_w, 16 * 8)
                ch.after(nc.vector.tensor_tensor(bc[:], bc[:], bb[:, :].unsqueeze(1).broadcast_to([T, E, D]), ALU.add))
                dv.wait_ge(s_l, 1)
                ch.after(nc.vector.tensor_scalar(nl[:], pl[0:NB, 256:256 + E], -1.0, None, ALU.mult))
                ch.after(nc.vector.max(top[:], nl[:]))
                nc.vector.max_index(ix[:], top[:], nl[:]).then_inc(s_ix, 1)
                dv.wait_ge(s_ix, 1)

        pc = [ps(f"pc{l}", [P, 512]) for l in range(2)]

        def over_pairs(eng, body):
            body(-1)
            with eng.Fori(0, NB // 2 - 1) as t:
                body(t)
            body(NB // 2 - 1)

        def parts(t):
            return [not isinstance(t, int) or t < NB // 2 - 1, not isinstance(t, int) or t >= 0]

        s_xs = [sem(f"xs_staged{l}") for l in range(2)]
        s_F = [sem(f"step_filled{l}") for l in range(2)]
        s_R = [sem(f"step_read{l}") for l in range(2)]
        s_ch = [sem(f"ln_chain{l}") for l in range(2)]
        s_mv, s_ln, s_rs, s_x = ([sem(f"{n}{l}") for l in range(2)] for n in ("ln_stats", "ln_log", "ln_rstd", "x_done"))
        NS = 6
        with nc.Block() as block:
            @block.gpsimd
            def _(po):
                def body(t):
                    if parts(t)[0]:
                        for l in range(2):
                            above(po, s_F[l], NS * t + 1)
                            nc.gpsimd.tensor_copy(xs[l][:], X[0:T, 2 * t + (l + 2), :]).then_inc(s_xs[l], 1)
                over_pairs(po, body)

            @block.tensor
            def _(pe):
                def body(t):
                    if not parts(t)[0]:
                        return
                    e = [pe.value_load(ixr[0:1, bass.ds(2 * t + (l + 2), 1)], min_val=0, max_val=E - 1)
                         for l in range(2)]
                    for s in range(NS):
                        for l in range(2):
                            if s == 0:
                                pe.wait_ge(s_xs[l], t + 2)
                            above(pe, s_R[l], NS * t + (NS + s))
                            if s == 0:
                                for k in range(KD):
                                    last = nc.tensor.transpose(pt[l][:, k * T:(k + 1) * T], xs[l][:, k * P:(k + 1) * P],
                                                               ident[0:T, 0:T])
                            elif s == 1:
                                for k in range(KD):
                                    last = nc.tensor.matmul(pt[l][0:T, 256:256 + R], xT[l][:, k, :], wd[:, e[l], k, :],
                                                            start=k == 0, stop=k == KD - 1)
                            elif s == 2:
                                last = nc.tensor.transpose(pt[l][:, 384:384 + T], hn[l][:, :], ident[0:T, 0:T])
                            elif s == 3:
                                last = nc.tensor.matmul(pt[l][0:T, 0:D], hT[l][0:R, :], wu[0:R, e[l], :],
                                                        start=True, stop=True)
                            elif s == 4:
                                for k in range(KD):
                                    last = nc.tensor.transpose(pt[l][:, 256 + k * T:256 + (k + 1) * T],
                                                               an[l][:, k * P:(k + 1) * P], ident[0:T, 0:T])
                            else:
                                for k in range(KD):
                                    last = nc.tensor.matmul(pc[l][0:T, 0:D], aT[l][:, k, :], wcT[:, e[l], k, :],
                                                            start=False, stop=k == KD - 1)
                            last.then_inc(s_F[l], 1)
                        if s in (1, 3):
                            for k in range(KD):
                                nc.tensor.matmul(pc[s // 2][0:T, 0:D], xT[s // 2][:, k, :], wbT[:, k, :],
                                                 start=k == 0, stop=False)
                over_pairs(pe, body)

            @block.scalar
            def _(ac):
                def body(t):
                    front, tail = parts(t)
                    for s in (0, 2, 4):
                        for l in range(2):
                            if not front:
                                continue
                            ac.wait_ge(s_F[l], NS * t + (NS + s + 1))
                            if s == 2:
                                nc.scalar.activation(hT[l][0:R, :], pt[l][0:R, 384:384 + T], ACT.Relu)\
                                    .then_inc(s_R[l], 1)
                            else:
                                o, dst = (0, xT[l]) if s == 0 else (256, aT[l])
                                nc.scalar.copy(dst[:, :, :].rearrange("p k t -> p (k t)"),
                                               pt[l][:, o:o + KD * T]).then_inc(s_R[l], 1)
                        for l in range(2):
                            if s == 0 and tail:
                                ac.wait_ge(s_mv[l], t + 1)
                                nc.scalar.activation(rs[l][:, 0:1], mv[l][:, 1:2], ACT.Ln, bias=eps[:, 0:1])\
                                    .then_inc(s_ln[l], 1)
                                ac.wait_ge(s_ln[l], t + 1)
                                nc.scalar.activation(rs[l][:, 1:2], rs[l][:, 0:1], ACT.Exp, scale=-0.5)\
                                    .then_inc(s_rs[l], 1)

                nc.scalar.preload_act_table_set("natural_log_exp_and_others")
                over_pairs(ac, body)

            @block.vector
            def _(dv):
                def body(t):
                    front, tail = parts(t)
                    if front:
                        e = [dv.value_load(ixr[0:1, bass.ds(2 * t + (l + 2), 1)], min_val=0, max_val=E - 1)
                             for l in range(2)]
                        for l in range(2):
                            dv.wait_ge(s_F[l], NS * t + (NS + 2))
                            nc.vector.tensor_tensor(hn[l][:, 0:R], pt[l][0:T, 256:256 + R], bd[:, e[l], :], ALU.add)\
                                .then_inc(s_R[l], 1)
                    if tail:
                        for l in range(2):
                            dv.wait_ge(s_rs[l], t + 1)
                            nc.vector.tensor_scalar(X[0:T, 2 * t + l, :], y[l][:], mv[l][:, 0:1], rs[l][:, 1:2],
                                                    ALU.subtract, ALU.mult).then_inc(s_x[l], 1)
                    if not front:
                        return
                    for l in range(2):
                        dv.wait_ge(s_F[l], NS * t + (NS + 4))
                        nc.vector.tensor_tensor(an[l][:], pt[l][0:T, 0:D], bu[:, e[l], :], ALU.add).then_inc(s_R[l], 1)
                    for l in range(2):
                        dv.wait_ge(s_F[l], NS * t + (NS + 6))
                        nc.vector.tensor_tensor(y0[l][:], pc[l][0:T, 0:D], bc[:, e[l], :], ALU.add).then_inc(s_R[l], 1)
                        dv.wait_ge(s_R[l], NS * t + (NS + 6))
                        nc.vector.tensor_tensor(y[l][:], y0[l][:], X[0:T, 2 * t + (l + 2), :], ALU.add)\
                            .then_inc(s_ch[l], 1)
                        dv.wait_ge(s_ch[l], 2 * t + 3)
                        nc.vector.bn_stats(stats[l][:], y[l][:]).then_inc(s_ch[l], 1)
                        dv.wait_ge(s_ch[l], 2 * t + 4)
                        nc.vector.memset(gap[:], 0.0)
                        nc.vector.bn_aggr(mv[l][:], stats[l][:]).then_inc(s_mv[l], 1)
                over_pairs(dv, body)


def bucket_attention(nc, X, ident, d):
    NQ, HQ, NHP = 4, 4, 6
    NBK = 2 ** NHP
    SCALE = D ** -0.5
    SLOTS = [["fx", "fq"], ["fh"], [], ["fv", "bo"]]
    st = Stage(nc, "ba")
    with st:
        sb, ps, sem = st.sb, st.ps, st.sem
        wqT, wvT = turned(nc, st, ["L1_attn_Wq", "L1_attn_Wv"], d, ident)
        bq, bv = sb("bq", [P, KD]), sb("bv", [T, D])
        hmask = sb("hmask", [P, HG])
        hyp, hb = sb("hyp", [P, HG * NHP]), sb("hb", [T, NHP])
        pw = sb("pw", [T, NH * NHP])
        xs, xT = sb("xs", [T, D]), sb("xT", [P, KD, T])
        qT = [sb(f"qT{b}", [P, KD, T]) for b in range(2)]
        qTm = [sb(f"qTm{b}", [P, KD, HG, T]) for b in range(2)]
        va = [sb(f"va{b}", [T, NH, 32]) for b in range(2)]
        pj, bk = sb("pj", [T, NH * NHP]), [sb(f"bk{b}", [T, NH]) for b in range(2)]
        dg = [sb(f"dg{b}", [T, NH, T], BF16) for b in range(2)]
        ones = sb("ones", [T, P], BF16)
        same = sb("same", [T, HQ, T])
        A = [sb(f"A{b}", [T, HQ, T]) for b in range(NQ)]
        mx = [sb(f"mx{b}", [T, HQ]) for b in range(NQ)]
        pr = [sb(f"pr{b}", [T, HQ, T]) for b in range(NQ)]
        pT = [sb(f"pT{b}", [T, HQ * T]) for b in range(2)]
        avT = sb("avT", [P, NQ, T])
        rc, o, y = sb("rc", [T, NH]), sb("o", [T, D]), sb("y", [T, D])
        stats, mv, rs, eps = sb("stats", [T, 6]), sb("mv", [T, 2]), sb("rs", [T, 2]), sb("eps", [T, 1])
        gap = sb("gap", [T, 1])
        pS = [ps(f"pS{b}", [P, 512]) for b in range(2)]
        pB = [ps(f"pB{b}", [P, 512]) for b in range(2)]
        pPT = [ps(f"pPT{b}", [P, 512]) for b in range(2)]
        pav, pf = ps("pav", [P, 512]), ps("side", [P, 512])

        s_w, s_z, s_z1 = sem("weights_loaded"), sem("padding_zeroed"), sem("hyperplanes_zeroed")
        s_xs, s_F, s_R = sem("xs_staged"), sem("side_filled"), sem("side_read")
        s_qm, s_dg = sem("masked_q_ready"), sem("diagonals_ready")
        s_S, s_mx, s_A, s_P = sem("scores_in_psum"), sem("max_ready"), sem("shift_ready"), sem("exp_ready")
        s_PTp, s_PT, s_AV, s_av = (sem(n) for n in ("probsT_in_psum", "probsT_ready", "values_summed", "sums_read"))
        s_mv, s_ln, s_rs, s_x = (sem(n) for n in ("ln_stats", "ln_log", "ln_rstd", "x_done"))
        s_dv, s_dq, s_df, s_pl = sem("setup_chain"), sem("quad_chain"), sem("step_chain"), sem("pool_chain")
        side = Side(SLOTS, s_F, s_R)
        NW = 5 + HG

        with nc.Block() as block:
            @block.sync
            def _(sp):
                with nc.allow_non_contiguous_dma("small constants"):
                    for dst, src in ((bq[:], d["L1_attn_bq"].rearrange("(k p) -> p k", p=P)),
                                     (bv[:], bcast(d["L1_attn_bv"], T)), (hmask[:], d["c_hmask"]),
                                     (pw[:], d["c_pow2"]),
                                     (hb[:], d["L1_attn_hyperplanes"][DH:DH + 1, :].broadcast_to([T, NHP]))):
                        sp.dma_start(dst, src).then_inc(s_w, 16)
                    sp.wait_ge(s_z1, 1)
                    for h in range(HG):
                        sp.dma_start(hyp[h * DH:(h + 1) * DH, h * NHP:(h + 1) * NHP],
                                     d["L1_attn_hyperplanes"][0:DH, :]).then_inc(s_w, 16)

            @block.tensor
            def _(pe):
                def step(name, n, i, b):
                    if name == "fx":
                        pe.wait_ge(s_xs, i + 1)
                    if name == "bo":
                        pe.wait_ge(s_av, i + 1)
                    above(pe, s_R, n)
                    if name == "fx":
                        for k in range(KD):
                            last = nc.tensor.transpose(pf[:, k * T:(k + 1) * T], xs[:, k * P:(k + 1) * P],
                                                       ident[0:T, 0:T])
                    elif name == "fq":
                        for e in range(KD):
                            for k in range(KD):
                                last = nc.tensor.matmul(pf[:, e * T:(e + 1) * T], wqT[:, k, e * P:(e + 1) * P],
                                                        xT[:, k, :], start=k == 0, stop=k == KD - 1)
                    elif name == "fh":
                        W = HG * NHP
                        for e in range(KD):
                            last = nc.tensor.matmul(pf[0:T, e * W:(e + 1) * W], qT[b][:, e, :], hyp[:, :],
                                                    start=True, stop=True)
                    elif name == "fv":
                        for k in range(KD):
                            last = nc.tensor.matmul(pf[0:T, 0:D], xT[:, k, :], wvT[:, k, :],
                                                    start=k == 0, stop=k == KD - 1)
                    else:
                        for q in range(NQ):
                            last = nc.tensor.transpose(pf[0:T, q * P:(q + 1) * P], avT[:, q, :], ident[:, :])
                    last.then_inc(s_F, 1)

                def scores(i, b, m):
                    n = i * NQ + m
                    if m == 0:
                        pe.wait_ge(s_R, side.front_done(i))
                        pe.wait_ge(s_qm, i + 1)
                        pe.wait_ge(s_dg, i + 1)
                    above(pe, s_mx, 2 * (n - 1))
                    h = HQ * m
                    nc.tensor.matmul(pB[m % 2][:, 0:HQ * T], ones[:, :], dg[b][:, h:h + HQ, :], start=True, stop=True)
                    nc.tensor.matmul(pS[m % 2][0:T, 0:HQ * T], qT[b][:, h // HG, :],
                                     qTm[b][:, h // HG, h % HG:h % HG + HQ, :], start=True, stop=True)\
                        .then_inc(s_S, 1)

                def turn(n, m):
                    pe.wait_ge(s_P, n + 1)
                    above(pe, s_PT, n - 1)
                    for e in range(HQ):
                        last = nc.tensor.transpose(pPT[m % 2][0:T, e * T:(e + 1) * T], pr[m][:, e, :],
                                                   ident[0:T, 0:T])
                    last.then_inc(s_PTp, 1)

                def values(n, i, b, m):
                    pe.wait_ge(s_PT, n + 1)
                    if m == 0:
                        above(pe, s_av, i)
                    for j in range(HQ):
                        last = nc.tensor.matmul(pav[32 * j:32 * j + 32, m * T:(m + 1) * T], va[b][:, HQ * m + j, :],
                                                pT[m % 2][:, j * T:(j + 1) * T], start=True, stop=True)
                    last.then_inc(s_AV, 1)

                def body(i, b):
                    first = isinstance(i, int) and i == 0
                    for m in range(NQ):
                        n = i * NQ + m
                        scores(i, b, m)
                        small = side.steps(i, m)
                        for name, k in small[:1]:
                            step(name, k, i + 1 if name[0] == "f" else i - 1, 1 - b)
                        if m >= 2 or not first:
                            turn(n - 2, (m - 2) % NQ)
                        for name, k in small[1:]:
                            step(name, k, i + 1 if name[0] == "f" else i - 1, 1 - b)
                        if m >= 3:
                            values(n - 3, i, b, m - 3)
                        elif not first:
                            values(n - 3, i - 1, 1 - b, NQ - 3 + m)

                pe.wait_ge(s_w, 16 * NW)
                pe.wait_ge(s_z, 1)
                for name, n in side.prologue():
                    step(name, n, 0, 0)
                over_batches(pe, body)
                n = NB * NQ
                turn(n - 2, NQ - 2)
                values(n - 3, NB - 1, 1, NQ - 3)
                turn(n - 1, NQ - 1)
                values(n - 2, NB - 1, 1, NQ - 2)
                values(n - 1, NB - 1, 1, NQ - 1)
                for name, k in side.epilogue():
                    step(name, k, NB - 1, 0)

            @block.vector
            def _(dv):
                SET = 6

                def step(name, n, i, b):
                    if name == "fq":
                        dv.wait_ge(s_F, n + 1)
                        for e in range(KD):
                            ins = nc.vector.tensor_scalar(qT[b][:, e, :], pf[:, e * T:(e + 1) * T], bq[:, e:e + 1],
                                                          None, ALU.add)
                        ins.then_inc(s_R, 1)
                    elif name == "fh":
                        dv.wait_ge(s_F, n + 1)
                        p3 = pj[:, :].rearrange("p (h n) -> p h n", n=NHP)
                        nc.vector.tensor_tensor(p3, pf[0:T, 0:NH * NHP].rearrange("p (h n) -> p h n", n=NHP),
                                                hb[:, :].unsqueeze(1).broadcast_to([T, NH, NHP]), ALU.add)\
                            .then_inc(s_df, 1)
                        dv.wait_ge(s_df, 2 * i + 1)
                        nc.vector.scalar_tensor_tensor(out=pj[:], in0=pj[:], scalar=0.0, in1=pw[:], op0=ALU.is_ge,
                                                       op1=ALU.mult).then_inc(s_df, 1)
                        dv.wait_ge(s_df, 2 * i + 2)
                        nc.vector.reduce_sum(bk[b][:], p3, AX).then_inc(s_R, 1)
                    elif name == "fv":
                        dv.wait_ge(s_F, n + 1)
                        nc.vector.tensor_tensor(va[b][:, :, 0:DH], pf[0:T, 0:D].rearrange("p (h c) -> p h c", c=DH),
                                                bv[:, :].rearrange("p (h c) -> p h c", c=DH), ALU.add).then_inc(s_R, 1)
                    elif name == "bo":
                        dv.wait_ge(s_F, n + 1)
                        o4 = pf[0:T, :].rearrange("p (h c) -> p h c", c=32)
                        nc.vector.reciprocal(rc[:], o4[:, :, DH]).then_inc(s_dv, 1)
                        dv.wait_ge(s_dv, SET + 3 * i + 1)
                        nc.vector.tensor_tensor(o[:, :].rearrange("p (h c) -> p h c", c=DH), o4[:, :, 0:DH],
                                                rc[:, :].unsqueeze(2).broadcast_to([T, NH, DH]), ALU.mult)\
                            .then_inc(s_R, 1)
                        dv.wait_ge(s_R, n + 1)
                        nc.vector.tensor_tensor(y[:], o[:], X[0:T, i, :], ALU.add).then_inc(s_dv, 1)
                        dv.wait_ge(s_dv, SET + 3 * i + 2)
                        nc.vector.bn_stats(stats[:], y[:]).then_inc(s_dv, 1)
                        dv.wait_ge(s_dv, SET + 3 * i + 3)
                        nc.vector.memset(gap[:], 0.0)
                        nc.vector.bn_aggr(mv[:], stats[:]).then_inc(s_mv, 1)

                def normed(i):
                    dv.wait_ge(s_rs, i + 1)
                    nc.vector.tensor_scalar(X[0:T, i, :], y[:], mv[:, 0:1], rs[:, 1:2], ALU.subtract, ALU.mult)\
                        .then_inc(s_x, 1)

                def weigh(i, b, m):
                    n = i * NQ + m
                    h = HQ * m
                    dv.wait_ge(s_S, n + 1)
                    above(dv, s_P, n - 3)
                    nc.vector.tensor_tensor(same[:], pB[m % 2][0:T, 0:HQ * T].rearrange("p (h t) -> p h t", h=HQ),
                                            bk[b][:, h:h + HQ].unsqueeze(2).broadcast_to([T, HQ, T]), ALU.is_equal)\
                        .then_inc(s_dq, 1)
                    dv.wait_ge(s_dq, n + 1)
                    nc.vector.scalar_tensor_tensor(
                        out=A[m][:, :, :].rearrange("p h t -> p (h t)"),
                        in0=same[:, :, :].rearrange("p h t -> p (h t)"), scalar=float(NBK - 2),
                        in1=pS[m % 2][0:T, 0:HQ * T], op0=ALU.add, op1=ALU.mult).then_inc(s_mx, 1)
                    dv.wait_ge(s_mx, 2 * n + 1)
                    nc.vector.reduce_max(mx[m][:], A[m][:], AX).then_inc(s_mx, 1)
                    dv.wait_ge(s_mx, 2 * n + 2)
                    nc.vector.tensor_scalar(mx[m][:], mx[m][:], -SCALE, None, ALU.mult).then_inc(s_A, 1)

                def body(i, b):
                    for m in range(NQ):
                        small = side.steps(i, m)
                        if m == NQ - 1:
                            for name, n in small[:1]:
                                step(name, n, i + 1 if name[0] == "f" else i - 1, 1 - b)
                            small = small[1:]
                        weigh(i, b, m)
                        for name, n in small:
                            step(name, n, i + 1 if name[0] == "f" else i - 1, 1 - b)
                        if m == NQ - 1 and not (isinstance(i, int) and i == 0):
                            normed(i - 1)

                ch = Chain(dv, s_dv, 0)
                ch.base, ch.n = 0, 0
                ch.after(nc.vector.memset(hyp[:], 0.0))
                nc.vector.memset(rc[:], 0.0).then_inc(s_z1, 1)
                for b in range(2):
                    ch.after(nc.vector.memset(va[b][:], 0.0))
                    ch.after(nc.vector.memset(va[b][:, :, DH:DH + 1], 1.0))
                ch.after(nc.vector.memset(eps[:], EPS))
                assert ch.n == SET
                nc.vector.memset(ones[:], 1.0).then_inc(s_z, 1)
                dv.wait_ge(s_z, 1)
                dv.wait_ge(s_w, 16 * NW)
                for name, n in side.prologue():
                    step(name, n, 0, 0)
                over_batches(dv, body)
                for name, n in side.epilogue():
                    step(name, n, NB - 1, 0)
                normed(NB - 1)

            @block.scalar
            def _(ac):
                def step(name, n, i, b):
                    if name == "fx":
                        ac.wait_ge(s_F, n + 1)
                        nc.scalar.copy(xT[:, :, :].rearrange("p k t -> p (k t)"), pf[:, 0:KD * T]).then_inc(s_R, 1)

                def rstd(i):
                    ac.wait_ge(s_mv, i + 1)
                    nc.scalar.activation(rs[:, 0:1], mv[:, 1:2], ACT.Ln, bias=eps[:, 0:1]).then_inc(s_ln, 1)
                    ac.wait_ge(s_ln, i + 1)
                    nc.scalar.activation(rs[:, 1:2], rs[:, 0:1], ACT.Exp, scale=-0.5).then_inc(s_rs, 1)

                def exps(i, m):
                    n = i * NQ + m
                    ac.wait_ge(s_A, n + 1)
                    above(ac, s_PTp, n - 3)
                    for e in range(HQ):
                        ins = nc.scalar.activation(pr[m][:, e, :], A[m][:, e, :], ACT.Exp, scale=SCALE,
                                                   bias=mx[m][:, e:e + 1])
                    ins.then_inc(s_P, 1)

                def evac(n, m):
                    ac.wait_ge(s_PTp, n + 1)
                    above(ac, s_AV, n - 1)
                    nc.scalar.copy(pT[m % 2][:], pPT[m % 2][0:T, 0:HQ * T]).then_inc(s_PT, 1)

                def sums(i):
                    ac.wait_ge(s_AV, i * NQ + NQ)
                    nc.scalar.copy(avT[:, :, :].rearrange("p q t -> p (q t)"), pav[:, 0:NQ * T]).then_inc(s_av, 1)

                def body(i, b):
                    first = isinstance(i, int) and i == 0
                    for m in range(NQ):
                        if m == 3 and not first:
                            sums(i - 1)
                        for name, n in side.steps(i, m):
                            step(name, n, i + 1 if name[0] == "f" else i - 1, 1 - b)
                        if m >= 2 or not first:
                            evac(i * NQ + m - 2, (m - 2) % NQ)
                        if m == 3 and not first:
                            rstd(i - 1)
                        exps(i, m)

                ac.wait_ge(s_z, 1)
                nc.scalar.preload_act_table_set("natural_log_exp_and_others")
                for name, n in side.prologue():
                    step(name, n, 0, 0)
                over_batches(ac, body)
                evac(NB * NQ - 2, NQ - 2)
                evac(NB * NQ - 1, NQ - 1)
                sums(NB - 1)
                for name, n in side.epilogue():
                    step(name, n, NB - 1, 0)
                rstd(NB - 1)

            @block.gpsimd
            def _(po):
                def stage(i):
                    if not isinstance(i, int) or i:
                        po.wait_ge(s_R, side.read_of(i - 1, "fx"))
                    nc.gpsimd.tensor_copy(xs[:], X[0:T, i, :]).then_inc(s_xs, 1)

                def masks(i, b):
                    po.wait_ge(s_R, side.read_of(i, "fq"))
                    for e in range(KD):
                        ins = nc.gpsimd.tensor_tensor(qTm[b][:, e, :, :],
                                                      qT[b][:, e, :].unsqueeze(1).broadcast_to([P, HG, T]),
                                                      hmask[:, :].unsqueeze(2).broadcast_to([P, HG, T]), ALU.mult)
                    ins.then_inc(s_qm, 1)

                def diagonals(i, b):
                    po.wait_ge(s_R, side.read_of(i, "fh"))
                    nc.gpsimd.tensor_tensor(dg[b][:], ident[0:T, 0:T].unsqueeze(1).broadcast_to([T, NH, T]),
                                            bk[b][:, :].unsqueeze(2).broadcast_to([T, NH, T]), ALU.mult)\
                        .then_inc(s_dg, 1)

                def ahead(i, b):
                    masks(i, b)
                    if not isinstance(i, int) or i < NB - 1:
                        stage(i + 1)
                    diagonals(i, b)

                po.wait_ge(s_w, 16 * NW)
                stage(0)
                for i in (0, 1):
                    ahead(i, i)
                with po.Fori(1, NB // 2 - 1) as j:
                    for b in range(2):
                        ahead(2 * j + b, b)
                for i in (NB - 2, NB - 1):
                    ahead(i, i % 2)


def latent_attention(nc, X, ident, d):
    DX = 64
    NE = NH * DX // P
    NC, SK = 4, SC + T
    KP_ = NC * P
    MP = NH // 2
    SCALE = DX ** -0.5
    ckeys = [P, P, SC - 2 * P]
    keys = [min(P, SK - c * P) for c in range(NC)]
    SLOTS = [["fl", "fc0", "fc1"], ["fk0", "fk1", "fk2"], ["by", "fk3", "fk4"], ["fk5", "fk6", "fk7"],
             ["fq0", "fq1", "fv00"], ["fv01", "fv10", "fv11"], ["fv20", "fv21", "fv30"], ["fv31"]]
    st = Stage(nc, "la")
    with st:
        sb, ps, sem = st.sb, st.ps, st.sem
        wq, wkv = sb("wq", [P, KD, NH * DX]), sb("wkv", [P, KD, 2 * NH * DX])
        wo = sb("wo", [P, NE, D])
        gx, bx, gl, bl = (sb(n, [P, KD]) for n in ("gx", "bx", "gl", "bl"))
        go, bo = sb("go", [T, D]), sb("bo", [T, D])
        half = sb("half", [P, 2])
        mk = sb("mk", [1, NB * SC], U8)
        mb = [sb(f"mb{b}", [P, SC + T + 1], BF16) for b in range(2)]
        row0 = sb("row0", [P, P], BF16)
        xs, cn = sb("xs", [T, D]), sb("cn", [P, 3, D])
        inT = sb("inT", [P, KD, SK])
        kT = [sb(f"kT{b}", [P, NE, SK]) for b in range(2)]
        v = [sb(f"v{b}", [P, NC, NH * DX]) for b in range(2)]
        qTm = [sb(f"qTm{b}", [P, NE, 2, T]) for b in range(2)]
        nm = [sb(f"nm{b}", [T, 2]) for b in range(2)]
        zs = [sb(f"zs{b}", [T, 4]) for b in range(2)]
        pr = [sb(f"pr{b}", [T, 2, KP_]) for b in range(2)]
        pT = [sb(f"pT{b}", [P, 2, NC * T]) for b in range(2)]
        oT = [sb(f"oT{b}", [P, NE, T]) for b in range(2)]
        xb, y0, y1, y2, y3 = (sb(n, [T, D]) for n in ("xb", "y0", "y1", "y2", "y3"))
        cst, cmv, crs = sb("cst", [P, 4, 6]), sb("cmv", [P, 4, 2]), sb("crs", [P, 2, 4])
        stats, mv, rs, eps = sb("stats", [T, 6]), sb("mv", [T, 2]), sb("rs", [T, 2]), sb("eps", [P, 1])
        gap = sb("gap", [T, 1])
        pS = ps("pS", [P, 4, 512])
        pPT = ps("pPT", [P, 2, 512])
        pav, pf = ps("pav", [P, 4, T]), ps("side", [P, 512])

        s_w, s_z = sem("weights_loaded"), sem("padding_zeroed")
        s_cn = sem("context_loaded")
        s_xs, s_F, s_R = sem("xs_staged"), sem("side_filled"), sem("side_read")
        s_cmv, s_cln, s_crs, s_n = (sem(n) for n in ("input_stats", "input_log", "input_rstd", "inputs_normed"))
        s_mb = sem("mask_ready")
        s_S, s_mx, s_P, s_Z = sem("scores_in_psum"), sem("max_ready"), sem("exp_ready"), sem("probs_ready")
        s_PTp, s_PT, s_AV, s_av = (sem(n) for n in ("probsT_in_psum", "probsT_ready", "values_summed", "sums_read"))
        s_xb, s_mv, s_ln, s_rs, s_x = (sem(n) for n in ("x_plus_bias", "ln_stats", "ln_log", "ln_rstd", "x_done"))
        s_nn = sem("input_applied")
        s_dv, s_dn, s_dy, s_dz = sem("setup_chain"), sem("input_chain"), sem("out_chain"), sem("norm_chain")
        side = Side(SLOTS, s_F, s_R)
        NW = 11

        with nc.Block() as block:
            @block.sync
            def _(sp):
                col = lambda n: d[n].rearrange("(k p) -> p k", p=P)
                with nc.allow_non_contiguous_dma("small constants"):
                    for dst, src in ((wq[:], rows(d["L1_xattn_Wq"])), (wkv[:], rows(d["L1_xattn_Wkv"])),
                                     (wo[:], rows(d["L1_xattn_Wout"])), (gx[:], col("L1_xattn_g_x")),
                                     (bx[:], col("L1_xattn_b_x")), (gl[:], col("L1_xattn_g_l")),
                                     (bl[:], col("L1_xattn_b_l")), (go[:], bcast(d["L1_xattn_g_o"], T)),
                                     (bo[:], bcast(d["L1_xattn_b_o"], T)), (half[:], d["c_half"]),
                                     (mk[:], d["mask_BxS2_bf1"].rearrange("(a b) s -> a (b s)", a=1))):
                        sp.dma_start(dst, src).then_inc(s_w, 16)

                def load(i):
                    if not isinstance(i, int) or i:
                        sp.wait_ge(s_R, side.read_of(i - 1, "fc1"))
                    sp.dma_start(cn[:, 0:2, :], d["ctx_1024"][i, 0:2 * P, :].rearrange("(c p) n -> p c n", p=P))\
                        .then_inc(s_cn, 16)
                    sp.dma_start(cn[0:ckeys[2], 2, :], d["ctx_1024"][i, 2 * P:SC, :]).then_inc(s_cn, 16)
                for i in range(3):
                    load(i)
                with sp.Fori(3, NB) as i:
                    load(i)

            @block.tensor
            def _(pe):
                def step(name, n, i, b):
                    if name == "fl":
                        pe.wait_ge(s_n, i + 1)
                    above(pe, s_R, n)
                    if name == "fl":
                        for k in range(KD):
                            last = nc.tensor.transpose(pf[:, k * T:(k + 1) * T], xs[:, k * P:(k + 1) * P],
                                                       ident[0:T, 0:T])
                    elif name in ("fc0", "fc1"):
                        k = int(name[-1])
                        for c in range(3):
                            last = nc.tensor.transpose(pf[:, c * P:c * P + ckeys[c]],
                                                       cn[0:ckeys[c], c, k * P:(k + 1) * P],
                                                       ident[0:ckeys[c], 0:ckeys[c]])
                    elif name[:2] == "fk":
                        e = int(name[2])
                        for k in range(KD):
                            last = nc.tensor.matmul(pf[:, 0:SK], wkv[:, k, e * P:(e + 1) * P], inT[:, k, :],
                                                    start=k == 0, stop=k == KD - 1)
                    elif name[:2] == "fq":
                        for q in range(4):
                            e = 4 * int(name[2]) + q
                            for k in range(KD):
                                last = nc.tensor.matmul(pf[:, q * T:(q + 1) * T], wq[:, k, e * P:(e + 1) * P],
                                                        inT[:, k, SC:SK], start=k == 0, stop=k == KD - 1)
                    elif name[:2] == "fv":
                        c, h = int(name[2]), int(name[3])
                        for k in range(KD):
                            o = NH * DX + h * 512
                            last = nc.tensor.matmul(pf[0:keys[c], :], inT[:, k, c * P:c * P + keys[c]],
                                                    wkv[:, k, o:o + 512], start=k == 0, stop=k == KD - 1)
                    else:
                        for e in range(NE):
                            last = nc.tensor.matmul(pf[0:T, 0:D], oT[1 - b][:, e, :], wo[:, e, :],
                                                    start=e == 0, stop=e == NE - 1)
                    last.then_inc(s_F, 1)

                def scores(i, b, m):
                    n = i * MP + m
                    if m == 0:
                        pe.wait_ge(s_R, side.front_done(i))
                        pe.wait_ge(s_mb, i + 1)
                    above(pe, s_P, n - 1)
                    for e in range(2):
                        o = pS[0:T, 2 * (m % 2) + e, 0:SK]
                        nc.tensor.matmul(o, row0[:, 0:T], mb[b][:, 0:SK], start=True, stop=False)
                        last = nc.tensor.matmul(o, qTm[b][:, m, e, :], kT[b][:, m, :], start=False, stop=True)
                    last.then_inc(s_S, 1)

                def turn(n, m):
                    pe.wait_ge(s_Z, n + 1)
                    above(pe, s_PT, n)
                    for e in range(2):
                        for c in range(NC):
                            last = nc.tensor.transpose(pPT[:, e, c * T:(c + 1) * T],
                                                       pr[m % 2][:, e, c * P:(c + 1) * P], ident[0:T, 0:T])
                    last.then_inc(s_PTp, 1)

                def values(n, b, m):
                    pe.wait_ge(s_PT, n + 1)
                    above(pe, s_av, n)
                    for e in range(2):
                        for c in range(NC):
                            last = nc.tensor.matmul(pav[DX * e:DX * (e + 1), m % 4, :],
                                                    v[b][:, c, (2 * m + e) * DX:(2 * m + e + 1) * DX],
                                                    pT[m % 2][:, e, c * T:(c + 1) * T], start=c == 0, stop=c == NC - 1)
                    last.then_inc(s_AV, 1)

                def body(i, b):
                    first = isinstance(i, int) and i == 0
                    for m in range(MP):
                        n = i * MP + m
                        small = side.steps(i, m) + [None] * 3

                        def between(s):
                            if s and s[0] == "by":
                                pe.wait_ge(s_av, i * MP)
                                step(*s, i - 1, b)
                            elif s:
                                step(*s, i + 1, 1 - b)
                        scores(i, b, m)
                        between(small[0])
                        if m >= 1 or not first:
                            turn(n - 1, (m - 1) % MP)
                        between(small[1])
                        if m >= 2:
                            values(n - 2, b, m - 2)
                        elif not first:
                            values(n - 2, 1 - b, MP - 2 + m)
                        between(small[2])

                pe.wait_ge(s_w, 16 * NW)
                pe.wait_ge(s_z, 1)
                for name, n in side.prologue():
                    step(name, n, 0, 0)
                over_batches(pe, body)
                n = NB * MP
                turn(n - 1, MP - 1)
                values(n - 2, 1, MP - 2)
                values(n - 1, 1, MP - 1)
                pe.wait_ge(s_av, n)
                for name, k in side.epilogue():
                    step(name, k, NB - 1, 0)

            @block.vector
            def _(dv):
                SET = 6
                NLN = 8

                def inputs(i):
                    dv.wait_ge(s_cn, 32 * i + 32)
                    dv.wait_ge(s_xs, i + 1)
                    if not isinstance(i, int) or i:
                        dv.wait_ge(s_crs, i)
                    srcs = [cn[:, 0, :], cn[:, 1, :], cn[0:ckeys[2], 2, :], xs[:, :]]
                    for c, src in enumerate(srcs):
                        r = src.shape[0]
                        nc.vector.bn_stats(cst[0:r, c, :], src).then_inc(s_dn, 1)
                    dv.wait_ge(s_dn, i * 4 + 4)
                    nc.vector.memset(gap[:], 0.0)
                    for c, src in enumerate(srcs):
                        r = src.shape[0]
                        nc.vector.bn_aggr(cmv[0:r, c, :], cst[0:r, c, :]).then_inc(s_cmv, 1)

                def apply_inputs(i):
                    dv.wait_ge(s_crs, i + 1)
                    srcs = [cn[:, 0, :], cn[:, 1, :], cn[0:ckeys[2], 2, :], xs[:, :]]
                    for c, src in enumerate(srcs):
                        r = src.shape[0]
                        nc.vector.tensor_scalar(src, src, cmv[0:r, c, 0:1], crs[0:r, 1, c:c + 1],
                                                ALU.subtract, ALU.mult).then_inc(s_nn, 1)
                    dv.wait_ge(s_nn, i * 4 + 8)
                    nc.vector.memset(gap[:], 0.0).then_inc(s_n, 1)

                def mask(i, b):
                    above(dv, s_S, (i - 1) * MP)
                    nc.vector.tensor_scalar(mb[b][0:1, 0:SC], mk[0:1, bass.ds(i * SC, SC)], -1.0, BIG, ALU.add,
                                            ALU.mult).then_inc(s_mb, 1)

                def step(name, n, i, b):
                    if name[:2] == "fq":
                        dv.wait_ge(s_F, n + 1)
                        for e in range(2):
                            ins = nc.vector.tensor_scalar(qTm[b][:, 4 * int(name[2]):4 * int(name[2]) + 4, e, :],
                                                          pf[:, 0:4 * T].rearrange("p (q t) -> p q t", q=4),
                                                          half[:, e:e + 1], None, ALU.mult)
                        ins.then_inc(s_R, 1)
                    elif name[:2] == "fv":
                        c, h = int(name[2]), int(name[3])
                        dv.wait_ge(s_F, n + 1)
                        nc.vector.tensor_copy(v[b][0:keys[c], c, h * 512:(h + 1) * 512], pf[0:keys[c], :])\
                            .then_inc(s_R, 1)
                    elif name == "by":
                        dv.wait_ge(s_F, n + 1)
                        nc.vector.tensor_copy(y0[:], pf[0:T, 0:D]).then_inc(s_R, 1)
                        dv.wait_ge(s_R, n + 1)
                        link(nc.vector.bn_stats(stats[:], y0[:]), i, 1)
                        nc.vector.memset(gap[:], 0.0)
                        nc.vector.bn_aggr(mv[:], stats[:]).then_inc(s_mv, 1)

                def link(ins, i, k):
                    ins.then_inc(s_dy, 1)
                    dv.wait_ge(s_dy, 5 * i + k)

                def out_norm(i):
                        dv.wait_ge(s_rs, 2 * i + 1)
                        link(nc.vector.tensor_scalar(y1[:], y0[:], mv[:, 0:1], rs[:, 1:2], ALU.subtract, ALU.mult), i, 2)
                        link(nc.vector.tensor_tensor(y2[:], y1[:], go[:], ALU.mult), i, 3)
                        dv.wait_ge(s_xb, i + 1)
                        link(nc.vector.tensor_tensor(y3[:], y2[:], xb[:], ALU.add), i, 4)
                        link(nc.vector.bn_stats(stats[:], y3[:]), i, 5)
                        nc.vector.memset(gap[:], 0.0)
                        nc.vector.bn_aggr(mv[:], stats[:]).then_inc(s_mv, 1)

                def x_norm(i):
                        dv.wait_ge(s_rs, 2 * i + 2)
                        nc.vector.tensor_scalar(X[0:T, i, :], y3[:], mv[:, 0:1], rs[:, 1:2], ALU.subtract, ALU.mult)\
                            .then_inc(s_x, 1)

                def maxima(i, m):
                    n = i * MP + m
                    dv.wait_ge(s_S, n + 1)
                    above(dv, s_P, n - 1)
                    nc.vector.reduce_max(nm[m % 2][:], pS[0:T, 2 * (m % 2):2 * (m % 2) + 2, 0:SK], AX)\
                        .then_inc(s_mx, 1)
                    dv.wait_ge(s_mx, 2 * n + 1)
                    nc.vector.tensor_scalar(nm[m % 2][:], nm[m % 2][:], -SCALE, None, ALU.mult).then_inc(s_mx, 1)

                def norm(n, m):
                    dv.wait_ge(s_P, n + 1)
                    nc.vector.reciprocal(zs[m % 2][:, 2:4], zs[m % 2][:, 0:2]).then_inc(s_dz, 1)
                    dv.wait_ge(s_dz, n + 1)
                    for e in range(2):
                        ins = nc.vector.tensor_scalar(pr[m % 2][:, e, 0:SK], pr[m % 2][:, e, 0:SK],
                                                      zs[m % 2][:, 2 + e:3 + e], None, ALU.mult)
                    ins.then_inc(s_Z, 1)

                def body(i, b):
                    first = isinstance(i, int) and i == 0
                    ahead = not isinstance(i, int) or i + 2 < NB
                    for m in range(MP):
                        if m or not first:
                            norm(i * MP + m - 1, (m - 1) % MP)
                        maxima(i, m)
                        if m == 3 and not first:
                            out_norm(i - 1)
                        if m == 4 and not first:
                            x_norm(i - 1)
                        if m == 5 and ahead:
                            inputs(i + 2)
                        if m == 6 and ahead:
                            apply_inputs(i + 2)
                        if m == 7 and (not isinstance(i, int) or i + 1 < NB):
                            mask(i + 1, 1 - b)
                        for name, n in side.steps(i, m):
                            step(name, n, i + 1 if name[0] == "f" else i - 1, 1 - b)

                ch = Chain(dv, s_dv, 0)
                ch.base, ch.n = 0, 0
                for b in range(2):
                    ch.after(nc.vector.memset(v[b][:, NC - 1, :], 0.0))
                    ch.after(nc.vector.memset(pr[b][:], 0.0))
                    ch.after(nc.vector.memset(mb[b][:], 0.0))
                nc.vector.memset(eps[:], EPS)
                nc.vector.memset(cmv[:], 1.0)
                nc.vector.memset(row0[:], 0.0).then_inc(s_nn, 4)
                dv.wait_ge(s_nn, 4)
                nc.vector.memset(row0[0:1, :], 1.0).then_inc(s_z, 1)
                dv.wait_ge(s_z, 1)
                dv.wait_ge(s_w, 16 * NW)
                inputs(0)
                apply_inputs(0)
                mask(0, 0)
                for name, n in side.prologue():
                    step(name, n, 0, 0)
                    if name == "fc1":
                        inputs(1)
                        apply_inputs(1)
                over_batches(dv, body, 3)
                norm(NB * MP - 1, MP - 1)
                for name, n in side.epilogue():
                    step(name, n, NB - 1, 0)
                out_norm(NB - 1)
                x_norm(NB - 1)

            @block.scalar
            def _(ac):
                def inputs(i):
                    ac.wait_ge(s_cmv, 4 * i + 4)
                    if not isinstance(i, int) or i:
                        ac.wait_ge(s_n, i)
                    nc.scalar.activation(crs[:, 0, :], cmv[:, :, 1], ACT.Ln, bias=eps[:, 0:1]).then_inc(s_cln, 1)
                    ac.wait_ge(s_cln, i + 1)
                    nc.scalar.activation(crs[:, 1, :], crs[:, 0, :], ACT.Exp, scale=-0.5).then_inc(s_crs, 1)

                def step(name, n, i, b):
                    if name == "fl":
                        ac.wait_ge(s_F, n + 1)
                        for k in range(KD):
                            ins = nc.scalar.activation(inT[:, k, SC:SK], pf[:, k * T:(k + 1) * T], ACT.Identity,
                                                       bias=bl[:, k:k + 1], scale=gl[:, k:k + 1])
                        ins.then_inc(s_R, 1)
                    elif name in ("fc0", "fc1"):
                        k = int(name[-1])
                        ac.wait_ge(s_F, n + 1)
                        nc.scalar.activation(inT[:, k, 0:SC], pf[:, 0:SC], ACT.Identity, bias=bx[:, k:k + 1],
                                             scale=gx[:, k:k + 1]).then_inc(s_R, 1)
                    elif name[:2] == "fk":
                        ac.wait_ge(s_F, n + 1)
                        nc.scalar.copy(kT[b][:, int(name[2]), :], pf[:, 0:SK]).then_inc(s_R, 1)

                def rstd(i, r):
                    ac.wait_ge(s_mv, 2 * i + (r + 1))
                    nc.scalar.activation(rs[:, 0:1], mv[:, 1:2], ACT.Ln, bias=eps[0:T, 0:1]).then_inc(s_ln, 1)
                    ac.wait_ge(s_ln, 2 * i + (r + 1))
                    nc.scalar.activation(rs[:, 1:2], rs[:, 0:1], ACT.Exp, scale=-0.5).then_inc(s_rs, 1)

                def exps(i, m):
                    n = i * MP + m
                    ac.wait_ge(s_mx, 2 * n + 2)
                    above(ac, s_PTp, n - 1)
                    for e in range(2):
                        ins = nc.scalar.activation(pr[m % 2][:, e, 0:SK], pS[0:T, 2 * (m % 2) + e, 0:SK], ACT.Exp,
                                                   bias=nm[m % 2][:, e:e + 1], scale=SCALE,
                                                   accum_out=zs[m % 2][:, e:e + 1])
                    ins.then_inc(s_P, 1)

                def evac(n, m):
                    ac.wait_ge(s_PTp, n + 1)
                    above(ac, s_AV, n - 1)
                    nc.scalar.copy(pT[m % 2][:], pPT[:, :, 0:NC * T]).then_inc(s_PT, 1)

                def sums(n, b, m):
                    ac.wait_ge(s_AV, n + 1)
                    nc.scalar.copy(oT[b][:, m, :], pav[:, m % 4, :]).then_inc(s_av, 1)

                def body(i, b):
                    first = isinstance(i, int) and i == 0
                    ahead = not isinstance(i, int) or i + 2 < NB
                    for m in range(MP):
                        n = i * MP + m
                        small = side.steps(i, m) + [None] * 3

                        def between(s):
                            if s:
                                step(*s, i + 1 if s[0][0] == "f" else i - 1, 1 - b)
                        if m == 3 and not first:
                            rstd(i - 1, 0)
                        if m == 4 and not first:
                            rstd(i - 1, 1)
                        if m == 6 and ahead:
                            inputs(i + 2)
                        between(small[0])
                        exps(i, m)
                        between(small[1])
                        if m or not first:
                            evac(n - 1, (m - 1) % MP)
                        if m >= 2:
                            sums(n - 2, b, m - 2)
                        elif not first:
                            sums(n - 2, 1 - b, MP - 2 + m)
                        between(small[2])

                ac.wait_ge(s_w, 16 * NW)
                ac.wait_ge(s_z, 1)
                nc.scalar.preload_act_table_set("natural_log_exp_and_others")
                inputs(0)
                for name, n in side.prologue():
                    step(name, n, 0, 0)
                    if name == "fc1":
                        inputs(1)
                over_batches(ac, body, 3)
                n = NB * MP
                evac(n - 1, MP - 1)
                sums(n - 2, 1, MP - 2)
                sums(n - 1, 1, MP - 1)
                for name, k in side.epilogue():
                    step(name, k, NB - 1, 0)
                rstd(NB - 1, 0)
                rstd(NB - 1, 1)

            @block.gpsimd
            def _(po):
                def stage(i):
                    if not isinstance(i, int) or i:
                        po.wait_ge(s_R, side.read_of(i - 1, "fl"))
                    nc.gpsimd.tensor_copy(xs[:], X[0:T, i, :]).then_inc(s_xs, 1)

                def residual(i):
                    above(po, s_x, i)
                    nc.gpsimd.tensor_tensor(xb[:], X[0:T, i, :], bo[:], ALU.add).then_inc(s_xb, 1)

                po.wait_ge(s_w, 16 * NW)
                stage(0)
                stage(1)
                residual(0)
                stage(2)
                residual(1)
                with po.Fori(2, NB - 1) as i:
                    stage(i + 1)
                    residual(i)
                residual(NB - 1)


NBK = (NB * T + 8 * (P - 1)) // P
NTH = -(-NB * T // P)


def routed_ffn(nc, X, ident, d, out, rows_in, rows_out, s_zero):
    E, F = 8, 1024
    KF = F // P
    st = Stage(nc, "rf")
    with st:
        sb, ps, sem = st.sb, st.ps, st.sem
        w1, w2 = sb("w1", [P, E, KD, F]), sb("w2", [P, E, KF, D])
        gate = sb("gate", [T, NB])
        slot = sb("slot", [T, NB], U32)
        ebu = sb("ebu", [1, NBK], U32)
        s_we = [sem(f"weights_loaded{e}") for e in range(E)]
        s_wr = sem("experts_ready")
        s_sc, s_rt = sem("rows_scattered"), sem("routing_ready")

        rt = Stage(nc, "rr")
        with rt:
            wr, br = rt.sb("wr", [P, KD, E]), rt.sb("br", [T, E])
            tri, ones = rt.sb("tri", [T, T]), rt.sb("ones", [T, T])
            ie = rt.sb("ie", [T, NB, E])
            thr, blk = rt.sb("thr", [T, E, NTH]), rt.sb("blk", [1, NBK, E])
            xs, xT = rt.sb("xs", [T, D]), rt.sb("xT", [P, KD, T])
            lg, ex, route, eq, oh, pos = (rt.sb(n, [T, NB, E]) for n in ("lg", "ex", "route", "eq", "oh", "pos"))
            sc = [rt.sb(f"sc{n}", [T, NB, E]) for n in range(2)]
            tot = rt.sb("tot", [T, NB, E])
            ixe, slf = rt.sb("ixe", [T, NB]), rt.sb("slf", [T, NB])
            gt, nb_ = rt.sb("gt", [T, E, NTH]), rt.sb("nb", [T, E])
            be = [rt.sb(f"be{n}", [T, E]) for n in range(2)]
            ge, eb = rt.sb("ge", [1, NBK, E]), rt.sb("eb", [1, NBK])
            pt = rt.ps("pt", [P, 512])
            pl, pp = rt.ps("pl", [P, 512]), rt.ps("pp", [P, 512])
            s_c, s_xs, s_xTp, s_xT = rt.sem("consts"), rt.sem("xs_staged"), rt.sem("xT_in_psum"), rt.sem("xT_ready")
            s_l, s_lg, s_ex = rt.sem("logits_in_psum"), rt.sem("logits_ready"), rt.sem("exp_ready")
            s_oh, s_pp, s_ch = rt.sem("onehot_ready"), rt.sem("prefixes_in_psum"), rt.sem("dve_chain")
            NC_ = 6
            with nc.Block() as block:
                @block.sync
                def _(sp):
                    with nc.allow_non_contiguous_dma("small constants"):
                        for dst, src in ((wr[:], rows(d["L1_ffn_Wr"])), (br[:], bcast(d["L1_ffn_br"], T)),
                                         (tri[:], d["c_tri"]), (ie[:], d["c_experts"]), (thr[:], d["c_thresholds"]),
                                         (blk[:], d["c_blocks"])):
                            sp.dma_start(dst, src).then_inc(s_c, 16)
                    for e in range(E):
                        sp.dma_start(w1[:, e], rows(d["L1_ffn_W1"][e])).then_inc(s_we[e], 16)
                        sp.dma_start(w2[:, e], rows(d["L1_ffn_W2"][e])).then_inc(s_we[e], 16)

                @block.tensor
                def _(pe):
                    pe.wait_ge(s_c, 16 * NC_)
                    with pe.Fori(0, NB) as i:
                        pe.wait_ge(s_xs, i + 1)
                        for k in range(KD):
                            last = nc.tensor.transpose(pt[:, k * T:(k + 1) * T], xs[:, k * P:(k + 1) * P],
                                                       ident[0:T, 0:T])
                        last.then_inc(s_xTp, 1)
                        pe.wait_ge(s_xT, i + 1)
                        for k in range(KD):
                            last = nc.tensor.matmul(pl[0:T, bass.ds(i * E, E)], xT[:, k, :], wr[:, k, :],
                                                    start=k == 0, stop=k == KD - 1)
                        last.then_inc(s_l, 1)
                    pe.wait_ge(s_oh, 1)
                    o = oh[:, :, :].rearrange("p b e -> p (b e)")
                    nc.tensor.matmul(pp[0:T, 0:NB * E], tri[:, :], o, start=True, stop=True)
                    nc.tensor.matmul(pp[0:T, 256:256 + NB * E], ones[:, :], o, start=True, stop=True)\
                        .then_inc(s_pp, 1)

                @block.scalar
                def _(ac):
                    ac.wait_ge(s_lg, 1)
                    nc.scalar.activation(ex[:], lg[:], ACT.Exp, scale=-1.0).then_inc(s_ex, 1)
                    ac.wait_ge(s_ex, 1)

                @block.vector
                def _(dv):
                    ch = Chain(dv, s_ch, 0)
                    ch.base, ch.n = 0, 0
                    tt = nc.vector.tensor_tensor
                    ch.after(nc.vector.memset(ones[:], 1.0))
                    def take(i):
                        above(dv, s_xTp, i)
                        nc.vector.tensor_copy(xs[:], X[0:T, i, :]).then_inc(s_xs, 1)
                        dv.wait_ge(s_xTp, i + 1)
                        above(dv, s_l, i)
                        nc.vector.tensor_copy(xT[:, :, :].rearrange("p k t -> p (k t)"), pt[:, 0:KD * T])\
                            .then_inc(s_xT, 1)
                    take(0)
                    with dv.Fori(1, NB) as i:
                        take(i)
                    dv.wait_ge(s_l, NB)
                    dv.wait_ge(s_c, 16 * NC_)
                    tt(lg[:], pl[0:T, 0:NB * E].rearrange("p (b e) -> p b e", e=E),
                       br[:, :].unsqueeze(1).broadcast_to([T, NB, E]), ALU.add).then_inc(s_lg, 1)
                    dv.wait_ge(s_ex, 1)
                    ch.after(nc.vector.tensor_scalar(ex[:], ex[:], 1.0, None, ALU.add))
                    ch.after(nc.vector.reciprocal(route[:], ex[:]))
                    ch.after(nc.vector.reduce_max(gate[:], route[:], AX))
                    ch.after(tt(eq[:], route[:], gate[:, :].unsqueeze(2).broadcast_to([T, NB, E]), ALU.is_equal))
                    ch.after(nc.vector.scalar_tensor_tensor(out=eq[:], in0=eq[:], scalar=-float(E), in1=ie[:],
                                                            op0=ALU.mult, op1=ALU.add))
                    ch.after(nc.vector.tensor_reduce(ixe[:], eq[:], AX, ALU.min))
                    ch.after(nc.vector.tensor_scalar(ixe[:], ixe[:], float(E), None, ALU.add))
                    tt(oh[:], ie[:], ixe[:, :].unsqueeze(2).broadcast_to([T, NB, E]), ALU.is_equal).then_inc(s_oh, 1)
                    dv.wait_ge(s_pp, 1)
                    ch.after(nc.vector.tensor_copy(tot[:], pp[0:T, 256:256 + NB * E].rearrange("p (b e) -> p b e", e=E)))
                    src, n = tot, 0
                    for s in (1, 2, 4, 8):
                        dst = sc[n % 2]
                        ch.after(nc.vector.tensor_copy(dst[:, 0:s, :], src[:, 0:s, :]))
                        ch.after(tt(dst[:, s:NB, :], src[:, s:NB, :], src[:, 0:NB - s, :], ALU.add))
                        src, n = dst, n + 1
                    ch.after(tt(gt[:], src[:, NB - 1, :].unsqueeze(2).broadcast_to([T, E, NTH]), thr[:], ALU.is_gt))
                    ch.after(nc.vector.reduce_sum(nb_[:], gt[:], AX))
                    bsrc, n = nb_, 0
                    for s in (1, 2, 4):
                        dst = be[n % 2]
                        ch.after(nc.vector.tensor_copy(dst[:, 0:s], bsrc[:, 0:s]))
                        ch.after(tt(dst[:, s:E], bsrc[:, s:E], bsrc[:, 0:E - s], ALU.add))
                        bsrc, n = dst, n + 1
                    ch.after(tt(ge[:], blk[:], bsrc[0:1, :].unsqueeze(1).broadcast_to([1, NBK, E]), ALU.is_ge))
                    ch.after(nc.vector.reduce_sum(eb[:], ge[:], AX))
                    ch.after(nc.vector.tensor_scalar(eb[:], eb[:], float(E - 1), None, ALU.min))
                    ch.after(nc.vector.tensor_copy(ebu[:], eb[:]))
                    ch.after(tt(be[n % 2][:], bsrc[:], nb_[:], ALU.subtract))
                    st_ = be[n % 2]
                    ch.after(nc.vector.tensor_scalar(st_[:], st_[:], float(P), None, ALU.mult))
                    ch.after(tt(pos[:], src[:], tot[:], ALU.subtract))
                    ch.after(tt(pos[:], pos[:], pp[0:T, 0:NB * E].rearrange("p (b e) -> p b e", e=E), ALU.add))
                    ch.after(tt(pos[:], pos[:], st_[:, :].unsqueeze(1).broadcast_to([T, NB, E]), ALU.add))
                    ch.after(tt(pos[:], pos[:], oh[:], ALU.mult))
                    ch.after(nc.vector.reduce_sum(slf[:], pos[:], AX))
                    nc.vector.tensor_copy(slot[:], slf[:]).then_inc(s_rt, 1)
                    dv.wait_ge(s_rt, 1)

                @block.gpsimd
                def _(po):
                    po.wait_ge(s_rt, 1)
                    po.wait_ge(s_zero, 16 * NBK)
                    for b in range(NB):
                        po.indirect_dma_start(rows_in[:, :], bass.IndirectOffsetOnAxis(ap=slot[:, b:b + 1], axis=0),
                                              X[0:T, b, :], None).then_inc(s_sc, 16)
                    po.wait_ge(s_sc, 16 * NB)

        bk = Stage(nc, "rb")
        with bk:
            xr = [bk.sb(f"xr{l}", [P, D]) for l in range(2)]
            xT = [bk.sb(f"xT{l}", [P, KD, P]) for l in range(2)]
            g, gT = bk.sb("g", [P, F]), bk.sb("gT", [P, KF, P])
            yr = [bk.sb(f"yr{l}", [P, D]) for l in range(2)]
            px, py = bk.ps("px", [P, 512]), bk.ps("py", [P, 512])
            ph, pg = bk.ps("ph", [P, 2, 512]), bk.ps("pg", [P, 2, 512])
            s_xr = [bk.sem(f"block_loaded{l}") for l in range(2)]
            s_st = [bk.sem(f"block_stored{l}") for l in range(2)]
            s_xTp, s_xT, s_h, s_g = (bk.sem(n) for n in ("xT_in_psum", "xT_ready", "h_in_psum", "gelu_ready"))
            s_gp, s_gT, s_y, s_yr = (bk.sem(n) for n in ("gT_in_psum", "gT_ready", "y_in_psum", "y_ready"))

            with nc.Block() as block:
                @block.sync
                def _(sp):
                    for e in range(E):
                        sp.wait_ge(s_we[e], 32)
                        sp.sem_inc(s_wr, 1)

                    def store(k, l):
                        sp.wait_ge(s_yr, k + 1)
                        sp.dma_start(rows_out[bass.ds(k * P, P), :], yr[l][:]).then_inc(s_st[l], 16)
                    with sp.Fori(0, NBK // 2) as j:
                        store(2 * j, 0)
                        store(2 * j + 1, 1)
                    for l in range(2):
                        sp.wait_ge(s_st[l], 16 * (NBK // 2))

                @block.gpsimd
                def _(po):
                    def body(k, l, n):
                        above(po, s_xTp, k - 1)
                        po.dma_start(xr[l][:], rows_in[bass.ds(k * P, P), :]).then_inc(s_xr[l], 16)
                    for k in range(2):
                        body(k, k, 0)
                    with po.Fori(1, NBK // 2) as j:
                        body(2 * j, 0, j)
                        body(2 * j + 1, 1, j)

                @block.tensor
                def _(pe):
                    def turn_x(k, l, n):
                        pe.wait_ge(s_xr[l], 16 * n + 16)
                        above(pe, s_xT, k)
                        for c in range(KD):
                            last = nc.tensor.transpose(px[:, c * P:(c + 1) * P], xr[l][:, c * P:(c + 1) * P], ident[:, :])
                        last.then_inc(s_xTp, 1)

                    def up(k, l, e):
                        pe.wait_ge(s_wr, e + 1)
                        pe.wait_ge(s_xT, k + 1)
                        above(pe, s_g, k)
                        for n in range(2):
                            for c in range(KD):
                                last = nc.tensor.matmul(ph[:, n, :], xT[l][:, c, :], w1[:, e, c, n * 512:(n + 1) * 512],
                                                        start=c == 0, stop=c == KD - 1)
                        last.then_inc(s_h, 1)

                    def turn_g(k):
                        pe.wait_ge(s_g, k + 1)
                        above(pe, s_gT, k)
                        for f in range(KF):
                            last = nc.tensor.transpose(pg[:, f // 4, (f % 4) * P:(f % 4 + 1) * P],
                                                       g[:, f * P:(f + 1) * P], ident[:, :])
                        last.then_inc(s_gp, 1)

                    def down(k, e):
                        pe.wait_ge(s_gT, k + 1)
                        above(pe, s_yr, k)
                        for f in range(KF):
                            last = nc.tensor.matmul(py[:, 0:D], gT[:, f, :], w2[:, e, f, :],
                                                    start=f == 0, stop=f == KF - 1)
                        last.then_inc(s_y, 1)

                    def expert(k):
                        return pe.value_load(ebu[0:1, bass.ds(k, 1)], min_val=0, max_val=E - 1)

                    def two(j):
                        for m in range(2):
                            k = 2 * j + (m + 1)
                            turn_g(k - 1)
                            up(k, (m + 1) % 2, expert(k))
                            turn_x(k + 1, m % 2, j + 1)
                            down(k - 1, expert(k - 1))
                    turn_x(0, 0, 0)
                    up(0, 0, expert(0))
                    turn_x(1, 1, 0)
                    two(0)
                    with pe.Fori(1, NBK // 2 - 1) as j:
                        two(j)
                    turn_g(NBK - 2)
                    up(NBK - 1, 1, expert(NBK - 1))
                    down(NBK - 2, expert(NBK - 2))
                    turn_g(NBK - 1)
                    down(NBK - 1, expert(NBK - 1))

                @block.scalar
                def _(ac):
                    def body(k):
                        ac.wait_ge(s_h, k + 1)
                        above(ac, s_gp, k)
                        nc.scalar.activation(g[:], ph[:, :, :].rearrange("p n c -> p (n c)"), ACT.Gelu).then_inc(s_g, 1)
                    body(0)
                    with ac.Fori(1, NBK) as k:
                        body(k)

                @block.vector
                def _(dv):
                    def take_x(k, l):
                        dv.wait_ge(s_xTp, k + 1)
                        above(dv, s_h, k - 1)
                        nc.vector.tensor_copy(xT[l][:, :, :].rearrange("p k t -> p (k t)"), px[:, 0:D]).then_inc(s_xT, 1)

                    def take_g(k):
                        dv.wait_ge(s_gp, k + 1)
                        above(dv, s_y, k)
                        nc.vector.tensor_copy(gT[:, :, :].rearrange("p f t -> p (f t)"),
                                              pg[:, :, :].rearrange("p n c -> p (n c)")).then_inc(s_gT, 1)

                    def take_y(k, l, n):
                        dv.wait_ge(s_y, k + 1)
                        above(dv, s_st[l], 16 * n)
                        nc.vector.tensor_copy(yr[l][:], py[:, 0:D]).then_inc(s_yr, 1)

                    take_x(0, 0)
                    take_x(1, 1)
                    def two(j):
                        for m in range(2):
                            k = 2 * j + (m + 1)
                            take_g(k - 1)
                            take_x(k + 1, m % 2)
                            take_y(k - 1, m % 2, j)
                    two(0)
                    with dv.Fori(1, NBK // 2 - 1) as j:
                        two(j)
                    take_g(NBK - 2)
                    take_y(NBK - 2, 0, NBK // 2 - 1)
                    take_g(NBK - 1)
                    take_y(NBK - 1, 1, NBK // 2 - 1)


        fn = Stage(nc, "rn")
        with fn:
            y = fn.sb("y", [T, NB, D])
            st6, mv, rs, eps = fn.sb("st6", [T, NB, 6]), fn.sb("mv", [T, NB, 2]), fn.sb("rs", [T, 2, NB]), fn.sb("eps", [T, 1])
            s_ga, s_z, s_sm, s_mv = fn.sem("rows_gathered"), fn.sem("sums_ready"), fn.sem("stats_ready"), fn.sem("means_ready")
            s_ln, s_rs, s_x, s_out = fn.sem("log_ready"), fn.sem("rstd_ready"), fn.sem("x_done"), fn.sem("out_stored")
            s_gb = [fn.sem(f"gathered{b}") for b in range(4)]
            with nc.Block() as block:
                @block.gpsimd
                def _(po):
                    for b in range(NB):
                        po.indirect_dma_start(y[:, b, :], None, rows_out[:, :],
                                              bass.IndirectOffsetOnAxis(ap=slot[:, b:b + 1], axis=0))\
                            .then_inc(s_gb[b // 4], 16)

                @block.vector
                def _(dv):
                    nc.vector.memset(eps[:], EPS).then_inc(s_z, 1)
                    for b in range(NB):
                        if b % 4 == 0:
                            dv.wait_ge(s_gb[b // 4], 64)
                        nc.vector.scalar_tensor_tensor(out=X[0:T, b, :], in0=y[:, b, :], scalar=gate[:, b:b + 1],
                                                       in1=X[0:T, b, :], op0=ALU.mult, op1=ALU.add).then_inc(s_sm, 1)
                        if b:
                            dv.wait_ge(s_sm, b)
                            nc.vector.bn_stats(st6[:, b - 1, :], X[0:T, b - 1, :]).then_inc(s_mv, 1)
                    dv.wait_ge(s_sm, NB)
                    nc.vector.bn_stats(st6[:, NB - 1, :], X[0:T, NB - 1, :]).then_inc(s_mv, 1)
                    dv.wait_ge(s_mv, NB)
                    for b in range(NB):
                        nc.vector.bn_aggr(mv[:, b, :], st6[:, b, :]).then_inc(s_mv, 1)
                    dv.wait_ge(s_rs, 1)
                    for b in range(NB):
                        nc.vector.tensor_scalar(X[0:T, b, :], X[0:T, b, :], mv[:, b, 0:1], rs[:, 1, b:b + 1],
                                                ALU.subtract, ALU.mult).then_inc(s_x, 1)

                @block.scalar
                def _(ac):
                    ac.wait_ge(s_z, 1)
                    ac.wait_ge(s_mv, 2 * NB)
                    nc.scalar.activation(rs[:, 0, :], mv[:, :, 1], ACT.Ln, bias=eps[:, 0:1]).then_inc(s_ln, 1)
                    ac.wait_ge(s_ln, 1)
                    nc.scalar.activation(rs[:, 1, :], rs[:, 0, :], ACT.Exp, scale=-0.5).then_inc(s_rs, 1)

                @block.sync
                def _(sp):
                    o = out.rearrange("b t d -> t b d")
                    for b in range(0, NB, 4):
                        sp.wait_ge(s_x, b + 4)
                        sp.dma_start(o[:, b:b + 4, :], X[0:T, b:b + 4, :]).then_inc(s_out, 16)
                    sp.wait_ge(s_out, 16 * (NB // 4))


def build(nc, d, out, stages=6, start=0):
    rows_in = nc.dram_tensor("rows_in", (NBK * P, D), F32).ap()
    rows_out = nc.dram_tensor("rows_out", (NBK * P, D), F32).ap()
    st = Stage(nc, "io")
    with st:
        X = st.sb("X", [P, NB, D])
        ident, zero = st.sb("ident", [P, P]), st.sb("zero", [P, D])
        s_in, s_out = st.sem("x_loaded"), st.sem("out_stored")
        s_z, s_zero = st.sem("zero_ready"), st.sem("rows_zeroed")
        with nc.Block() as block:
            @block.vector
            def _(dv):
                nc.vector.memset(zero[:], 0.0).then_inc(s_z, 1)

            @block.sync
            def _(sp):
                sp.dma_start(ident[:], d["c_ident"]).then_inc(s_in, 16)
                sp.dma_start(X[0:T, :, :], d["x"].rearrange("b t d -> t b d")).then_inc(s_in, 16)
                sp.wait_ge(s_z, 1)
                for k in range(NBK):
                    sp.dma_start(rows_in[k * P:(k + 1) * P, :], zero[:]).then_inc(s_zero, 16)
                sp.wait_ge(s_in, 32)
        for n, stage in enumerate((self_attention, cross_attention, expert_adapter, bucket_attention,
                                   latent_attention)):
            if start <= n < stages:
                stage(nc, X, ident, d)
        if stages == 6:
            routed_ffn(nc, X, ident, d, out, rows_in, rows_out, s_zero)
            return
        with nc.Block() as block:
            @block.sync
            def _(sp):
                sp.wait_ge(s_zero, 16 * NBK)
                sp.dma_start(out.rearrange("b t d -> t b d"), X[0:T, :, :]).then_inc(s_out, 16)
                sp.wait_ge(s_out, 16)


def shape_constants():
    f = np.float32
    inv = (f(1.0) / (f(10000.0) ** (np.arange(0, DH, 2, dtype=f) / f(DH)))).astype(f)
    fr = (np.arange(T, dtype=f)[:, None] * inv[None, :]).astype(f)
    s, t = np.arange(T)[:, None], np.arange(T)[None, :]
    return {
        "c_cos": np.cos(fr).astype(f), "c_sin": np.sin(fr).astype(f),
        "c_causal": np.where(s <= t, 0.0, -BIG).astype(f),
        "c_hmask": (np.arange(P)[:, None] // DH == np.arange(HG)[None, :]).astype(f),
        "c_sel": np.broadcast_to(np.eye(NB, dtype=f), (T, NB, NB)).copy(),
        "c_pow2": np.tile((2.0 ** np.arange(6)).astype(f), (T, NH)),
        "c_half": (np.arange(P)[:, None] // (P // 2) == np.arange(2)[None, :]).astype(f),
        "c_tri": (s < t).astype(f), "c_experts": np.broadcast_to(np.arange(8, dtype=f), (T, NB, 8)).copy(),
        "c_thresholds": np.broadcast_to(P * np.arange(NTH, dtype=f), (T, 8, NTH)).copy(),
        "c_blocks": np.broadcast_to(np.arange(NBK, dtype=f)[None, :, None], (1, NBK, 8)).copy(),
        "c_ident": np.eye(P, dtype=f),
    }


def kernel(**inputs):
    import concourse.bacc as bacc
    from concourse.bass_utils import run_bass_kernel_spmd

    nc = bacc.Bacc("TRN2", target_bir_lowering=False, num_devices=1)
    arrays, d = {}, {}
    for name, a in {**inputs, **shape_constants()}.items():
        a = np.ascontiguousarray(a)
        if a.dtype == np.bool_:
            a = a.view(np.uint8)
        arrays[f"in_{name}"] = a
        d[name] = nc.dram_tensor(f"in_{name}", a.shape, mybir.dt.from_np(a.dtype), kind="ExternalInput").ap()
    out = nc.dram_tensor("out", (NB, T, D), F32, kind="ExternalOutput").ap()
    build(nc, d, out)
    r = run_bass_kernel_spmd(nc, [arrays], core_ids=[0])
    return r.results[0]["out"]
```
